# Optimizing a Trainium2 kernel written in Bass

```python
import numpy as np
import jax
import jax.numpy as jnp

def _softmax(x, axis=-1):
    return jax.nn.softmax(x, axis=axis)

def _gelu(x):
    return jax.nn.gelu(x, approximate=True)

def _silu(x):
    return jax.nn.silu(x)

def _sigmoid(x):
    return jax.nn.sigmoid(x)

def _layernorm(x, axis=-1, eps=1e-05):
    m = jnp.mean(x, axis=axis, keepdims=True)
    v = jnp.var(x, axis=axis, keepdims=True)
    return (x - m) / jnp.sqrt(v + eps)

def _scatter_add(tgt, idx, src, axis=0):
    return tgt.at[idx].add(src)

def _segment_sum(src, seg, n):
    return jax.ops.segment_sum(src, seg, n)
kernel_name = 'mk_seq_preln_d4_jaxref_r8_b746d8'

def setup_inputs(seed: int=0):
    np.random.seed(seed)
    _w = jnp.asarray

    def _L0_attn_setup():
        import jax, jax.numpy as jnp
        import numpy as np
        D_MODEL = 128
        NUM_HEADS = 16
        HEAD_DIM = D_MODEL // NUM_HEADS
        key = jax.random.key(seed)
        ks = jax.random.split(key, 7)
        B, T, C = (4, 256, D_MODEL)
        s = 1.0 / np.sqrt(C)
        return {'x': jax.random.normal(ks[0], (B, T, C), dtype=jnp.float32), 'ln_gamma': jnp.ones((C,), dtype=jnp.float32), 'ln_beta': jnp.zeros((C,), dtype=jnp.float32), 'w_qkv': jax.random.normal(ks[1], (C, 3 * C), dtype=jnp.float32) * s, 'b_qkv': jnp.zeros((3 * C,), dtype=jnp.float32), 'w_out': jax.random.normal(ks[2], (C, C), dtype=jnp.float32) * s, 'b_out': jnp.zeros((C,), dtype=jnp.float32)}
    _L0_attn_in = _L0_attn_setup()

    def _L0_ffn_setup():
        import jax, jax.numpy as jnp
        import numpy as np
        H = 128
        I = 64
        IS = 128
        E = 16
        G = 4
        TOPK_G = 2
        TOPK = 4
        SCALE = 2.5
        B, S = (2, 128)

        def _relu2(x):
            r = jax.nn.relu(x)
            return r * r

        def _route(scores, bias_corr):
            T = scores.shape[0]
            s_choice = scores + bias_corr
            gs = s_choice.reshape(T, G, E // G)
            group_scores = jnp.sum(jax.lax.top_k(gs, 2)[0], axis=-1)
            gidx = jax.lax.top_k(group_scores, TOPK_G)[1]
            gmask = jnp.sum(jax.nn.one_hot(gidx, G, dtype=scores.dtype), axis=1)
            smask = jnp.repeat(gmask, E // G, axis=1)
            masked = jnp.where(smask > 0, s_choice, 0.0)
            topk_idx = jax.lax.top_k(masked, TOPK)[1]
            topk_w = jnp.take_along_axis(scores, topk_idx, axis=1)
            topk_w = topk_w / (jnp.sum(topk_w, axis=-1, keepdims=True) + 1e-20)
            topk_w = topk_w * SCALE
            return (topk_idx, topk_w)
        key = jax.random.key(seed)
        ks = jax.random.split(key, 8)
        sd = 0.02
        return {'hidden_states': jax.random.normal(ks[0], (B, S, H), jnp.float32), 'Wg': jax.random.normal(ks[1], (E, H), jnp.float32) * sd, 'bias_corr': jax.random.normal(ks[2], (E,), jnp.float32) * 0.01, 'W1': jax.random.normal(ks[3], (E, I, H), jnp.float32) * sd, 'W2': jax.random.normal(ks[4], (E, H, I), jnp.float32) * sd, 'Ws1': jax.random.normal(ks[5], (IS, H), jnp.float32) * sd, 'Ws2': jax.random.normal(ks[6], (H, IS), jnp.float32) * sd}
    _L0_ffn_in = _L0_ffn_setup()

    def _L1_attn_setup():
        import jax, jax.numpy as jnp
        import numpy as np
        N_HEAD = 16
        NEG_BIG = -10000000000.0

        def _rope_cos_sin(T, head_dim):
            t = jnp.arange(T, dtype=jnp.float32)[:, None]
            i = jnp.arange(head_dim // 2, dtype=jnp.float32)
            theta = jnp.power(10000.0, 2.0 * i / head_dim)
            ang = t * theta[None, :]
            return (jnp.cos(ang), jnp.sin(ang))

        def _apply_rope(x, cos, sin):
            B, H, T, D = x.shape
            xr = x.reshape(B, H, T, D // 2, 2)
            x0, x1 = (xr[..., 0], xr[..., 1])
            c = cos[None, None, :, :]
            s = sin[None, None, :, :]
            o0 = x0 * c - x1 * s
            o1 = x0 * s + x1 * c
            return jnp.stack([o0, o1], axis=-1).reshape(B, H, T, D)
        key = jax.random.key(seed)
        ks = jax.random.split(key, 9)
        B, T, C = (2, 256, 128)
        sc = 1.0 / np.sqrt(C)
        return {'x': jax.random.normal(ks[0], (B, T, C), jnp.float32), 'Wq': jax.random.normal(ks[1], (C, C), jnp.float32) * sc, 'bq': jax.random.normal(ks[2], (C,), jnp.float32) * 0.01, 'Wk': jax.random.normal(ks[3], (C, C), jnp.float32) * sc, 'bk': jax.random.normal(ks[4], (C,), jnp.float32) * 0.01, 'Wv': jax.random.normal(ks[5], (C, C), jnp.float32) * sc, 'bv': jax.random.normal(ks[6], (C,), jnp.float32) * 0.01, 'Wp': jax.random.normal(ks[7], (C, C), jnp.float32) * sc, 'bp': jax.random.normal(ks[8], (C,), jnp.float32) * 0.01}
    _L1_attn_in = _L1_attn_setup()

    def _L1_ffn_setup():
        import jax, jax.numpy as jnp
        import numpy as np
        D = 128
        H = 4
        DF = 512
        E = 8
        EPS = 1e-05

        def _layer_norm(x, g, b):
            mu = jnp.mean(x, axis=-1, keepdims=True)
            var = jnp.mean(jnp.square(x - mu), axis=-1, keepdims=True)
            return (x - mu) * jax.lax.rsqrt(var + EPS) * g + b

        def _mha(x, Wqkv, bqkv, Wo, bo):
            S, B, _ = x.shape
            hd = D // H
            qkv = x @ Wqkv.T + bqkv
            q, k, v = jnp.split(qkv, 3, axis=-1)
            to_heads = lambda t: t.reshape(S, B, H, hd).transpose(1, 2, 0, 3)
            q, k, v = (to_heads(q), to_heads(k), to_heads(v))
            scores = jnp.einsum('bhqd,bhkd->bhqk', q, k) * (1.0 / np.sqrt(hd))
            att = jax.nn.softmax(scores, axis=-1)
            o = jnp.einsum('bhqk,bhkd->bhqd', att, v)
            o = o.transpose(2, 0, 1, 3).reshape(S, B, D)
            return o @ Wo.T + bo

        def _moe(x, Wg, W1, b1, W2, b2):
            S, B, _ = x.shape
            xf = x.reshape(S * B, D)
            logits = xf @ Wg.T
            idx = jnp.argmax(logits, axis=-1)
            out = jnp.zeros_like(xf)
            for e in range(E):
                m = (idx == e)[:, None].astype(xf.dtype)
                h = jax.nn.relu(xf @ W1[e] + b1[e])
                out = out + m * (h @ W2[e] + b2[e])
            return out.reshape(S, B, D)
        key = jax.random.key(seed)
        ks = jax.random.split(key, 16)
        S, B = (64, 8)
        s = lambda k, shape, fan: jax.random.normal(k, shape, jnp.float32) * (1.0 / np.sqrt(fan))
        return {'x': jax.random.normal(ks[0], (S, B, D), jnp.float32), 'Wqkv': s(ks[1], (3 * D, D), D), 'bqkv': jnp.zeros((3 * D,), jnp.float32), 'Wo': s(ks[2], (D, D), D), 'bo': jnp.zeros((D,), jnp.float32), 'g1': jnp.ones((D,), jnp.float32), 'be1': jnp.zeros((D,), jnp.float32), 'g2': jnp.ones((D,), jnp.float32), 'be2': jnp.zeros((D,), jnp.float32), 'Wg': s(ks[3], (E, D), D), 'W1': s(ks[4], (E, D, DF), D), 'b1': jnp.zeros((E, DF), jnp.float32), 'W2': s(ks[5], (E, DF, D), DF), 'b2': jnp.zeros((E, D), jnp.float32)}
    _L1_ffn_in = _L1_ffn_setup()

    def _L2_attn_setup():
        import jax, jax.numpy as jnp
        import numpy as np
        D_MODEL = 128
        D_STATE = 16
        D_CONV = 4
        EXPAND = 2
        D_INNER = EXPAND * D_MODEL
        B, L = (4, 256)

        def _mamba_forward(x, W_in, conv_w, conv_b, W_x, w_dt, b_dt, A_log, D, W_out):
            Bb, Ll, _ = x.shape
            xz = x @ W_in
            xc, z = jnp.split(xz, 2, axis=-1)
            xp = jnp.pad(xc, ((0, 0), (D_CONV - 1, 0), (0, 0)))
            xconv = conv_b
            for k in range(D_CONV):
                xconv = xconv + xp[:, k:k + Ll, :] * conv_w[:, k]
            xs = jax.nn.silu(xconv)
            A = -jnp.exp(A_log)
            x_dbl = xs @ W_x
            d_raw = x_dbl[..., :1]
            Bp = x_dbl[..., 1:1 + D_STATE]
            Cp = x_dbl[..., 1 + D_STATE:]
            delta = jax.nn.softplus(d_raw * w_dt + b_dt)

            def step(h, inp):
                dt, b, c, xt = inp
                At = jnp.exp(dt[..., None] * A)
                h = At * h + (dt * xt)[..., None] * b[:, None, :]
                y = jnp.einsum('bdn,bn->bd', h, c)
                return (h, y)
            h0 = jnp.zeros((Bb, D_INNER, D_STATE), x.dtype)
            seq = (jnp.swapaxes(delta, 0, 1), jnp.swapaxes(Bp, 0, 1), jnp.swapaxes(Cp, 0, 1), jnp.swapaxes(xs, 0, 1))
            _, ys = jax.lax.scan(step, h0, seq)
            y = jnp.swapaxes(ys, 0, 1) + xs * D
            y = y * jax.nn.silu(z)
            return y @ W_out
        key = jax.random.key(seed)
        ks = jax.random.split(key, 8)
        s = 0.02
        x = jax.random.normal(ks[0], (B, L, D_MODEL), jnp.float32)
        W_in = jax.random.normal(ks[1], (D_MODEL, 2 * D_INNER), jnp.float32) * s
        conv_w = jax.random.normal(ks[2], (D_INNER, D_CONV), jnp.float32) * 0.1
        conv_b = jnp.zeros((D_INNER,), jnp.float32)
        W_x = jax.random.normal(ks[3], (D_INNER, 1 + 2 * D_STATE), jnp.float32) * s
        w_dt = jax.random.normal(ks[4], (D_INNER,), jnp.float32) * 0.1
        b_dt = jnp.zeros((D_INNER,), jnp.float32)
        A_log = jnp.log(jnp.tile(jnp.arange(1, D_STATE + 1, dtype=jnp.float32), (D_INNER, 1)))
        D = jnp.ones((D_INNER,), jnp.float32)
        W_out = jax.random.normal(ks[5], (D_INNER, D_MODEL), jnp.float32) * s
        return {'x': x, 'W_in': W_in, 'conv_w': conv_w, 'conv_b': conv_b, 'W_x': W_x, 'w_dt': w_dt, 'b_dt': b_dt, 'A_log': A_log, 'D': D, 'W_out': W_out}
    _L2_attn_in = _L2_attn_setup()

    def _L2_ffn_setup():
        import jax, jax.numpy as jnp
        import numpy as np
        B, S, H, E, K, I = (4, 256, 128, 8, 2, 512)
        GATE_EPS = 1e-06
        LN_EPS = 1e-05
        key = jax.random.key(seed)
        k0, k1, k2, k3 = jax.random.split(key, 4)
        x = jax.random.normal(k0, (B, S, H), jnp.float32)
        gate_w = jax.random.normal(k1, (E, H), jnp.float32) * np.float32(np.sqrt(2.0 / (H + E)))
        expert_bias = jnp.zeros((E,), jnp.float32)
        w_up = jax.random.normal(k2, (E, I, H), jnp.float32) * np.float32(np.sqrt(2.0 / (H + I)))
        w_down = jax.random.normal(k3, (E, H, I), jnp.float32) * np.float32(np.sqrt(2.0 / (H + I)))
        return {'x': x, 'gate_w': gate_w, 'expert_bias': expert_bias, 'w_up': w_up, 'w_down': w_down}
    _L2_ffn_in = _L2_ffn_setup()

    def _L3_attn_setup():
        import jax, jax.numpy as jnp
        import numpy as np
        NEG = -1000000000.0

        def _attention(x, Wq, bq, Wk, bk, Wv, bv, Wo, num_heads=16):
            B, N, E = x.shape
            H = num_heads
            D = E // H
            scale = D ** (-0.5)
            q = (jnp.einsum('bne,fe->bnf', x, Wq) + bq).reshape(B, N, H, D).transpose(0, 2, 1, 3)
            k = (jnp.einsum('bne,fe->bnf', x, Wk) + bk).reshape(B, N, H, D).transpose(0, 2, 1, 3)
            v = (jnp.einsum('bne,fe->bnf', x, Wv) + bv).reshape(B, N, H, D).transpose(0, 2, 1, 3)
            scores = jnp.einsum('bhqd,bhkd->bhqk', q, k) * scale
            scores = scores.at[:, :, 0, -1].set(NEG)
            scores = scores.at[:, :, -1, 0].set(NEG)
            weights = jax.nn.softmax(scores, axis=-1)
            out = jnp.einsum('bhqk,bhkd->bhqd', weights, v)
            out = out.transpose(0, 2, 1, 3).reshape(B, N, E)
            return jnp.einsum('bne,fe->bnf', out, Wo)
        key = jax.random.key(seed)
        ks = jax.random.split(key, 8)
        B, N, E = (4, 256, 128)
        s = E ** (-0.5)
        return {'x': jax.random.normal(ks[0], (B, N, E), jnp.float32), 'Wq': jax.random.normal(ks[1], (E, E), jnp.float32) * s, 'bq': jax.random.normal(ks[2], (E,), jnp.float32) * 0.02, 'Wk': jax.random.normal(ks[3], (E, E), jnp.float32) * s, 'bk': jax.random.normal(ks[4], (E,), jnp.float32) * 0.02, 'Wv': jax.random.normal(ks[5], (E, E), jnp.float32) * s, 'bv': jax.random.normal(ks[6], (E,), jnp.float32) * 0.02, 'Wo': jax.random.normal(ks[7], (E, E), jnp.float32) * s}
    _L3_attn_in = _L3_attn_setup()

    def _L3_ffn_setup():
        import jax, jax.numpy as jnp
        import numpy as np
        B, L, H = (8, 256, 128)
        E, K, R = (8, 2, 64)

        def _gates(cls_tok, Wr):
            logits = cls_tok @ Wr.T
            top_vals, top_idx = jax.lax.top_k(logits, K)
            neg_inf = jnp.full_like(logits, -jnp.inf)
            rows = jnp.arange(logits.shape[0])[:, None]
            masked = neg_inf.at[rows, top_idx].set(top_vals)
            return jax.nn.softmax(masked, axis=-1)
        key = jax.random.key(seed)
        k1, k2, k3, k4 = jax.random.split(key, 4)
        x = jax.random.normal(k1, (B, L, H), dtype=jnp.float32)
        Wr = jax.random.normal(k2, (E, H), dtype=jnp.float32) * (1.0 / np.sqrt(H))
        A = jax.random.normal(k3, (E, R, H), dtype=jnp.float32) * (1.0 / np.sqrt(H))
        Bw = jax.random.normal(k4, (E, H, R), dtype=jnp.float32) * (1.0 / np.sqrt(R))
        return {'x': x, 'Wr': Wr, 'A': A, 'Bw': Bw}
    _L3_ffn_in = _L3_ffn_setup()
    _d = {'L0_attn_x': _L0_attn_in['x'], 'L0_attn_ln_gamma': _L0_attn_in['ln_gamma'], 'L0_attn_ln_beta': _L0_attn_in['ln_beta'], 'L0_attn_w_qkv': _L0_attn_in['w_qkv'], 'L0_attn_b_qkv': _L0_attn_in['b_qkv'], 'L0_attn_w_out': _L0_attn_in['w_out'], 'L0_attn_b_out': _L0_attn_in['b_out'], 'L0_ffn_Wg': _L0_ffn_in['Wg'], 'L0_ffn_bias_corr': _L0_ffn_in['bias_corr'], 'L0_ffn_W1': _L0_ffn_in['W1'], 'L0_ffn_W2': _L0_ffn_in['W2'], 'L0_ffn_Ws1': _L0_ffn_in['Ws1'], 'L0_ffn_Ws2': _L0_ffn_in['Ws2'], 'L1_attn_Wq': _L1_attn_in['Wq'], 'L1_attn_bq': _L1_attn_in['bq'], 'L1_attn_Wk': _L1_attn_in['Wk'], 'L1_attn_bk': _L1_attn_in['bk'], 'L1_attn_Wv': _L1_attn_in['Wv'], 'L1_attn_bv': _L1_attn_in['bv'], 'L1_attn_Wp': _L1_attn_in['Wp'], 'L1_attn_bp': _L1_attn_in['bp'], 'L1_ffn_Wqkv': _L1_ffn_in['Wqkv'], 'L1_ffn_bqkv': _L1_ffn_in['bqkv'], 'L1_ffn_Wo': _L1_ffn_in['Wo'], 'L1_ffn_bo': _L1_ffn_in['bo'], 'L1_ffn_g1': _L1_ffn_in['g1'], 'L1_ffn_be1': _L1_ffn_in['be1'], 'L1_ffn_g2': _L1_ffn_in['g2'], 'L1_ffn_be2': _L1_ffn_in['be2'], 'L1_ffn_Wg': _L1_ffn_in['Wg'], 'L1_ffn_W1': _L1_ffn_in['W1'], 'L1_ffn_b1': _L1_ffn_in['b1'], 'L1_ffn_W2': _L1_ffn_in['W2'], 'L1_ffn_b2': _L1_ffn_in['b2'], 'L2_attn_W_in': _L2_attn_in['W_in'], 'L2_attn_conv_w': _L2_attn_in['conv_w'], 'L2_attn_conv_b': _L2_attn_in['conv_b'], 'L2_attn_W_x': _L2_attn_in['W_x'], 'L2_attn_w_dt': _L2_attn_in['w_dt'], 'L2_attn_b_dt': _L2_attn_in['b_dt'], 'L2_attn_A_log': _L2_attn_in['A_log'], 'L2_attn_D': _L2_attn_in['D'], 'L2_attn_W_out': _L2_attn_in['W_out'], 'L2_ffn_gate_w': _L2_ffn_in['gate_w'], 'L2_ffn_expert_bias': _L2_ffn_in['expert_bias'], 'L2_ffn_w_up': _L2_ffn_in['w_up'], 'L2_ffn_w_down': _L2_ffn_in['w_down'], 'L3_attn_Wq': _L3_attn_in['Wq'], 'L3_attn_bq': _L3_attn_in['bq'], 'L3_attn_Wk': _L3_attn_in['Wk'], 'L3_attn_bk': _L3_attn_in['bk'], 'L3_attn_Wv': _L3_attn_in['Wv'], 'L3_attn_bv': _L3_attn_in['bv'], 'L3_attn_Wo': _L3_attn_in['Wo'], 'L3_ffn_Wr': _L3_ffn_in['Wr'], 'L3_ffn_A': _L3_ffn_in['A'], 'L3_ffn_Bw': _L3_ffn_in['Bw']}
    _x0 = _d['L0_attn_x']
    _d['L0_attn_x'] = jax.random.normal(jax.random.fold_in(jax.random.key(seed), 1), (8, 512, 128), dtype=_x0.dtype)
    del _x0
    return _d

def reference(L0_attn_x, L0_attn_ln_gamma, L0_attn_ln_beta, L0_attn_w_qkv, L0_attn_b_qkv, L0_attn_w_out, L0_attn_b_out, L0_ffn_Wg, L0_ffn_bias_corr, L0_ffn_W1, L0_ffn_W2, L0_ffn_Ws1, L0_ffn_Ws2, L1_attn_Wq, L1_attn_bq, L1_attn_Wk, L1_attn_bk, L1_attn_Wv, L1_attn_bv, L1_attn_Wp, L1_attn_bp, L1_ffn_Wqkv, L1_ffn_bqkv, L1_ffn_Wo, L1_ffn_bo, L1_ffn_g1, L1_ffn_be1, L1_ffn_g2, L1_ffn_be2, L1_ffn_Wg, L1_ffn_W1, L1_ffn_b1, L1_ffn_W2, L1_ffn_b2, L2_attn_W_in, L2_attn_conv_w, L2_attn_conv_b, L2_attn_W_x, L2_attn_w_dt, L2_attn_b_dt, L2_attn_A_log, L2_attn_D, L2_attn_W_out, L2_ffn_gate_w, L2_ffn_expert_bias, L2_ffn_w_up, L2_ffn_w_down, L3_attn_Wq, L3_attn_bq, L3_attn_Wk, L3_attn_bk, L3_attn_Wv, L3_attn_bv, L3_attn_Wo, L3_ffn_Wr, L3_ffn_A, L3_ffn_Bw):

    def _L0_attn_ref(x, ln_gamma, ln_beta, w_qkv, b_qkv, w_out, b_out):
        import jax, jax.numpy as jnp
        import numpy as np
        D_MODEL = 128
        NUM_HEADS = 16
        HEAD_DIM = D_MODEL // NUM_HEADS
        B, T, C = x.shape
        residual = x
        mu = jnp.mean(x, axis=-1, keepdims=True)
        var = jnp.var(x, axis=-1, keepdims=True)
        h = (x - mu) * jax.lax.rsqrt(var + 1e-05) * ln_gamma + ln_beta
        qkv = (h @ w_qkv + b_qkv).reshape(B, T, 3, NUM_HEADS, HEAD_DIM)
        qkv = jnp.transpose(qkv, (2, 0, 3, 1, 4))
        q, k, v = (qkv[0], qkv[1], qkv[2])
        scores = jnp.einsum('bhqd,bhkd->bhqk', q, k) / np.sqrt(HEAD_DIM)
        attn = jax.nn.softmax(scores, axis=-1)
        out = jnp.einsum('bhqk,bhkd->bhqd', attn, v)
        out = jnp.transpose(out, (0, 2, 1, 3)).reshape(B, T, C)
        out = out @ w_out + b_out
        return residual + out

    def _L0_ffn_ref(hidden_states, Wg, bias_corr, W1, W2, Ws1, Ws2):
        import jax, jax.numpy as jnp
        import numpy as np
        H = 128
        I = 64
        IS = 128
        E = 16
        G = 4
        TOPK_G = 2
        TOPK = 4
        SCALE = 2.5
        B, S = (2, 128)

        def _relu2(x):
            r = jax.nn.relu(x)
            return r * r

        def _route(scores, bias_corr):
            T = scores.shape[0]
            s_choice = scores + bias_corr
            gs = s_choice.reshape(T, G, E // G)
            group_scores = jnp.sum(jax.lax.top_k(gs, 2)[0], axis=-1)
            gidx = jax.lax.top_k(group_scores, TOPK_G)[1]
            gmask = jnp.sum(jax.nn.one_hot(gidx, G, dtype=scores.dtype), axis=1)
            smask = jnp.repeat(gmask, E // G, axis=1)
            masked = jnp.where(smask > 0, s_choice, 0.0)
            topk_idx = jax.lax.top_k(masked, TOPK)[1]
            topk_w = jnp.take_along_axis(scores, topk_idx, axis=1)
            topk_w = topk_w / (jnp.sum(topk_w, axis=-1, keepdims=True) + 1e-20)
            topk_w = topk_w * SCALE
            return (topk_idx, topk_w)
        b, s, h = hidden_states.shape
        flat = hidden_states.reshape(-1, h)
        T = flat.shape[0]
        logits = flat.astype(jnp.float32) @ Wg.T
        scores = jax.nn.sigmoid(logits)
        topk_idx, topk_w = _route(scores, bias_corr)
        topk_w = topk_w.astype(hidden_states.dtype)
        cw = jnp.zeros((T, E), flat.dtype)
        cw = cw.at[jnp.arange(T)[:, None], topk_idx].add(topk_w)
        hid = _relu2(jnp.einsum('th,eih->eti', flat, W1))
        y = jnp.einsum('eti,ehi->eth', hid, W2)
        out = jnp.einsum('eth,te->th', y, cw)
        shared = _relu2(flat @ Ws1.T) @ Ws2.T
        return (out + shared).reshape(b, s, h)

    def _L1_attn_ref(x, Wq, bq, Wk, bk, Wv, bv, Wp, bp):
        import jax, jax.numpy as jnp
        import numpy as np
        N_HEAD = 16
        NEG_BIG = -10000000000.0

        def _rope_cos_sin(T, head_dim):
            t = jnp.arange(T, dtype=jnp.float32)[:, None]
            i = jnp.arange(head_dim // 2, dtype=jnp.float32)
            theta = jnp.power(10000.0, 2.0 * i / head_dim)
            ang = t * theta[None, :]
            return (jnp.cos(ang), jnp.sin(ang))

        def _apply_rope(x, cos, sin):
            B, H, T, D = x.shape
            xr = x.reshape(B, H, T, D // 2, 2)
            x0, x1 = (xr[..., 0], xr[..., 1])
            c = cos[None, None, :, :]
            s = sin[None, None, :, :]
            o0 = x0 * c - x1 * s
            o1 = x0 * s + x1 * c
            return jnp.stack([o0, o1], axis=-1).reshape(B, H, T, D)
        B, T, C = x.shape
        H = N_HEAD
        D = C // H

        def heads(W, b):
            y = jnp.einsum('btc,oc->bto', x, W) + b
            return y.reshape(B, T, H, D).transpose(0, 2, 1, 3)
        q, k, v = (heads(Wq, bq), heads(Wk, bk), heads(Wv, bv))
        cos, sin = _rope_cos_sin(T, D)
        q = _apply_rope(q, cos, sin)
        k = _apply_rope(k, cos, sin)
        att = jnp.einsum('bhqd,bhkd->bhqk', q, k) * (1.0 / np.sqrt(D))
        causal = jnp.tril(jnp.ones((T, T), bool))
        att = jnp.where(causal[None, None], att, NEG_BIG)
        att = jax.nn.softmax(att, axis=-1)
        y = jnp.einsum('bhqk,bhkd->bhqd', att, v)
        y = y.transpose(0, 2, 1, 3).reshape(B, T, C)
        return jnp.einsum('btc,oc->bto', y, Wp) + bp

    def _L1_ffn_ref(x, Wqkv, bqkv, Wo, bo, g1, be1, g2, be2, Wg, W1, b1, W2, b2):
        import jax, jax.numpy as jnp
        import numpy as np
        D = 128
        H = 4
        DF = 512
        E = 8
        EPS = 1e-05

        def _layer_norm(x, g, b):
            mu = jnp.mean(x, axis=-1, keepdims=True)
            var = jnp.mean(jnp.square(x - mu), axis=-1, keepdims=True)
            return (x - mu) * jax.lax.rsqrt(var + EPS) * g + b

        def _mha(x, Wqkv, bqkv, Wo, bo):
            S, B, _ = x.shape
            hd = D // H
            qkv = x @ Wqkv.T + bqkv
            q, k, v = jnp.split(qkv, 3, axis=-1)
            to_heads = lambda t: t.reshape(S, B, H, hd).transpose(1, 2, 0, 3)
            q, k, v = (to_heads(q), to_heads(k), to_heads(v))
            scores = jnp.einsum('bhqd,bhkd->bhqk', q, k) * (1.0 / np.sqrt(hd))
            att = jax.nn.softmax(scores, axis=-1)
            o = jnp.einsum('bhqk,bhkd->bhqd', att, v)
            o = o.transpose(2, 0, 1, 3).reshape(S, B, D)
            return o @ Wo.T + bo

        def _moe(x, Wg, W1, b1, W2, b2):
            S, B, _ = x.shape
            xf = x.reshape(S * B, D)
            logits = xf @ Wg.T
            idx = jnp.argmax(logits, axis=-1)
            out = jnp.zeros_like(xf)
            for e in range(E):
                m = (idx == e)[:, None].astype(xf.dtype)
                h = jax.nn.relu(xf @ W1[e] + b1[e])
                out = out + m * (h @ W2[e] + b2[e])
            return out.reshape(S, B, D)
        y = _layer_norm(x + _mha(x, Wqkv, bqkv, Wo, bo), g1, be1)
        z = _layer_norm(y + _moe(y, Wg, W1, b1, W2, b2), g2, be2)
        return z

    def _L2_attn_ref(x, W_in, conv_w, conv_b, W_x, w_dt, b_dt, A_log, D, W_out):
        import jax, jax.numpy as jnp
        import numpy as np
        D_MODEL = 128
        D_STATE = 16
        D_CONV = 4
        EXPAND = 2
        D_INNER = EXPAND * D_MODEL
        B, L = (4, 256)

        def _mamba_forward(x, W_in, conv_w, conv_b, W_x, w_dt, b_dt, A_log, D, W_out):
            Bb, Ll, _ = x.shape
            xz = x @ W_in
            xc, z = jnp.split(xz, 2, axis=-1)
            xp = jnp.pad(xc, ((0, 0), (D_CONV - 1, 0), (0, 0)))
            xconv = conv_b
            for k in range(D_CONV):
                xconv = xconv + xp[:, k:k + Ll, :] * conv_w[:, k]
            xs = jax.nn.silu(xconv)
            A = -jnp.exp(A_log)
            x_dbl = xs @ W_x
            d_raw = x_dbl[..., :1]
            Bp = x_dbl[..., 1:1 + D_STATE]
            Cp = x_dbl[..., 1 + D_STATE:]
            delta = jax.nn.softplus(d_raw * w_dt + b_dt)

            def step(h, inp):
                dt, b, c, xt = inp
                At = jnp.exp(dt[..., None] * A)
                h = At * h + (dt * xt)[..., None] * b[:, None, :]
                y = jnp.einsum('bdn,bn->bd', h, c)
                return (h, y)
            h0 = jnp.zeros((Bb, D_INNER, D_STATE), x.dtype)
            seq = (jnp.swapaxes(delta, 0, 1), jnp.swapaxes(Bp, 0, 1), jnp.swapaxes(Cp, 0, 1), jnp.swapaxes(xs, 0, 1))
            _, ys = jax.lax.scan(step, h0, seq)
            y = jnp.swapaxes(ys, 0, 1) + xs * D
            y = y * jax.nn.silu(z)
            return y @ W_out
        return _mamba_forward(x, W_in, conv_w, conv_b, W_x, w_dt, b_dt, A_log, D, W_out)

    def _L2_ffn_ref(x, gate_w, expert_bias, w_up, w_down):
        import jax, jax.numpy as jnp
        import numpy as np
        B, S, H, E, K, I = (4, 256, 128, 8, 2, 512)
        GATE_EPS = 1e-06
        LN_EPS = 1e-05
        logits = jnp.einsum('bsh,eh->bse', x, gate_w) + expert_bias
        weights = jax.nn.softmax(logits, axis=-1)
        top_w, top_i = jax.lax.top_k(weights, K)
        top_w = top_w / (jnp.sum(top_w, axis=-1, keepdims=True) + GATE_EPS)
        sparse_w = jnp.sum(jax.nn.one_hot(top_i, E, dtype=weights.dtype) * top_w[..., None], axis=-2)
        out = jnp.zeros_like(x)
        for e in range(E):
            h = jax.nn.gelu(jnp.einsum('bsh,ih->bsi', x, w_up[e]), approximate=False)
            y = jnp.einsum('bsi,hi->bsh', h, w_down[e])
            out = out + sparse_w[..., e:e + 1] * y
        mu = jnp.mean(out, axis=-1, keepdims=True)
        var = jnp.mean(jnp.square(out - mu), axis=-1, keepdims=True)
        out = (out - mu) * jax.lax.rsqrt(var + LN_EPS)
        return out + x

    def _L3_attn_ref(x, Wq, bq, Wk, bk, Wv, bv, Wo):
        import jax, jax.numpy as jnp
        import numpy as np
        NEG = -1000000000.0

        def _attention(x, Wq, bq, Wk, bk, Wv, bv, Wo, num_heads=16):
            B, N, E = x.shape
            H = num_heads
            D = E // H
            scale = D ** (-0.5)
            q = (jnp.einsum('bne,fe->bnf', x, Wq) + bq).reshape(B, N, H, D).transpose(0, 2, 1, 3)
            k = (jnp.einsum('bne,fe->bnf', x, Wk) + bk).reshape(B, N, H, D).transpose(0, 2, 1, 3)
            v = (jnp.einsum('bne,fe->bnf', x, Wv) + bv).reshape(B, N, H, D).transpose(0, 2, 1, 3)
            scores = jnp.einsum('bhqd,bhkd->bhqk', q, k) * scale
            scores = scores.at[:, :, 0, -1].set(NEG)
            scores = scores.at[:, :, -1, 0].set(NEG)
            weights = jax.nn.softmax(scores, axis=-1)
            out = jnp.einsum('bhqk,bhkd->bhqd', weights, v)
            out = out.transpose(0, 2, 1, 3).reshape(B, N, E)
            return jnp.einsum('bne,fe->bnf', out, Wo)
        return _attention(x, Wq, bq, Wk, bk, Wv, bv, Wo, num_heads=16)

    def _L3_ffn_ref(x, Wr, A, Bw):
        import jax, jax.numpy as jnp
        import numpy as np
        B, L, H = (8, 256, 128)
        E, K, R = (8, 2, 64)

        def _gates(cls_tok, Wr):
            logits = cls_tok @ Wr.T
            top_vals, top_idx = jax.lax.top_k(logits, K)
            neg_inf = jnp.full_like(logits, -jnp.inf)
            rows = jnp.arange(logits.shape[0])[:, None]
            masked = neg_inf.at[rows, top_idx].set(top_vals)
            return jax.nn.softmax(masked, axis=-1)
        gates = _gates(x[:, 0, :], Wr)
        mid = jnp.einsum('blh,erh->belr', x, A)
        expert_out = jnp.einsum('belr,ehr->belh', mid, Bw)
        weighted = jnp.einsum('be,belh->blh', gates, expert_out)
        return x + weighted
    x = L0_attn_x
    x = x + _L0_attn_ref(_layernorm(x, axis=-1), L0_attn_ln_gamma, L0_attn_ln_beta, L0_attn_w_qkv, L0_attn_b_qkv, L0_attn_w_out, L0_attn_b_out)
    x = x + _L0_ffn_ref(_layernorm(x, axis=-1), L0_ffn_Wg, L0_ffn_bias_corr, L0_ffn_W1, L0_ffn_W2, L0_ffn_Ws1, L0_ffn_Ws2)
    x = x + _L1_attn_ref(_layernorm(x, axis=-1), L1_attn_Wq, L1_attn_bq, L1_attn_Wk, L1_attn_bk, L1_attn_Wv, L1_attn_bv, L1_attn_Wp, L1_attn_bp)
    x = x + _L1_ffn_ref(_layernorm(x, axis=-1), L1_ffn_Wqkv, L1_ffn_bqkv, L1_ffn_Wo, L1_ffn_bo, L1_ffn_g1, L1_ffn_be1, L1_ffn_g2, L1_ffn_be2, L1_ffn_Wg, L1_ffn_W1, L1_ffn_b1, L1_ffn_W2, L1_ffn_b2)
    x = x + _L2_attn_ref(_layernorm(x, axis=-1), L2_attn_W_in, L2_attn_conv_w, L2_attn_conv_b, L2_attn_W_x, L2_attn_w_dt, L2_attn_b_dt, L2_attn_A_log, L2_attn_D, L2_attn_W_out)
    x = x + _L2_ffn_ref(_layernorm(x, axis=-1), L2_ffn_gate_w, L2_ffn_expert_bias, L2_ffn_w_up, L2_ffn_w_down)
    x = x + _L3_attn_ref(_layernorm(x, axis=-1), L3_attn_Wq, L3_attn_bq, L3_attn_Wk, L3_attn_bk, L3_attn_Wv, L3_attn_bv, L3_attn_Wo)
    x = x + _L3_ffn_ref(_layernorm(x, axis=-1), L3_ffn_Wr, L3_ffn_A, L3_ffn_Bw)
    return x

_drawn_inputs = setup_inputs


def setup_inputs(seed=0):
    import zlib

    import numpy as np

    out = dict(_drawn_inputs(seed))
    spreads = {'L0_attn_ln_gamma': (1.0, 0.2),
     'L0_attn_ln_beta': (0.0, 0.1),
     'L0_attn_b_qkv': (0.0, 0.1),
     'L0_attn_b_out': (0.0, 0.1),
     'L1_ffn_bqkv': (0.0, 0.1),
     'L1_ffn_bo': (0.0, 0.1),
     'L1_ffn_g1': (1.0, 0.2),
     'L1_ffn_be1': (0.0, 0.1),
     'L1_ffn_g2': (1.0, 0.2),
     'L1_ffn_be2': (0.0, 0.1),
     'L1_ffn_b1': (0.0, 0.1),
     'L1_ffn_b2': (0.0, 0.1),
     'L2_attn_conv_b': (0.0, 0.8),
     'L2_attn_b_dt': (0.0, 0.8),
     'L2_attn_D': (1.0, 0.6),
     'L2_ffn_expert_bias': (0.0, 2.0)}
    factors = {'L0_ffn_bias_corr': 3.447,
     'L1_attn_bq': 8.0,
     'L1_attn_bk': 5.081,
     'L2_attn_W_in': 8.0,
     'L2_attn_conv_w': 8.0,
     'L2_attn_W_x': 8.0,
     'L2_attn_w_dt': 8.0,
     'L2_attn_A_log': 8.0,
     'L2_attn_W_out': 8.0,
     'L3_attn_bq': 64.0,
     'L3_attn_bk': 64.0,
     'L3_attn_bv': 200.0,
     'L2_ffn_gate_w': 64.0,
     'L2_ffn_w_up': 64.0,
     'L2_ffn_w_down': 40.684,
     'L3_attn_Wq': 8.0,
     'L3_attn_Wk': 8.0,
     'L3_attn_Wv': 8.0,
     'L3_attn_Wo': 8.0,
     'L3_ffn_Wr': 8.0,
     'L3_ffn_A': 8.0,
     'L3_ffn_Bw': 8.0}
    for name, (base, spread) in spreads.items():
        noise = np.random.default_rng([zlib.crc32(name.encode()), seed]).standard_normal(out[name].shape)
        drawn = base * np.exp(spread * noise) if base else spread * noise
        out[name] = jnp.asarray(drawn.astype(out[name].dtype))
    for name, factor in factors.items():
        out[name] = (out[name] * factor).astype(out[name].dtype)
    return out
```

```python
from contextlib import ExitStack

import concourse.bass as bass
import numpy as np
from concourse import mybir

F32 = mybir.dt.float32
BF16 = mybir.dt.bfloat16
ALU = mybir.AluOpType
ACT = mybir.ActivationFunctionType
AX = mybir.AxisListType

P = 128
B, T, C = 8, 512, 128
NT = T // P
H, HD = 16, 8
GH = 4
NG = H // GH
TERMS = [(0, 0), (1, 0), (2, 0), (0, 1), (1, 1), (0, 2)]
KT = len(TERMS) * HD
NEG = -3.0e10
EPS = 1e-5
LOG1P = [1.99999999981, 0.666666790265, 0.399987112464, 0.286202074065, 0.213985606305, 0.243939073439]
E0, I0 = 16, 64
E8, FF, NF = 8, 512, 4
SB, SH, SD = 8, 4, 32
DI, DS, DC = 256, 16, 4
NCH = DI // P
GD = P // DS
NGR = DI // GD

PACK_A = [("wq0", 128), ("wk0", 128), ("wv0", 128), ("wo0", 128), ("bv0", 128), ("bo0", 128),
          ("cols0", 4), ("wg0", 16), ("bc0", 16), ("w1_0", 1024), ("ws1_0", 128), ("w2_0", 1024),
          ("ws2_0", 128), ("wq1", 128), ("wk1", 128), ("wv1", 128), ("wp1", 128), ("wqs1", 128),
          ("wks1", 128), ("bv1", 128), ("bp1", 128), ("cols1", 4), ("cos1", 512), ("sin1", 512)]
PACK_B = [("wq", 128), ("wk", 128), ("wv", 128), ("wo", 128), ("cols", 2), ("bv", 128), ("bo", 128),
          ("g1", 128), ("be1", 128), ("g2", 128), ("be2", 128), ("wg", 8), ("b1", 32),
          ("w1", 4096), ("w2", 4096)]
PACK_C = [("win", 512), ("convw", 8), ("convb", 2), ("wxd", 256), ("wxb", 256), ("wxc", 256),
          ("wdt", 2), ("bdt", 2), ("alog", 32), ("dcol", 2), ("wout", 256), ("gw", 8), ("eb", 8),
          ("wup", 4096), ("wdn", 4096), ("wq3", 128), ("wk3", 128), ("wv3", 128), ("wo3", 128),
          ("cols3", 2), ("bv3", 128), ("wr3", 8), ("a3", 512), ("b3", 512)]
PACK_K = [("ident", 128), ("tri16", 256), ("sel16", 1024)]
PACK_KB = [("identb", 128), ("causal", 128), ("causalT", 128), ("cornA", 128), ("cornB", 128),
           ("block", 512), ("selG", 512), ("ones", 512)]


def width(pack):
    return sum(n for _, n in pack)


class Pieces:

    def __init__(self, tensor, pack):
        self.tensor, self.at, o = tensor, {}, 0
        for name, n in pack:
            self.at[name] = (o, n)
            o += n

    def __call__(self, name, p=P):
        o, n = self.at[name]
        return self.tensor[0:p, o:o + n]


class Signals:

    def __init__(self, pool):
        self.pool, self.named = pool, {}

    def __call__(self, name):
        if name not in self.named:
            self.named[name] = self.pool[len(self.named)]
        return self.named[name]


class Chain:

    def __init__(self, eng, sem):
        self.eng, self.sem, self.n = eng, sem, 0

    def __call__(self, instruction):
        self.n += 1
        instruction.then_inc(self.sem, 1)
        self.eng.wait_ge(self.sem, self.n)


def build(nc, x, pa, pb, pc, pk, pkb, b2, pk_sel, out):
    top = ExitStack()
    with top:
        def sb(ctx, name, shape, dt=F32):
            return ctx.enter_context(nc.sbuf_tensor(name, shape, dt))

        pool = [top.enter_context(nc.semaphore(f"signal_{i}")) for i in range(48)]
        load_sem = top.enter_context(nc.semaphore("weights_loaded"))
        bank = top.enter_context(nc.psum_tensor("bank", [P, 8, 512], F32))
        kc = Pieces(sb(top, "kc", [P, width(PACK_K)]), PACK_K)
        kb = Pieces(sb(top, "kb", [P, width(PACK_KB)], BF16), PACK_KB)
        ident, identb = kc("ident"), kb("identb")
        x_sb = sb(top, "x_sb", [P, NT, C])
        y_sb = sb(top, "y_sb", [P, NT, C])
        h_sb = sb(top, "h_sb", [P, NT, C])
        base = sb(top, "base", [P, NT, C])
        hT = sb(top, "hT", [P, T])
        stats = sb(top, "stats", [P, NT, 6])
        mom = sb(top, "mom", [P, NT, 2])
        veps = sb(top, "veps", [P, NT])
        rstd = sb(top, "rstd", [P, NT])
        mhalf = sb(top, "mhalf", [P, NT])
        x1 = nc.dram_tensor("x1", (B * T, C), F32, kind="Internal").ap()
        x2 = nc.dram_tensor("x2", (B * T, C), F32, kind="Internal").ap()
        parts_dram = nc.dram_tensor("parts_dram", (3, 2, P, T), BF16, kind="Internal").ap()
        dt_dram = nc.dram_tensor("dt_dram", (3, 2, DI, T), BF16, kind="Internal").ap()
        loads = [0]

        def stage(body):
            S = Signals(pool)
            with nc.Block() as block:
                body(block, S)
            if S.named:
                nums = [s.num for s in S.named.values()]
                nc.gpsimd.sem_clear(range(min(nums), max(nums) + 1))
            nc.all_engine_barrier()

        def norm_dve(dve, chain, S, tag, src, dst):
            for j in range(NT):
                i = dve.bn_stats(stats[:, j, :], src[:, j, :])
            chain(i)
            for j in range(NT):
                i = dve.bn_aggr(mom[:, j, :], stats[:, j, :])
            i.then_inc(S(tag + "_moments"), 1)
            dve.wait_ge(S(tag + "_rstd"), 1)
            for j in range(NT):
                i = dve.tensor_scalar(dst[:, j, :], src[:, j, :], mom[:, j, 0:1], rstd[:, j:j + 1],
                                      ALU.subtract, ALU.mult)
            return i

        def norm_pool(gp, chain, S, tag):
            gp.wait_ge(S(tag + "_moments"), 1)
            chain(gp.tensor_scalar(veps[:, :], mom[:, :, 1], EPS, None, ALU.add))
            gp.tensor_tensor(rstd[:, :], veps[:, :], mhalf[:, :], ALU.pow).then_inc(S(tag + "_rstd"), 1)

        def turn(pe, src, b, col=0, n=NT):
            for j in range(n):
                i = pe.transpose(bank[:, b, col + j * P:col + (j + 1) * P], src[:, j, :], ident)
            return i

        def attention(buf, src, res, wq, wk, wv, wo, bq, bk, bv, bo, scale, causal, corners,
                      swapped, affine, double):
            Qs, Ks, prob, q32, parts, r32, vaug, mx, negm, oT, rden, onorm, ro = (
                buf[k] for k in ("Qs", "Ks", "prob", "q32", "parts", "r32", "vaug", "mx", "negm",
                                 "oT", "rden", "onorm", "ro"))
            if causal:
                units = [[(0, 0, 512, 0), (1, 128, 384, 512), (3, 384, 128, 896)], [(2, 256, 256, 0)]]
                keys = [P * (j + 1) for j in range(NT)]
            else:
                units = [[(0, 0, 512, 0), (1, 0, 512, 512)], [(2, 0, 512, 0), (3, 0, 512, 512)]]
                keys = [T] * NT
            U = len(units)
            spot = {}
            for u, unit in enumerate(units):
                for kt, q0, qn, col in unit:
                    spot[kt] = (u * 1024 + col, q0, qn)
            unit_n = [sum(w[2] for w in unit) for unit in units]

            def body(block, S):
                @block.vector
                def _(dve):
                    chain = Chain(dve, S("vector_chain"))
                    if double:
                        chain(norm_dve(dve, chain, S, "outer", res, src))
                        norm_dve(dve, chain, S, "inner", src, h_sb).then_inc(S("normed"), 1)
                    else:
                        norm_dve(dve, chain, S, "outer", res, src).then_inc(S("normed"), 1)
                    dve.wait_ge(S("turned"), 1)
                    if affine:
                        dve.tensor_scalar(hT[:, :], bank[:, 7, :], affine[0], affine[1],
                                          ALU.mult, ALU.add).then_inc(S("hT_ready"), 1)
                    else:
                        dve.tensor_copy(hT[:, :], bank[:, 7, :]).then_inc(S("hT_ready"), 1)
                    if swapped:
                        dve.wait_ge(S("qk_projected"), 1)
                        for i, (b, s) in enumerate(((bq, swapped[2]), (bk, swapped[3]))):
                            dve.scalar_tensor_tensor(q32[:, i, :], bank[:, i, :], b, swapped[4],
                                                     ALU.add, ALU.mult)
                            k = dve.scalar_tensor_tensor(ro[:, i, :], bank[:, 2 + i, :], s, swapped[5],
                                                         ALU.add, ALU.mult)
                        chain(k)
                        dve.tensor_tensor(q32[:, :, :], q32[:, :, :], ro[:, :, :],
                                          ALU.add).then_inc(S("qk_taken"), 1)
                        dve.wait_ge(S("qk_taken"), 1)
                    else:
                        dve.wait_ge(S("qk_taken"), 2)
                    chain(dve.tensor_copy(parts[:, 0, :, :], q32[:, :, :]))
                    chain(dve.tensor_tensor(r32[:, :, :], q32[:, :, :], parts[:, 0, :, :], ALU.subtract))
                    chain(dve.tensor_copy(parts[:, 1, :, :], r32[:, :, :]))
                    dve.tensor_tensor(parts[:, 2, :, :], r32[:, :, :], parts[:, 1, :, :],
                                      ALU.subtract).then_inc(S("parts_ready"), 1)
                    dve.wait_ge(S("v_projected"), 1)
                    for j in range(NT):
                        i = dve.tensor_tensor(vaug[:, j, :, 0:HD],
                                              bank[:, 6, j * P:(j + 1) * P].rearrange("p (h d) -> p h d", h=H),
                                              bv.rearrange("p (h d) -> p h d", h=H), ALU.add)
                    i.then_inc(S("v_ready"), 1)
                    for k in range(NG + 3):
                        if k < NG:
                            for i in range(GH * NT):
                                dve.wait_ge(S("max_scored"), k * 16 + i + 1)
                                dve.tensor_reduce(mx[:, k, i:i + 1], bank[:, i % 2, 0:keys[i % NT]], AX.X,
                                                  ALU.max).then_inc(S("max_reduced"), 1)
                            dve.wait_ge(S("max_turned"), k + 1)
                            dve.tensor_scalar(negm[:, k, :], bank[0:16, 0, 0:P], -1.0, None,
                                              ALU.mult).then_inc(S("negmax_ready"), 1)
                        if k >= 3:
                            g = k - 3
                            dve.wait_ge(S("o_turned"), g + 1)
                            o4 = bank[:, 7, :].rearrange("p (t h w) -> p t h w", t=NT, h=GH)
                            chain(dve.reciprocal(rden[:, g, :, :], o4[:, :, :, HD]))
                            dve.tensor_tensor(
                                onorm[:, :, g * 32:(g + 1) * 32].rearrange("p t (h d) -> p t h d", h=GH),
                                o4[:, :, :, 0:HD],
                                rden[:, g, :, :].unsqueeze(3).broadcast_to([P, NT, GH, HD]),
                                ALU.mult).then_inc(S("o_normed"), 1)
                    dve.wait_ge(S("o_back"), 1)
                    dve.tensor_copy(hT[:, :], bank[:, 0, :]).then_inc(S("oT_ready"), 1)
                    dve.wait_ge(S("out_projected"), 1)
                    dve.wait_ge(S("base_ready"), 1)
                    dve.tensor_tensor(res[:, :, :], base[:, :, :],
                                      bank[:, 1, :].rearrange("p (t c) -> p t c", t=NT),
                                      ALU.add).then_inc(S("done"), 1)

                @block.gpsimd
                def _(gp):
                    chain = Chain(gp, S("gpsimd_chain"))
                    norm_pool(gp, chain, S, "outer")
                    if double:
                        norm_pool(gp, chain, S, "inner")
                    gp.wait_ge(S("normed"), 1)
                    add = src if double else None
                    if add is not None:
                        chain(gp.tensor_tensor(base[:, :, :], res[:, :, :], src[:, :, :], ALU.add))
                        frm = base
                    else:
                        frm = res
                    if bo is not None:
                        for j in range(NT):
                            i = gp.tensor_tensor(base[:, j, :], frm[:, j, :], bo, ALU.add)
                    else:
                        i = gp.tensor_copy(base[:, :, :], frm[:, :, :])
                    i.then_inc(S("base_ready"), 1)

                @block.scalar
                def _(act):
                    if not swapped:
                        act.wait_ge(S("qk_projected"), 1)
                        act.activation(q32[:, 0, :], bank[:, 0, :], ACT.Identity, bias=bq).then_inc(S("qk_taken"), 1)
                        act.activation(q32[:, 1, :], bank[:, 1, :], ACT.Identity, bias=bk).then_inc(S("qk_taken"), 1)
                    for k in range(1, NG + 2):
                        if k <= NG:
                            g = k - 1
                            if g >= 2:
                                act.wait_ge(S("av_done"), g - 1)
                            for m in range(GH * U):
                                n, u = g * GH * U + m, m % U
                                act.wait_ge(S("scored"), n + 1)
                                act.activation(prob[:, (g % 2) * GH + m // U, u * 1024:u * 1024 + unit_n[u]],
                                               bank[:, 2 + 2 * (n % 2):4 + 2 * (n % 2), :]
                                               .rearrange("p b n -> p (b n)")[:, 0:unit_n[u]],
                                               ACT.Exp, scale=scale).then_inc(S("exped"), 1)
                        if k >= 2:
                            g = k - 2
                            act.wait_ge(S("av_done"), g + 1)
                            if g >= 1:
                                act.wait_ge(S("o_turned"), g)
                            act.activation(oT[:, :], bank[:, 6, :], ACT.Copy).then_inc(S("av_taken"), 1)

                @block.sync
                def _(sp):
                    sp.wait_ge(S("parts_ready"), 1)
                    for i in range(3):
                        sp.dma_start(parts_dram[i].rearrange("q p t -> p q t"),
                                     parts[:, i, :, :]).then_inc(S("parts_stored"), 16)
                    sp.wait_ge(S("parts_stored"), 48)
                    for t, (tq, tk) in enumerate(TERMS):
                        sp.dma_start(Qs[t * HD:(t + 1) * HD, :, :],
                                     parts_dram[tq, 0].rearrange("(h d) t -> d h t", d=HD)).then_inc(S("grouped"), 16)
                        sp.dma_start(Ks[t * HD:(t + 1) * HD, :, :],
                                     parts_dram[tk, 1].rearrange("(h d) t -> d h t", d=HD)).then_inc(S("grouped"), 16)
                    for g in range(NG):
                        sp.wait_ge(S("negmax_ready"), g + 1)
                        sp.dma_start(Qs[KT:KT + 1, g * GH:(g + 1) * GH, :], negm[:, g, :]).then_inc(S("negmax_placed"), 16)

                @block.tensor
                def _(pe):
                    pe.wait_ge(S("normed"), 1)
                    turn(pe, h_sb if double else src, 7).then_inc(S("turned"), 1)
                    pe.wait_ge(S("hT_ready"), 1)
                    pe.matmul(bank[:, 0, :], wq, hT[:, :], start=True, stop=True)
                    i = pe.matmul(bank[:, 1, :], wk, hT[:, :], start=True, stop=True)
                    if swapped:
                        pe.matmul(bank[:, 2, :], swapped[0], hT[:, :], start=True, stop=True)
                        i = pe.matmul(bank[:, 3, :], swapped[1], hT[:, :], start=True, stop=True)
                    i.then_inc(S("qk_projected"), 1)
                    for j in range(NT):
                        i = pe.matmul(bank[:, 6, j * P:(j + 1) * P], hT[:, j * P:(j + 1) * P], wv,
                                      start=True, stop=True)
                    i.then_inc(S("v_projected"), 1)

                    def max_unit(k, i):
                        n, h, j = k * 16 + i, k * GH + i // NT, i % NT
                        if n == 0:
                            pe.wait_ge(S("grouped"), 16 * 2 * len(TERMS))
                            pe.wait_ge(S("qk_taken"), 1 if swapped else 2)
                        if n >= 2:
                            pe.wait_ge(S("max_reduced"), n - 1)
                        if i == 0 and k >= 1:
                            pe.wait_ge(S("negmax_ready"), k)
                        masks = []
                        if causal:
                            masks = [(j * P, kb("causal"))]
                        if corners and j == 0:
                            masks = [(T - P, kb("cornB"))]
                        if corners and j == NT - 1:
                            masks = [(0, kb("cornA"))]
                        m = pe.matmul(bank[:, i % 2, 0:keys[j]], Qs[0:KT, h, j * P:(j + 1) * P],
                                      Ks[0:KT, h, 0:keys[j]], start=True, stop=not masks)
                        for c, mask in masks:
                            m = pe.matmul(bank[:, i % 2, c:c + P], identb, mask, start=False, stop=True)
                        m.then_inc(S("max_scored"), 1)

                    def score_unit(g, m):
                        n, h = g * GH * U + m, g * GH + m // U
                        if m == 0:
                            pe.wait_ge(S("negmax_placed"), 16 * (g + 1))
                        if n >= 2:
                            pe.wait_ge(S("exped"), n - 1)
                        for kt, q0, qn, col in units[m % U]:
                            b, o = 2 + 2 * (n % 2) + col // 512, col % 512
                            masks = []
                            if causal:
                                masks = [(0, kb("causalT"))]
                            if corners and kt == NT - 1:
                                masks = [(0, kb("cornA"))]
                            if corners and kt == 0:
                                masks = [(T - P, kb("cornB"))]
                            i = pe.matmul(bank[:, b, o:o + qn], Ks[0:KT + 1, h, kt * P:(kt + 1) * P],
                                          Qs[0:KT + 1, h, q0:q0 + qn], start=True, stop=not masks)
                            for c, mask in masks:
                                i = pe.matmul(bank[:, b, o + c:o + c + P], identb, mask, start=False, stop=True)
                        i.then_inc(S("scored"), 1)

                    def av(g, i):
                        kt, hl = divmod(i, GH)
                        if i == 0:
                            pe.wait_ge(S("exped"), GH * U * (g + 1))
                            pe.wait_ge(S("v_ready"), 1)
                            if g >= 1:
                                pe.wait_ge(S("av_taken"), g)
                        col, q0, qn = spot[kt]
                        m = pe.matmul(bank[32 * hl:32 * hl + 32, 6, q0:q0 + qn], vaug[:, kt, g * GH + hl, :],
                                      prob[:, (g % 2) * GH + hl, col:col + qn], start=kt == 0, stop=kt == NT - 1,
                                      skip_group_check=True)
                        if i == 15:
                            m.then_inc(S("av_done"), 1)

                    for k in range(NG + 3):
                        for i in range(16):
                            if k < NG:
                                max_unit(k, i)
                            if 1 <= k <= NG and i % 2 == 1:
                                score_unit(k - 1, i // 2)
                            if i == 8 and k >= 3:
                                g = k - 3
                                pe.wait_ge(S("av_taken"), g + 1)
                                if g >= 1:
                                    pe.wait_ge(S("o_normed"), g)
                                for j in range(NT):
                                    m = pe.transpose(bank[:, 7, j * P:(j + 1) * P], oT[:, j * P:(j + 1) * P], ident)
                                m.then_inc(S("o_turned"), 1)
                            if 2 <= k < NG + 2:
                                av(k - 2, i)
                        if k < NG:
                            pe.wait_ge(S("max_reduced"), 16 * (k + 1))
                            pe.transpose(bank[0:16, 0, 0:P], mx[:, k, :], ident).then_inc(S("max_turned"), 1)
                    pe.wait_ge(S("o_normed"), NG)
                    turn(pe, onorm, 0).then_inc(S("o_back"), 1)
                    pe.wait_ge(S("oT_ready"), 1)
                    for j in range(NT):
                        i = pe.matmul(bank[:, 1, j * P:(j + 1) * P], hT[:, j * P:(j + 1) * P], wo,
                                      start=True, stop=True)
                    i.then_inc(S("out_projected"), 1)

            stage(body)

        def attention_buffers(ctx):
            s = {"Qs": sb(ctx, "Qs", [96, H, T], BF16), "Ks": sb(ctx, "Ks", [KT + 1, H, T], BF16),
                 "prob": sb(ctx, "prob", [P, 2 * GH, 2048]), "q32": sb(ctx, "q32", [P, 2, T]),
                 "parts": sb(ctx, "parts", [P, 3, 2, T], BF16), "r32": sb(ctx, "r32", [P, 2, T]),
                 "vaug": sb(ctx, "vaug", [P, NT, H, 32]), "mx": sb(ctx, "mx", [P, NG, 16]),
                 "negm": sb(ctx, "negm", [16, NG, P], BF16), "oT": sb(ctx, "oTu", [P, T]),
                 "rden": sb(ctx, "rden", [P, NG, NT, GH]), "onorm": sb(ctx, "onorm", [P, NT, C]),
                 "ro": sb(ctx, "ro", [P, 2, T])}
            return s

        def carve(room, at, shape, dt=F32):
            n = int(np.prod(shape[1:]))
            words = n if dt == F32 else n // 2
            flat = room[:, :, :].rearrange("p a b -> p (a b)")[:, at[0]:at[0] + words]
            at[0] += words
            assert at[0] <= 2 * GH * 2048
            if dt == BF16:
                flat = flat.bitcast(BF16)
            if len(shape) == 2:
                return flat
            names = "abcde"[:len(shape) - 1]
            return flat.rearrange("p (%s) -> p %s" % (" ".join(names), " ".join(names)),
                                  **{k: s for k, s in zip(names, shape[1:])})

        def tri(n):
            full = kc("tri16").rearrange("p (a b) -> p a b", a=16)
            return full[:, 0:n, 0:n]

        def rank(dve, chain, big, vals, n, tri, ranks):
            shape = [P, NT, n, n]
            other, own = vals.unsqueeze(2).broadcast_to(shape), vals.unsqueeze(3).broadcast_to(shape)
            gt, eq = (big[:, i, 0:NT * n * n].rearrange("p (t a b) -> p t a b", t=NT, a=n) for i in range(2))
            dve.tensor_tensor(gt, other, own, ALU.is_gt)
            chain(dve.tensor_tensor(eq, other, own, ALU.is_equal))
            chain(dve.tensor_tensor(eq, eq, tri.unsqueeze(1).broadcast_to(shape), ALU.mult))
            chain(dve.tensor_tensor(gt, gt, eq, ALU.add))
            chain(dve.tensor_reduce(ranks, gt, AX.X, ALU.add))

        buf = attention_buffers(top)

        def load_constants(block, S):
            wide = buf["prob"][:, 0:2, :].rearrange("p a b -> p (a b)")[:, 0:width(PACK_KB)]

            @block.sync
            def _(sp):
                sp.dma_start(kc.tensor[:, :], pk).then_inc(load_sem, 16)
                sp.dma_start(wide, pkb).then_inc(load_sem, 16)
                sp.wait_ge(load_sem, 32)

            @block.vector
            def _(dve):
                dve.wait_ge(load_sem, 32)
                dve.tensor_copy(kb.tensor[:, :], wide)

            @block.gpsimd
            def _(gp):
                gp.memset(mhalf[:, :], -0.5)
        loads[0] = 32
        stage(load_constants)

        def prepare(buf, extra):
            def body(block, S):
                @block.sync
                def _(sp):
                    for tensor, src in extra:
                        n = tensor.shape[1]
                        for a in range(0, n, 2048):
                            sp.dma_start(tensor[:, a:min(n, a + 2048)], src[:, a:min(n, a + 2048)]).then_inc(load_sem, 16)
                            loads[0] += 16
                    if buf:
                        sp.dma_start(buf["Ks"][KT:KT + 1, :, :], kb("ones", H)).then_inc(load_sem, 16)
                        loads[0] += 16
                    sp.wait_ge(load_sem, loads[0])

                @block.gpsimd
                def _(gp):
                    if buf:
                        chain = Chain(gp, S("gpsimd_chain"))
                        chain(gp.memset(buf["vaug"][:, :, :, :], 0.0))
                        chain(gp.memset(buf["vaug"][:, :, :, HD:HD + 1], 1.0))
            stage(body)

        with ExitStack() as ctx:
            w_a = sb(ctx, "w_a", [P, width(PACK_A)])
            wa = Pieces(w_a, PACK_A)
            prepare(buf, [(w_a, pa)])
            at = [0]
            hid, relu, sq, big = (carve(buf["prob"], at, [P, n, w])
                                  for n, w in ((9, T), (2, T), (2, T), (2, 1024)))
            sc = sb(ctx, "sc", [P, 12, NT, E0])
            gsc = sb(ctx, "gsc", [P, 8, NT, 4, 2])
            cwT = sb(ctx, "cwT", [E0, T])

            def moe0(block, S):
                score, choice, masked, ranks, sel, wsel = (sc[:, i] for i in range(6))

                @block.vector
                def _(dve):
                    chain = Chain(dve, S("vector_chain"))
                    norm_dve(dve, chain, S, "outer", x_sb, y_sb).then_inc(S("normed"), 1)
                    dve.wait_ge(S("turned"), 1)
                    dve.tensor_copy(hT[:, :], bank[:, 7, :]).then_inc(S("hT_ready"), 1)
                    dve.wait_ge(S("exp_logits"), 1)
                    chain(dve.tensor_scalar(sc[:, 6], score, 1.0, None, ALU.add))
                    chain(dve.reciprocal(sc[:, 7], sc[:, 6]))
                    sig = sc[:, 7]
                    chain(dve.tensor_tensor(choice, sig, wa("bc0").unsqueeze(1).broadcast_to([P, NT, E0]), ALU.add))
                    c4 = choice.rearrange("p t (g q r) -> p (t g) q r", q=2, r=2)
                    hi, lo = (gsc[:, i].rearrange("p t g q -> p (t g) q") for i in range(2))
                    dve.tensor_tensor(hi, c4[:, :, :, 0], c4[:, :, :, 1], ALU.max)
                    chain(dve.tensor_tensor(lo, c4[:, :, :, 0], c4[:, :, :, 1], ALU.min))
                    t1, t2, t3 = (gsc[:, i, :, :, 0].rearrange("p t g -> p (t g)") for i in (2, 3, 4))
                    dve.tensor_tensor(t1, hi[:, :, 0], hi[:, :, 1], ALU.max)
                    dve.tensor_tensor(t2, hi[:, :, 0], hi[:, :, 1], ALU.min)
                    chain(dve.tensor_tensor(t3, lo[:, :, 0], lo[:, :, 1], ALU.max))
                    chain(dve.tensor_tensor(t2, t2, t3, ALU.max))
                    gs = sc[:, 8, :, 0:4]
                    chain(dve.tensor_tensor(gs, gsc[:, 2, :, :, 0], gsc[:, 3, :, :, 0], ALU.add))
                    gr = sc[:, 9, :, 0:4]
                    rank(dve, chain, big, gs, 4, tri(4), gr)
                    chain(dve.tensor_scalar(gr, gr, 1.5, None, ALU.is_lt))
                    chain(dve.tensor_tensor(masked.rearrange("p t (g r) -> p t g r", g=4),
                                            choice.rearrange("p t (g r) -> p t g r", g=4),
                                            gr.unsqueeze(3).broadcast_to([P, NT, 4, 4]), ALU.mult))
                    rank(dve, chain, big, masked, E0, tri(E0), ranks)
                    chain(dve.tensor_scalar(sel, ranks, 3.5, None, ALU.is_lt))
                    chain(dve.tensor_tensor(wsel, sel, sig, ALU.mult))
                    tot = sc[:, 10, :, 0:1]
                    chain(dve.tensor_reduce(tot, wsel, AX.X, ALU.add))
                    chain(dve.tensor_scalar(tot, tot, 1e-20, None, ALU.add))
                    chain(dve.reciprocal(sc[:, 11, :, 0:1], tot))
                    chain(dve.tensor_scalar(wsel, wsel, 2.5, None, ALU.mult))
                    dve.tensor_tensor(sc[:, 6], wsel, sc[:, 11, :, 0:1].broadcast_to([P, NT, E0]),
                                      ALU.mult).then_inc(S("weights_ready"), 1)
                    dve.wait_ge(S("weights_turned"), 1)
                    dve.tensor_copy(cwT[:, :], bank[0:E0, 6, :]).then_inc(S("cwT_ready"), 1)
                    for c in range(8):
                        dve.wait_ge(S("squared"), c + 1)
                        dve.wait_ge(S("spread"), c + 1)
                        dve.tensor_tensor(hid[:, c, :], sq[:, c % 2, :], bank[:, 2 + c % 2, :],
                                          ALU.mult).then_inc(S("weighted"), 1)
                    dve.wait_ge(S("moe_out"), 1)
                    dve.tensor_tensor(x_sb[:, :, :], x_sb[:, :, :],
                                      bank[:, 4, :].rearrange("p (t c) -> p t c", t=NT),
                                      ALU.add).then_inc(S("done"), 1)

                @block.gpsimd
                def _(gp):
                    chain = Chain(gp, S("gpsimd_chain"))
                    norm_pool(gp, chain, S, "outer")
                    for c in range(9):
                        gp.wait_ge(S("relued"), c + 1)
                        if 2 <= c < 8:
                            gp.wait_ge(S("weighted"), c - 1)
                        dst = sq[:, c % 2, :] if c < 8 else hid[:, 8, :]
                        gp.tensor_tensor(dst, relu[:, c % 2, :], relu[:, c % 2, :], ALU.mult).then_inc(S("squared"), 1)

                @block.scalar
                def _(act):
                    act.wait_ge(S("logits"), 1)
                    act.activation(score, bank[:, 5, 0:NT * E0].rearrange("p (t e) -> p t e", t=NT), ACT.Exp,
                                   scale=-1.0).then_inc(S("exp_logits"), 1)
                    for c in range(9):
                        act.wait_ge(S("hidden"), c + 1)
                        if c >= 2:
                            act.wait_ge(S("squared"), c - 1)
                        act.activation(relu[:, c % 2, :], bank[:, c % 2, :], ACT.Relu).then_inc(S("relued"), 1)

                @block.tensor
                def _(pe):
                    pe.wait_ge(S("normed"), 1)
                    turn(pe, y_sb, 7).then_inc(S("turned"), 1)
                    pe.wait_ge(S("hT_ready"), 1)
                    for j in range(NT):
                        i = pe.matmul(bank[:, 5, j * E0:(j + 1) * E0], hT[:, j * P:(j + 1) * P], wa("wg0"),
                                      start=True, stop=True)
                    i.then_inc(S("logits"), 1)

                    def hidden(c):
                        if c >= 2:
                            pe.wait_ge(S("relued"), c - 1)
                        w = wa("w1_0")[:, c * P:(c + 1) * P] if c < 8 else wa("ws1_0")
                        pe.matmul(bank[:, c % 2, :], w, hT[:, :], start=True, stop=True).then_inc(S("hidden"), 1)

                    hidden(0)
                    hidden(1)
                    pe.wait_ge(S("weights_ready"), 1)
                    for j in range(NT):
                        i = pe.transpose(bank[0:E0, 6, j * P:(j + 1) * P], sc[:, 6, j, :], ident)
                    i.then_inc(S("weights_turned"), 1)
                    pe.wait_ge(S("cwT_ready"), 1)
                    for c in range(8):
                        if c >= 2:
                            pe.wait_ge(S("weighted"), c - 1)
                        pe.matmul(bank[:, 2 + c % 2, :], kc("sel16", E0)[:, c * P:(c + 1) * P], cwT[:, :],
                                  start=True, stop=True).then_inc(S("spread"), 1)
                        if c + 2 <= 8:
                            hidden(c + 2)
                    pe.wait_ge(S("weighted"), 8)
                    pe.wait_ge(S("squared"), 9)
                    for j in range(NT):
                        for c in range(9):
                            w = wa("w2_0")[:, c * P:(c + 1) * P] if c < 8 else wa("ws2_0")
                            i = pe.matmul(bank[:, 4, j * P:(j + 1) * P], hid[:, c, j * P:(j + 1) * P], w,
                                          start=c == 0, stop=c == 8)
                    i.then_inc(S("moe_out"), 1)

            def load_x(src):
                def body(block, S):
                    @block.sync
                    def _(sp):
                        sp.dma_start(x_sb[:, :, :], src).then_inc(S("x_loaded"), 16)
                        sp.wait_ge(S("x_loaded"), 16)
                return body

            def store_x(dst):
                def body(block, S):
                    @block.sync
                    def _(sp):
                        sp.dma_start(dst, x_sb[:, :, :]).then_inc(S("x_stored"), 16)
                        sp.wait_ge(S("x_stored"), 16)
                return body

            x_b = x.rearrange("(b t p) c -> p b t c", b=B, p=P)
            x1_b = x1.rearrange("(b t p) c -> p b t c", b=B, p=P)
            with nc.Fori(0, B) as b:
                stage(load_x(x_b[:, bass.ds(b, 1), :, :]))
                col = wa("cols0")
                attention(buf, y_sb, x_sb, wa("wq0"), wa("wk0"), wa("wv0"), wa("wo0"), col[:, 2:3], col[:, 3:4],
                          wa("bv0"), wa("bo0"), float(HD) ** -0.5, False, False, None,
                          (col[:, 0:1], col[:, 1:2]), True)
                stage(moe0)
                col = wa("cols1")
                attention(buf, y_sb, x_sb, wa("wq1"), wa("wk1"), wa("wv1"), wa("wp1"), col[:, 0:1], col[:, 1:2],
                          wa("bv1"), wa("bp1"), float(HD) ** -0.5, True, False,
                          (wa("wqs1"), wa("wks1"), col[:, 2:3], col[:, 3:4], wa("cos1"), wa("sin1")), None, False)
                stage(store_x(x1_b[:, bass.ds(b, 1), :, :]))

        def experts(S, block, func, w_up, w_down, bias, weight, acc, hbuf, tail_pe, tail_dve, head_pe, head_dve,
                    head_act, head_pool, tail_pool):
            @block.tensor
            def _(pe):
                head_pe(pe)

                def up(e):
                    for f in range(NF):
                        n = e * NF + f
                        if n >= 2:
                            pe.wait_ge(S("acted"), n - 1)
                        pe.matmul(bank[:, n % 2, :], w_up[:, n * P:(n + 1) * P], hT[:, :],
                                  start=True, stop=True).then_inc(S("up"), 1)

                def down(e):
                    pe.wait_ge(S("acted"), NF * (e + 1))
                    if e >= 2:
                        pe.wait_ge(S("mixed"), e - 1)
                    for j in range(NT):
                        for f in range(NF):
                            n = e * NF + f
                            i = pe.matmul(bank[:, 2 + e % 2, j * P:(j + 1) * P], hbuf[:, n % 8, j * P:(j + 1) * P],
                                          w_down[:, n * P:(n + 1) * P], start=f == 0, stop=f == NF - 1)
                    i.then_inc(S("down"), 1)

                up(0)
                for e in range(E8):
                    if e + 1 < E8:
                        up(e + 1)
                    down(e)
                tail_pe(pe)

            @block.scalar
            def _(act):
                head_act(act)
                for n in range(E8 * NF):
                    act.wait_ge(S("up"), n + 1)
                    if n % NF == 0 and n >= 2 * NF:
                        act.wait_ge(S("down"), n // NF - 1)
                    act.activation(hbuf[:, n % 8, :], bank[:, n % 2, :], func,
                                   bias=bias[:, n:n + 1] if bias is not None else 0.0).then_inc(S("acted"), 1)

            @block.vector
            def _(dve):
                chain = Chain(dve, S("vector_chain"))
                head_dve(dve, chain)
                for e in range(E8):
                    dve.wait_ge(S("down"), e + 1)
                    if e:
                        dve.wait_ge(S("mixed"), e)
                    for j in range(NT):
                        src = bank[:, 2 + e % 2, j * P:(j + 1) * P]
                        if e == 0:
                            i = dve.tensor_scalar(acc[:, j, :], src, weight[:, j, e:e + 1], None, ALU.mult)
                        else:
                            i = dve.scalar_tensor_tensor(acc[:, j, :], src, weight[:, j, e:e + 1], acc[:, j, :],
                                                         ALU.mult, ALU.add)
                    i.then_inc(S("mixed"), 1)
                dve.wait_ge(S("mixed"), E8)
                tail_dve(dve, chain)

            @block.gpsimd
            def _(gp):
                chain = Chain(gp, S("gpsimd_chain"))
                head_pool(gp, chain)
                tail_pool(gp, chain)

        with ExitStack() as ctx:
            w_b = sb(ctx, "w_b", [P, width(PACK_B)])
            wb = Pieces(w_b, PACK_B)
            b2_sb = sb(ctx, "b2_sb", [E8, C])
            prepare(None, [(w_b, pb), (b2_sb, b2)])
            at = [0]
            qkT, v_sb, s32, e32, pT, acc, hold, hbuf = (carve(buf["prob"], at, shape) for shape in (
                [P, 2, T], [P, NT, C], [P, 2, T], [P, 2, T], [P, 2, T], [P, NT, C], [P, NT, C], [P, 8, T]))
            smx = sb(ctx, "smx", [P, NT, SH])
            ssum = sb(ctx, "ssum", [P, NT, SH])
            srec = sb(ctx, "srec", [P, NT, SH])
            lg = sb(ctx, "lg", [P, 4, NT, E8])
            big8 = sb(ctx, "big8", [P, 2, 256])
            mT = sb(ctx, "mT", [E8, T])

            def rep(piece):
                return piece.unsqueeze(1).broadcast_to([P, NT, C])

            def mha(block, S):
                @block.vector
                def _(dve):
                    chain = Chain(dve, S("vector_chain"))
                    norm_dve(dve, chain, S, "outer", x_sb, y_sb).then_inc(S("normed"), 1)
                    dve.wait_ge(S("turned"), 1)
                    dve.tensor_copy(hT[:, :], bank[:, 7, :]).then_inc(S("hT_ready"), 1)
                    dve.wait_ge(S("v_projected"), 1)
                    dve.tensor_tensor(v_sb[:, :, :], bank[:, 6, :].rearrange("p (t c) -> p t c", t=NT), rep(wb("bv")),
                                      ALU.add).then_inc(S("v_ready"), 1)
                    for j in range(NT):
                        s4 = bank[:, 2:6, j * P:(j + 1) * P]
                        dve.wait_ge(S("scored"), 1)
                        chain(dve.tensor_reduce(smx[:, j, :], s4, AX.X, ALU.max))
                        if j >= 2:
                            dve.wait_ge(S("exped"), j - 1)
                        dve.tensor_tensor(s32[:, j % 2, :].rearrange("p (h k) -> p h k", h=SH), s4,
                                          smx[:, j, :].unsqueeze(2).broadcast_to([P, SH, P]),
                                          ALU.subtract).then_inc(S("centred"), 1)
                        dve.wait_ge(S("exped"), j + 1)
                        chain(dve.tensor_reduce(ssum[:, j, :], e32[:, j % 2, :].rearrange("p (h k) -> p h k", h=SH),
                                                AX.X, ALU.add))
                        chain(dve.reciprocal(srec[:, j, :], ssum[:, j, :]))
                        dve.wait_ge(S("av"), j + 1)
                        dve.tensor_tensor(h_sb[:, j, :].rearrange("p (h d) -> p h d", h=SH),
                                          bank[:, 6 + j % 2, 0:P].rearrange("p (h d) -> p h d", h=SH),
                                          srec[:, j, :].unsqueeze(2).broadcast_to([P, SH, SD]),
                                          ALU.mult).then_inc(S("o_normed"), 1)
                    dve.wait_ge(S("o_back"), 1)
                    dve.tensor_copy(hT[:, :], bank[:, 7, :]).then_inc(S("oT_ready"), 1)
                    dve.wait_ge(S("base_ready"), 1)
                    dve.wait_ge(S("out_projected"), 1)
                    chain(dve.tensor_tensor(acc[:, :, :], base[:, :, :],
                                            bank[:, 0, :].rearrange("p (t c) -> p t c", t=NT), ALU.add))
                    chain(norm_dve(dve, chain, S, "post", acc, h_sb))
                    chain(dve.tensor_tensor(h_sb[:, :, :], h_sb[:, :, :], rep(wb("g1")), ALU.mult))
                    dve.tensor_tensor(hold[:, :, :], h_sb[:, :, :], rep(wb("be1")), ALU.add).then_inc(S("done"), 1)

                @block.gpsimd
                def _(gp):
                    chain = Chain(gp, S("gpsimd_chain"))
                    norm_pool(gp, chain, S, "outer")
                    gp.wait_ge(S("normed"), 1)
                    for j in range(NT):
                        i = gp.tensor_tensor(base[:, j, :], y_sb[:, j, :], wb("bo"), ALU.add)
                    i.then_inc(S("base_ready"), 1)
                    norm_pool(gp, chain, S, "post")

                @block.scalar
                def _(act):
                    act.wait_ge(S("qk_projected"), 1)
                    act.activation(qkT[:, 0, :], bank[:, 0, :], ACT.Identity, bias=wb("cols")[:, 0:1])
                    act.activation(qkT[:, 1, :], bank[:, 1, :], ACT.Identity, bias=wb("cols")[:, 1:2]).then_inc(S("qk_taken"), 1)
                    for j in range(NT):
                        act.wait_ge(S("centred"), j + 1)
                        if j >= 2:
                            act.wait_ge(S("p_turned"), j - 1)
                            act.wait_ge(S("o_normed"), j - 1)
                        act.activation(e32[:, j % 2, :], s32[:, j % 2, :], ACT.Exp,
                                       scale=float(SD) ** -0.5).then_inc(S("exped"), 1)
                        act.wait_ge(S("p_turned"), j + 1)
                        if j >= 2:
                            act.wait_ge(S("av"), j - 1)
                        act.activation(pT[:, j % 2, :], bank[:, j % 2, :], ACT.Copy).then_inc(S("pT_ready"), 1)

                @block.tensor
                def _(pe):
                    pe.wait_ge(S("normed"), 1)
                    turn(pe, y_sb, 7).then_inc(S("turned"), 1)
                    pe.wait_ge(S("hT_ready"), 1)
                    pe.matmul(bank[:, 0, :], wb("wq"), hT[:, :], start=True, stop=True)
                    pe.matmul(bank[:, 1, :], wb("wk"), hT[:, :], start=True, stop=True).then_inc(S("qk_projected"), 1)
                    for j in range(NT):
                        i = pe.matmul(bank[:, 6, j * P:(j + 1) * P], hT[:, j * P:(j + 1) * P], wb("wv"),
                                      start=True, stop=True)
                    i.then_inc(S("v_projected"), 1)
                    pe.wait_ge(S("qk_taken"), 1)

                    for h in range(SH):
                        pe.matmul(bank[:, 2 + h, :], identb, kb("block"), start=True, stop=False,
                                  skip_group_check=True)
                    for j in range(NT):
                        for h in range(SH):
                            i = pe.matmul(bank[:, 2 + h, j * P:(j + 1) * P],
                                          qkT[SD * h:SD * (h + 1), 0, j * P:(j + 1) * P],
                                          qkT[SD * h:SD * (h + 1), 1, j * P:(j + 1) * P], start=False,
                                          stop=j == NT - 1, skip_group_check=True)
                    i.then_inc(S("scored"), 1)
                    for j in range(NT):
                        pe.wait_ge(S("exped"), j + 1)
                        if j >= 2:
                            pe.wait_ge(S("pT_ready"), j - 1)
                        for h in range(SH):
                            i = pe.transpose(bank[:, j % 2, h * P:(h + 1) * P], e32[:, j % 2, h * P:(h + 1) * P], ident)
                        i.then_inc(S("p_turned"), 1)
                        pe.wait_ge(S("pT_ready"), j + 1)
                        if j == 0:
                            pe.wait_ge(S("v_ready"), 1)
                        if j >= 2:
                            pe.wait_ge(S("o_normed"), j - 1)
                        for h in range(SH):
                            i = pe.matmul(bank[:, 6 + j % 2, h * SD:(h + 1) * SD], pT[:, j % 2, h * P:(h + 1) * P],
                                          v_sb[:, j, h * SD:(h + 1) * SD], start=True, stop=True)
                        i.then_inc(S("av"), 1)
                    pe.wait_ge(S("o_normed"), NT)
                    turn(pe, h_sb, 7).then_inc(S("o_back"), 1)
                    pe.wait_ge(S("oT_ready"), 1)
                    for j in range(NT):
                        i = pe.matmul(bank[:, 0, j * P:(j + 1) * P], hT[:, j * P:(j + 1) * P], wb("wo"),
                                      start=True, stop=True)
                    i.then_inc(S("out_projected"), 1)

            def moe1(block, S):
                mask = lg[:, 2]

                def head_pe(pe):
                    turn(pe, hold, 7).then_inc(S("turned"), 1)
                    pe.wait_ge(S("hT_ready"), 1)
                    for j in range(NT):
                        i = pe.matmul(bank[:, 6, j * E8:(j + 1) * E8], hT[:, j * P:(j + 1) * P], wb("wg"),
                                      start=True, stop=True)
                    i.then_inc(S("logits"), 1)

                def head_dve(dve, chain):
                    dve.wait_ge(S("turned"), 1)
                    dve.tensor_copy(hT[:, :], bank[:, 7, :]).then_inc(S("hT_ready"), 1)
                    dve.wait_ge(S("logits"), 1)
                    chain(dve.tensor_copy(lg[:, 0], bank[:, 6, 0:NT * E8].rearrange("p (t e) -> p t e", t=NT)))
                    rank(dve, chain, big8, lg[:, 0], E8, tri(E8), lg[:, 1])
                    dve.tensor_scalar(mask, lg[:, 1], 0.5, None, ALU.is_lt).then_inc(S("mask_ready"), 1)
                    dve.wait_ge(S("mask_ready"), 1)

                def tail_pe(pe):
                    pe.wait_ge(S("mask_ready"), 1)
                    for j in range(NT):
                        i = pe.transpose(bank[0:E8, 5, j * P:(j + 1) * P], lg[:, 2, j, :], ident)
                    i.then_inc(S("mask_turned"), 1)
                    pe.wait_ge(S("mT_ready"), 1)
                    for j in range(NT):
                        i = pe.matmul(bank[:, 4, j * P:(j + 1) * P], mT[:, j * P:(j + 1) * P], b2_sb[:, :],
                                      start=True, stop=True)
                    i.then_inc(S("bias2"), 1)

                def tail_dve(dve, chain):
                    dve.wait_ge(S("mask_turned"), 1)
                    dve.tensor_copy(mT[:, :], bank[0:E8, 5, :]).then_inc(S("mT_ready"), 1)
                    chain(dve.tensor_tensor(acc[:, :, :], acc[:, :, :], hold[:, :, :], ALU.add))
                    dve.wait_ge(S("bias2"), 1)
                    chain(dve.tensor_tensor(acc[:, :, :], acc[:, :, :],
                                            bank[:, 4, :].rearrange("p (t c) -> p t c", t=NT), ALU.add))
                    chain(norm_dve(dve, chain, S, "post", acc, h_sb))
                    chain(dve.tensor_tensor(h_sb[:, :, :], h_sb[:, :, :], rep(wb("g2")), ALU.mult))
                    dve.wait_ge(S("base_ready"), 1)
                    dve.tensor_tensor(x_sb[:, :, :], h_sb[:, :, :], base[:, :, :], ALU.add).then_inc(S("done"), 1)

                def head_pool(gp, chain):
                    for j in range(NT):
                        i = gp.tensor_tensor(base[:, j, :], x_sb[:, j, :], wb("be2"), ALU.add)
                    i.then_inc(S("base_ready"), 1)

                experts(S, block, ACT.Relu, wb("w1"), wb("w2"), wb("b1"), mask, acc, hbuf, tail_pe, tail_dve,
                        head_pe, head_dve, lambda act: None, head_pool, lambda gp, chain: norm_pool(gp, chain, S, "post"))

            def slices(t, i):
                v = t.rearrange("(s i j l) c -> s l i j c", s=SB, i=T // 64, j=NT)
                return [v[s, :, bass.ds(i, 1), :, :] for s in range(SB)]

            def move(i, tensor, store):
                def body(block, S):
                    @block.sync
                    def _(sp):
                        for s, v in enumerate(slices(tensor, i)):
                            own = x_sb[s * 16:(s + 1) * 16, :, :]
                            sp.dma_start(v if store else own, own if store else v).then_inc(S("moved"), 16)
                        sp.wait_ge(S("moved"), 16 * SB)
                return body

            with nc.Fori(0, T // 64) as i:
                stage(move(i, x1, False))
                stage(mha)
                stage(moe1)
                stage(move(i, x2, True))

        with ExitStack() as ctx:
            w_c = sb(ctx, "w_c", [P, width(PACK_C)])
            wc = Pieces(w_c, PACK_C)
            acoef = sb(ctx, "acoef", [P, NGR])

            def mamba(m):
                xpad, conv, e2, xs, zs, u2, dtx, r2, parts2, G, Bb, Cb, ab, ub, hb, hc, yf = (m[k] for k in (
                    "xpad", "conv", "e2", "xs", "zs", "u2", "dtx", "r2", "parts2", "G", "Bb", "Cb", "ab", "ub",
                    "hb", "hc", "yf"))

                def body(block, S):
                    def two(b):
                        return bank[:, b:b + 2, :]

                    @block.vector
                    def _(dve):
                        chain = Chain(dve, S("vector_chain"))
                        norm_dve(dve, chain, S, "outer", x_sb, y_sb).then_inc(S("normed"), 1)
                        dve.wait_ge(S("turned"), 1)
                        dve.tensor_copy(hT[:, :], bank[:, 7, :]).then_inc(S("hT_ready"), 1)
                        dve.wait_ge(S("x_taken"), 1)
                        for c in range(NCH):
                            i = dve.tensor_scalar(conv[:, c, :], xpad[:, c, 0:T], wc("convw")[:, c * DC:c * DC + 1],
                                                  wc("convb")[:, c:c + 1], ALU.mult, ALU.add)
                        chain(i)
                        for k in range(1, DC):
                            for c in range(NCH):
                                i = dve.scalar_tensor_tensor(conv[:, c, :], xpad[:, c, k:k + T],
                                                             wc("convw")[:, c * DC + k:c * DC + k + 1], conv[:, c, :],
                                                             ALU.mult, ALU.add)
                            if k < DC - 1:
                                chain(i)
                        i.then_inc(S("convolved"), 1)
                        dve.wait_ge(S("z_exp"), 1)
                        chain(dve.tensor_scalar(zs[:, :, :], zs[:, :, :], 1.0, None, ALU.add))
                        chain(dve.reciprocal(zs[:, :, :], zs[:, :, :]))
                        dve.tensor_tensor(zs[:, :, :], two(2), zs[:, :, :], ALU.mult)
                        dve.wait_ge(S("x_exp"), 1)
                        chain(dve.tensor_scalar(e2[:, :, :], e2[:, :, :], 1.0, None, ALU.add))
                        chain(dve.reciprocal(e2[:, :, :], e2[:, :, :]))
                        dve.tensor_tensor(xs[:, :, :], conv[:, :, :], e2[:, :, :], ALU.mult).then_inc(S("xs_ready"), 1)
                        dve.wait_ge(S("x_dbl"), 1)
                        for c in range(NCH):
                            i = dve.tensor_scalar(u2[:, c, :], bank[:, 4, :], wc("wdt")[:, c:c + 1], wc("bdt")[:, c:c + 1],
                                                  ALU.mult, ALU.add)
                        i.then_inc(S("dt_in"), 1)
                        e, s, z, q = r2[:, 1], r2[:, 0], e2[:, :, :], conv[:, :, :]
                        dve.wait_ge(S("e_ready"), 1)
                        chain(dve.tensor_scalar(z, e, 2.0, None, ALU.add))
                        chain(dve.reciprocal(q, z))
                        chain(dve.tensor_tensor(s, e, q, ALU.mult))
                        chain(dve.tensor_tensor(z, s, s, ALU.mult))
                        chain(dve.tensor_scalar(q, z, LOG1P[-1], None, ALU.mult))
                        for coefficient in LOG1P[-2:0:-1]:
                            chain(dve.scalar_tensor_tensor(q, q, coefficient, z, ALU.add, ALU.mult))
                        chain(dve.scalar_tensor_tensor(q, q, LOG1P[0], s, ALU.add, ALU.mult))
                        chain(dve.scalar_tensor_tensor(dtx[:, 0, :, :], u2[:, :, :], 0.0, q, ALU.max, ALU.add))
                        chain(dve.tensor_tensor(dtx[:, 1, :, :], dtx[:, 0, :, :], xs[:, :, :], ALU.mult))
                        chain(dve.tensor_copy(parts2[:, 0], dtx[:, :, :, :]))
                        chain(dve.tensor_tensor(r2[:, :, :, :], dtx[:, :, :, :], parts2[:, 0], ALU.subtract))
                        chain(dve.tensor_copy(parts2[:, 1], r2[:, :, :, :]))
                        dve.tensor_tensor(parts2[:, 2], r2[:, :, :, :], parts2[:, 1], ALU.subtract).then_inc(S("parts_ready"), 1)
                        dve.wait_ge(S("bc_taken"), 1)
                        for g in range(NGR):
                            dve.wait_ge(S("dtx_spread"), g + 1)
                            dve.tensor_tensor(ub[:, g % 2, :], bank[:, 2 + g % 2, :], Bb[:, :], ALU.mult).then_inc(S("u_ready"), 1)
                            dve.wait_ge(S("decay"), g + 1)
                            dve.wait_ge(S("u_ready"), g + 1)
                            if g >= 3:
                                dve.wait_ge(S("hc_ready"), g - 2)
                            dve.tensor_tensor_scan(hb[:, g % 3, :], ab[:, g % 2, :], ub[:, g % 2, :], 0.0,
                                                   ALU.mult, ALU.add).then_inc(S("scanned"), 1)
                        dve.wait_ge(S("summed"), NGR)
                        for c in range(NCH):
                            i = dve.scalar_tensor_tensor(yf[:, c, :], xs[:, c, :], wc("dcol")[:, c:c + 1], bank[:, 5 + c, :],
                                                         ALU.mult, ALU.add)
                        chain(i)
                        dve.tensor_tensor(yf[:, :, :], yf[:, :, :], zs[:, :, :], ALU.mult).then_inc(S("gated"), 1)
                        dve.wait_ge(S("out_projected"), 1)
                        dve.tensor_tensor(x_sb[:, :, :], x_sb[:, :, :], bank[:, 4, :].rearrange("p (t c) -> p t c", t=NT),
                                          ALU.add).then_inc(S("done"), 1)

                    @block.gpsimd
                    def _(gp):
                        chain = Chain(gp, S("gpsimd_chain"))
                        norm_pool(gp, chain, S, "outer")
                        gp.wait_ge(S("bc_taken"), 1)
                        for g in range(NGR):
                            gp.wait_ge(S("scanned"), g + 1)
                            if g >= 3:
                                gp.wait_ge(S("summed"), g - 2)
                            gp.tensor_tensor(hc[:, g % 3, :], hb[:, g % 3, :], Cb[:, :], ALU.mult).then_inc(S("hc_ready"), 1)

                    @block.scalar
                    def _(act):
                        act.wait_ge(S("in_projected"), 1)
                        act.activation(xpad[:, :, DC - 1:DC - 1 + T], two(0), ACT.Copy).then_inc(S("x_taken"), 1)
                        act.activation(zs[:, :, :], two(2), ACT.Exp, scale=-1.0).then_inc(S("z_exp"), 1)
                        act.wait_ge(S("convolved"), 1)
                        act.activation(e2[:, :, :], conv[:, :, :], ACT.Exp, scale=-1.0).then_inc(S("x_exp"), 1)
                        act.wait_ge(S("x_dbl"), 1)
                        act.activation(Bb[:, :], bank[:, 5, :], ACT.Copy)
                        act.activation(Cb[:, :], bank[:, 6, :], ACT.Copy).then_inc(S("bc_taken"), 1)
                        act.wait_ge(S("dt_in"), 1)
                        act.activation(r2[:, 0], u2[:, :, :], ACT.Abs).then_inc(S("scalar_chain"), 1)
                        act.wait_ge(S("scalar_chain"), 1)
                        act.activation(r2[:, 1], r2[:, 0], ACT.Exp, scale=-1.0).then_inc(S("e_ready"), 1)
                        for g in range(NGR):
                            act.wait_ge(S("dt_spread"), g + 1)
                            if g >= 2:
                                act.wait_ge(S("scanned"), g - 1)
                            act.activation(ab[:, g % 2, :], bank[:, g % 2, :], ACT.Exp, scale=acoef[:, g:g + 1]).then_inc(S("decay"), 1)

                    @block.sync
                    def _(sp):
                        sp.wait_ge(S("parts_ready"), 1)
                        for i in range(3):
                            for q in range(2):
                                sp.dma_start(dt_dram[i, q].rearrange("(c p) t -> p c t", p=P),
                                             parts2[:, i, q]).then_inc(S("parts_stored"), 16)
                        sp.wait_ge(S("parts_stored"), 96)
                        for i in range(3):
                            for q in range(2):
                                sp.dma_start(G[32 * i:32 * i + 32, q, :, :],
                                             dt_dram[i, q].rearrange("(b l) t -> l b t", l=32)).then_inc(S("grouped"), 16)

                    @block.tensor
                    def _(pe):
                        pe.wait_ge(S("normed"), 1)
                        turn(pe, y_sb, 7).then_inc(S("turned"), 1)
                        pe.wait_ge(S("hT_ready"), 1)
                        for c in range(4):
                            i = pe.matmul(bank[:, c, :], wc("win")[:, c * P:(c + 1) * P], hT[:, :], start=True, stop=True)
                        i.then_inc(S("in_projected"), 1)
                        pe.wait_ge(S("xs_ready"), 1)
                        for n, w in enumerate(("wxd", "wxb", "wxc")):
                            for c in range(NCH):
                                i = pe.matmul(bank[:, 4 + n, :], wc(w)[:, c * P:(c + 1) * P], xs[:, c, :],
                                              start=c == 0, stop=c == NCH - 1)
                        i.then_inc(S("x_dbl"), 1)
                        pe.wait_ge(S("grouped"), 96)
                        pe.wait_ge(S("x_taken"), 1)
                        pe.wait_ge(S("bc_taken"), 1)

                        def spread(g):
                            if g >= 2:
                                pe.wait_ge(S("decay"), g - 1)
                            sel = kb("selG", 96)[:, (g % 4) * P:(g % 4 + 1) * P]
                            pe.matmul(bank[:, g % 2, :], sel, G[0:96, 0, g // 4, :], start=True, stop=True).then_inc(S("dt_spread"), 1)
                            if g >= 2:
                                pe.wait_ge(S("u_ready"), g - 1)
                            pe.matmul(bank[:, 2 + g % 2, :], sel, G[0:96, 1, g // 4, :], start=True, stop=True).then_inc(S("dtx_spread"), 1)

                        def collect(g):
                            pe.wait_ge(S("hc_ready"), g + 1)
                            c, q = g // 16, g // 4 % 4
                            pe.matmul(bank[32 * q:32 * q + 32, 5 + c, :], m["selY"][:, (g % 4) * 32:(g % 4 + 1) * 32],
                                      hc[:, g % 3, :], start=g % 4 == 0, stop=g % 4 == 3,
                                      skip_group_check=True).then_inc(S("summed"), 1)

                        for g in range(NGR + 2):
                            if g < NGR:
                                spread(g)
                            if g >= 2:
                                collect(g - 2)
                        pe.wait_ge(S("gated"), 1)
                        for j in range(NT):
                            for c in range(NCH):
                                i = pe.matmul(bank[:, 4, j * P:(j + 1) * P], yf[:, c, j * P:(j + 1) * P],
                                              wc("wout")[:, c * P:(c + 1) * P], start=c == 0, stop=c == NCH - 1)
                        i.then_inc(S("out_projected"), 1)
                stage(body)

            def moe2(m):
                lg, big8, acc, hbuf = m["lg2"], m["big8b"], m["acc2"], m["hbuf2"]

                def body(block, S):
                    def head_pe(pe):
                        pe.wait_ge(S("normed"), 1)
                        turn(pe, y_sb, 7).then_inc(S("turned"), 1)
                        pe.wait_ge(S("hT_ready"), 1)
                        for j in range(NT):
                            i = pe.matmul(bank[:, 6, j * E8:(j + 1) * E8], hT[:, j * P:(j + 1) * P], wc("gw"),
                                          start=True, stop=True)
                        i.then_inc(S("logits"), 1)

                    def head_dve(dve, chain):
                        norm_dve(dve, chain, S, "outer", x_sb, y_sb).then_inc(S("normed"), 1)
                        dve.wait_ge(S("turned"), 1)
                        dve.tensor_copy(hT[:, :], bank[:, 7, :]).then_inc(S("hT_ready"), 1)
                        dve.wait_ge(S("logits"), 1)
                        row = [P, NT, E8]
                        chain(dve.tensor_tensor(lg[:, 0], bank[:, 6, 0:NT * E8].rearrange("p (t e) -> p t e", t=NT),
                                                wc("eb").unsqueeze(1).broadcast_to(row), ALU.add))
                        one = lg[:, 6, :, 0:1]
                        chain(dve.tensor_reduce(one, lg[:, 0], AX.X, ALU.max))
                        dve.tensor_tensor(lg[:, 1], lg[:, 0], one.broadcast_to(row), ALU.subtract).then_inc(S("centred"), 1)
                        dve.wait_ge(S("exped"), 1)
                        chain(dve.tensor_reduce(lg[:, 6, :, 1:2], lg[:, 2], AX.X, ALU.add))
                        chain(dve.reciprocal(lg[:, 6, :, 2:3], lg[:, 6, :, 1:2]))
                        chain(dve.tensor_tensor(lg[:, 3], lg[:, 2], lg[:, 6, :, 2:3].broadcast_to(row), ALU.mult))
                        rank(dve, chain, big8, lg[:, 3], E8, tri(E8), lg[:, 4])
                        chain(dve.tensor_scalar(lg[:, 4], lg[:, 4], 1.5, None, ALU.is_lt))
                        chain(dve.tensor_tensor(lg[:, 3], lg[:, 3], lg[:, 4], ALU.mult))
                        chain(dve.tensor_reduce(lg[:, 6, :, 3:4], lg[:, 3], AX.X, ALU.add))
                        chain(dve.tensor_scalar(lg[:, 6, :, 4:5], lg[:, 6, :, 3:4], 1e-6, None, ALU.add))
                        chain(dve.reciprocal(lg[:, 6, :, 5:6], lg[:, 6, :, 4:5]))
                        chain(dve.tensor_tensor(lg[:, 5], lg[:, 3], lg[:, 6, :, 5:6].broadcast_to(row), ALU.mult))

                    def tail_dve(dve, chain):
                        chain(norm_dve(dve, chain, S, "post", acc, h_sb))
                        dve.wait_ge(S("base_ready"), 1)
                        dve.tensor_tensor(x_sb[:, :, :], h_sb[:, :, :], base[:, :, :], ALU.add).then_inc(S("done"), 1)

                    def head_act(act):
                        act.wait_ge(S("centred"), 1)
                        act.activation(lg[:, 2], lg[:, 1], ACT.Exp).then_inc(S("exped"), 1)

                    def head_pool(gp, chain):
                        norm_pool(gp, chain, S, "outer")
                        gp.wait_ge(S("normed"), 1)
                        gp.tensor_tensor(base[:, :, :], x_sb[:, :, :], y_sb[:, :, :], ALU.add).then_inc(S("base_ready"), 1)

                    experts(S, block, ACT.Gelu, wc("wup"), wc("wdn"), None, lg[:, 5], acc, hbuf, lambda pe: None,
                            tail_dve, head_pe, head_dve, head_act, head_pool,
                            lambda gp, chain: norm_pool(gp, chain, S, "post"))
                stage(body)

            def lora3(m, dst):
                mid, gt = m["mid"], m["gt3"]

                def body(block, S):
                    @block.vector
                    def _(dve):
                        chain = Chain(dve, S("vector_chain"))
                        norm_dve(dve, chain, S, "outer", x_sb, y_sb).then_inc(S("normed"), 1)
                        dve.wait_ge(S("turned"), 1)
                        i = dve.tensor_copy(hT[:, :], bank[:, 7, :])
                        chain(i)
                        dve.tensor_copy(m["cls"][:, :], hT[:, 0:1].broadcast_to([P, P])).then_inc(S("hT_ready"), 1)
                        dve.wait_ge(S("logits"), 1)
                        chain(dve.tensor_copy(gt[:, 0], bank[:, 6, 0:E8]))
                        shape = [P, E8, E8]
                        a, b = (m["big8b"][:, i, 0:64].rearrange("p (a b) -> p a b", a=E8) for i in range(2))
                        dve.tensor_tensor(a, gt[:, 0].unsqueeze(1).broadcast_to(shape), gt[:, 0].unsqueeze(2).broadcast_to(shape), ALU.is_gt)
                        chain(dve.tensor_tensor(b, gt[:, 0].unsqueeze(1).broadcast_to(shape), gt[:, 0].unsqueeze(2).broadcast_to(shape), ALU.is_equal))
                        chain(dve.tensor_tensor(b, b, tri(E8), ALU.mult))
                        chain(dve.tensor_tensor(a, a, b, ALU.add))
                        chain(dve.tensor_reduce(gt[:, 1], a, AX.X, ALU.add))
                        chain(dve.tensor_scalar(gt[:, 1], gt[:, 1], 1.5, None, ALU.is_lt))
                        chain(dve.tensor_reduce(gt[:, 6, 0:1], gt[:, 0], AX.X, ALU.max))
                        dve.tensor_scalar(gt[:, 2], gt[:, 0], gt[:, 6, 0:1], None, ALU.subtract).then_inc(S("centred"), 1)
                        dve.wait_ge(S("exped"), 1)
                        chain(dve.tensor_tensor(gt[:, 4], gt[:, 3], gt[:, 1], ALU.mult))
                        chain(dve.tensor_reduce(gt[:, 6, 1:2], gt[:, 4], AX.X, ALU.add))
                        chain(dve.reciprocal(gt[:, 6, 2:3], gt[:, 6, 1:2]))
                        chain(dve.tensor_scalar(gt[:, 5], gt[:, 4], gt[:, 6, 2:3], None, ALU.mult))
                        pair = gt[:, 5].rearrange("p (c two) -> p c two", two=2)
                        dve.tensor_copy(gt[0:64, 7, 0:4], pair[0:64, :, 0])
                        dve.tensor_copy(gt[64:128, 7, 0:4], pair[64:128, :, 1]).then_inc(S("gates_ready"), 1)
                        dve.wait_ge(S("out"), 1)
                        dve.wait_ge(S("base_ready"), 1)
                        dve.tensor_tensor(x_sb[:, :, :], base[:, :, :], bank[:, 4, :].rearrange("p (t c) -> p t c", t=NT),
                                          ALU.add).then_inc(S("done"), 1)

                    @block.gpsimd
                    def _(gp):
                        chain = Chain(gp, S("gpsimd_chain"))
                        norm_pool(gp, chain, S, "outer")
                        gp.wait_ge(S("normed"), 1)
                        gp.tensor_tensor(base[:, :, :], x_sb[:, :, :], y_sb[:, :, :], ALU.add).then_inc(S("base_ready"), 1)

                    @block.scalar
                    def _(act):
                        act.wait_ge(S("centred"), 1)
                        act.activation(gt[:, 3], gt[:, 2], ACT.Exp).then_inc(S("exped"), 1)
                        act.wait_ge(S("gates_ready"), 1)
                        act.wait_ge(S("mid"), 1)
                        for c in range(4):
                            i = act.activation(mid[:, c, :], bank[:, c, :], ACT.Copy, scale=gt[:, 7, c:c + 1])
                        i.then_inc(S("mid_ready"), 1)

                    @block.tensor
                    def _(pe):
                        pe.wait_ge(S("normed"), 1)
                        turn(pe, y_sb, 7).then_inc(S("turned"), 1)
                        pe.wait_ge(S("hT_ready"), 1)
                        pe.matmul(bank[:, 6, 0:E8], m["cls"][:, :], wc("wr3"), start=True, stop=True).then_inc(S("logits"), 1)
                        for c in range(4):
                            i = pe.matmul(bank[:, c, :], wc("a3")[:, c * P:(c + 1) * P], hT[:, :], start=True, stop=True)
                        i.then_inc(S("mid"), 1)
                        pe.wait_ge(S("mid_ready"), 1)
                        for j in range(NT):
                            for c in range(4):
                                i = pe.matmul(bank[:, 4, j * P:(j + 1) * P], mid[:, c, j * P:(j + 1) * P],
                                              wc("b3")[:, c * P:(c + 1) * P], start=c == 0, stop=c == 3)
                        i.then_inc(S("out"), 1)

                    @block.sync
                    def _(sp):
                        sp.wait_ge(S("done"), 1)
                        sp.dma_start(dst, x_sb[:, :, :]).then_inc(S("x_stored"), 16)
                        sp.wait_ge(S("x_stored"), 16)
                stage(body)

            def prepare_c(m):
                def body(block, S):
                    @block.scalar
                    def _(act):
                        act.activation(acoef[:, :], wc("alog"), ACT.Exp).then_inc(S("a_exp"), 1)

                    @block.vector
                    def _(dve):
                        dve.memset(m["xpad"][:, :, 0:DC - 1], 0.0)
                        dve.wait_ge(S("a_exp"), 1)
                        dve.tensor_scalar(acoef[:, :], acoef[:, :], -1.0, None, ALU.mult)

                    @block.sync
                    def _(sp):
                        sp.dma_start(m["selY"][:, :], m["selY_src"]).then_inc(S("sel"), 16)
                        sp.wait_ge(S("sel"), 16)
                stage(body)

            small = sb(ctx, "small", [P, NCH, DC - 1 + T])
            prob = buf["prob"]

            at = [0]
            m = {"xpad": small[:, :, :], "selY_src": pk_sel}
            for name, shape, dt in (("conv", [P, 2, T], F32), ("e2", [P, 2, T], F32), ("xs", [P, 2, T], F32),
                                    ("zs", [P, 2, T], F32), ("u2", [P, 2, T], F32), ("dtx", [P, 2, 2, T], F32),
                                    ("r2", [P, 2, 2, T], F32), ("Bb", [P, T], F32),
                                    ("Cb", [P, T], F32), ("yf", [P, 2, T], F32)):
                m[name] = carve(prob, at, shape, dt)
            m["parts2"] = carve(prob, [at[0]], [P, 3, 2, 2, T], BF16)
            for name, n in (("ab", 2), ("ub", 2), ("hb", 3), ("hc", 3)):
                m[name] = carve(prob, at, [P, n, T])
            at = [0]
            for name, shape in (("acc2", [P, NT, C]), ("hbuf2", [P, 8, T])):
                m[name] = carve(prob, at, shape)
            at = [0]
            m["mid"] = carve(prob, at, [P, 4, T])
            m["G"] = buf["Qs"][:, :, :].rearrange("p (q b) t -> p q b t", q=2)
            m["selY"] = sb(ctx, "selY", [P, P])
            m["lg2"] = sb(ctx, "lg2", [P, 7, NT, E8])
            m["big8b"] = sb(ctx, "big8b", [P, 2, 256])
            m["gt3"] = sb(ctx, "gt3", [P, 8, E8])
            m["cls"] = sb(ctx, "cls", [P, P])
            prepare(None, [(w_c, pc)])
            prepare_c(m)

            x2_b = x2.rearrange("(b t p) c -> p b t c", b=B, p=P)
            out_b = out.rearrange("(b t p) c -> p b t c", b=B, p=P)
            with nc.Fori(0, B) as b:
                stage(load_x(x2_b[:, bass.ds(b, 1), :, :]))
                mamba(m)
                moe2(m)
                col = wc("cols3")
                attention(buf, y_sb, x_sb, wc("wq3"), wc("wk3"), wc("wv3"), wc("wo3"), col[:, 0:1], col[:, 1:2],
                          wc("bv3"), None, float(HD) ** -0.5, False, True, None, None, False)
                lora3(m, out_b[:, bass.ds(b, 1), :, :])


def fixed_tables():
    ident = np.eye(P, dtype=np.float32)
    tri16 = np.tile((np.arange(16)[None, :] < np.arange(16)[:, None]).astype(np.float32).reshape(1, 256), (P, 1))
    sel16 = np.zeros((P, 8, P), np.float32)
    for e in range(E0):
        sel16[e, e // 2, (e % 2) * 64:(e % 2 + 1) * 64] = 1
    sel_y = np.zeros((P, 4, 32), np.float32)
    for n in range(DS):
        for l in range(GD):
            for j in range(4):
                sel_y[n * GD + l, j, j * GD + l] = 1
    p = np.arange(P)
    causal = np.where(p[None, :] > p[:, None], NEG, 0.0)
    corner_a, corner_b = np.zeros((P, P)), np.zeros((P, P))
    corner_a[P - 1, 0] = NEG
    corner_b[0, P - 1] = NEG
    same = np.where(p[None, :] % 16 == p[:, None] % 16, 0.0, NEG)
    sel_g = np.zeros((P, 4, P))
    for part in range(3):
        for j in range(4):
            for l in range(GD):
                sel_g[part * 32 + j * GD + l, j, l::GD] = 1
    kb = np.concatenate([ident, causal, causal.T, corner_a, corner_b, np.tile(same, (1, 4)),
                         sel_g.reshape(P, -1), np.ones((P, 512))], 1).astype(np.float32)
    theta = np.power(np.float32(10000.0), (2.0 * np.arange(HD // 2) / HD).astype(np.float32)).astype(np.float32)
    angle = (np.arange(T, dtype=np.float32)[None, :] * theta[:, None]).astype(np.float32).astype(np.float64)
    rows = np.arange(P) % HD
    cos = np.cos(angle)[rows // 2].astype(np.float32)
    sin = (np.sin(angle)[rows // 2] * np.where(rows % 2 == 0, -1.0, 1.0)[:, None]).astype(np.float32)
    return np.concatenate([ident, tri16, sel16.reshape(P, -1)], 1), kb, sel_y.reshape(P, P), cos, sin


def kernel(**inputs):
    import concourse.bacc as bacc
    from concourse.bass_utils import run_bass_kernel_spmd

    a = {k: np.asarray(v) for k, v in inputs.items()}

    def row(v):
        return np.broadcast_to(v.reshape(1, -1), (P, v.size))

    def packed(pieces, pack):
        for (name, n) in pack:
            assert pieces[name].shape == (P, n), (name, pieces[name].shape)
        return np.ascontiguousarray(np.concatenate([pieces[name] for name, _ in pack], 1))

    tables, tables_b, sel_y, cos, sin = fixed_tables()
    wqkv0, bqkv0 = a["L0_attn_w_qkv"], a["L0_attn_b_qkv"]
    swap = np.arange(P) ^ 1
    pa = {
        "wq0": wqkv0[:, 0:128], "wk0": wqkv0[:, 128:256], "wv0": wqkv0[:, 256:384], "wo0": a["L0_attn_w_out"],
        "bv0": row(bqkv0[256:384]), "bo0": row(a["L0_attn_b_out"]),
        "cols0": np.stack([a["L0_attn_ln_gamma"], a["L0_attn_ln_beta"], bqkv0[0:128], bqkv0[128:256]], 1),
        "wg0": a["L0_ffn_Wg"].T, "bc0": row(a["L0_ffn_bias_corr"]),
        "w1_0": a["L0_ffn_W1"].reshape(1024, 128).T, "ws1_0": a["L0_ffn_Ws1"].T,
        "w2_0": a["L0_ffn_W2"].transpose(0, 2, 1).reshape(8, 128, 128).transpose(1, 0, 2).reshape(128, 1024),
        "ws2_0": a["L0_ffn_Ws2"].T,
        "wq1": a["L1_attn_Wq"].T, "wk1": a["L1_attn_Wk"].T, "wv1": a["L1_attn_Wv"].T, "wp1": a["L1_attn_Wp"].T,
        "wqs1": a["L1_attn_Wq"][swap].T, "wks1": a["L1_attn_Wk"][swap].T,
        "bv1": row(a["L1_attn_bv"]), "bp1": row(a["L1_attn_bp"]),
        "cols1": np.stack([a["L1_attn_bq"], a["L1_attn_bk"], a["L1_attn_bq"][swap], a["L1_attn_bk"][swap]], 1),
        "cos1": cos, "sin1": sin,
    }
    wqkv, bqkv = a["L1_ffn_Wqkv"], a["L1_ffn_bqkv"]
    pb = {
        "wq": wqkv[0:128].T, "wk": wqkv[128:256].T, "wv": wqkv[256:384].T, "wo": a["L1_ffn_Wo"].T,
        "cols": np.stack([bqkv[0:128], bqkv[128:256]], 1), "bv": row(bqkv[256:384]), "bo": row(a["L1_ffn_bo"]),
        "g1": row(a["L1_ffn_g1"]), "be1": row(a["L1_ffn_be1"]), "g2": row(a["L1_ffn_g2"]),
        "be2": row(a["L1_ffn_be2"]), "wg": a["L1_ffn_Wg"].T,
        "b1": a["L1_ffn_b1"].reshape(32, 128).T,
        "w1": a["L1_ffn_W1"].transpose(1, 0, 2).reshape(128, 4096),
        "w2": a["L1_ffn_W2"].reshape(32, 128, 128).transpose(1, 0, 2).reshape(128, 4096),
    }
    wx = a["L2_attn_W_x"]

    def chunked(w):
        return w.reshape(2, 128, -1).transpose(1, 0, 2).reshape(128, -1)

    state = np.arange(P) // GD
    pc = {
        "win": a["L2_attn_W_in"], "convw": chunked(a["L2_attn_conv_w"]), "convb": chunked(a["L2_attn_conv_b"]),
        "wxd": chunked(wx[:, np.zeros(P, int)]), "wxb": chunked(wx[:, 1 + state]), "wxc": chunked(wx[:, 17 + state]),
        "wdt": chunked(a["L2_attn_w_dt"]), "bdt": chunked(a["L2_attn_b_dt"]),
        "alog": a["L2_attn_A_log"].reshape(NGR, GD, DS).transpose(2, 1, 0).reshape(P, NGR),
        "dcol": chunked(a["L2_attn_D"]), "wout": chunked(a["L2_attn_W_out"]),
        "gw": a["L2_ffn_gate_w"].T, "eb": row(a["L2_ffn_expert_bias"]),
        "wup": a["L2_ffn_w_up"].transpose(2, 0, 1).reshape(128, 4096),
        "wdn": a["L2_ffn_w_down"].transpose(0, 2, 1).reshape(32, 128, 128).transpose(1, 0, 2).reshape(128, 4096),
        "wq3": a["L3_attn_Wq"].T, "wk3": a["L3_attn_Wk"].T, "wv3": a["L3_attn_Wv"].T, "wo3": a["L3_attn_Wo"].T,
        "cols3": np.stack([a["L3_attn_bq"], a["L3_attn_bk"]], 1), "bv3": row(a["L3_attn_bv"]),
        "wr3": a["L3_ffn_Wr"].T, "a3": a["L3_ffn_A"].reshape(512, 128).T,
        "b3": a["L3_ffn_Bw"].transpose(0, 2, 1).reshape(4, 128, 128).transpose(1, 0, 2).reshape(128, 512),
    }
    arrays = {"x": np.ascontiguousarray(a["L0_attn_x"].reshape(B * T, C)), "pa": packed(pa, PACK_A),
              "pb": packed(pb, PACK_B), "pc": packed(pc, PACK_C), "pk": tables, "pkb": tables_b,
              "b2": np.ascontiguousarray(a["L1_ffn_b2"]), "sel_y": sel_y}
    nc = bacc.Bacc("TRN2", target_bir_lowering=False, num_devices=1)
    handles = {k: nc.dram_tensor(f"in_{k}", v.shape, mybir.dt.from_np(v.dtype), kind="ExternalInput").ap()
               for k, v in arrays.items()}
    out = nc.dram_tensor("out", (B * T, C), F32, kind="ExternalOutput").ap()
    build(nc, *(handles[k] for k in ("x", "pa", "pb", "pc", "pk", "pkb", "b2", "sel_y")), out)
    r = run_bass_kernel_spmd(nc, [{f"in_{k}": v for k, v in arrays.items()}], core_ids=[0])
    return r.results[0]["out"].reshape(B, T, C)
```

```python
from contextlib import ExitStack

import concourse.bass as bass
import numpy as np
from concourse import mybir

F32 = mybir.dt.float32
BF16 = mybir.dt.bfloat16
ALU = mybir.AluOpType
ACT = mybir.ActivationFunctionType
AX = mybir.AxisListType

P = 128
B, T, C = 8, 512, 128
NT = T // P
H, HD = 16, 8
GH = 4
NG = H // GH
TERMS = [(0, 0), (1, 0), (2, 0), (0, 1), (1, 1), (0, 2)]
KT = len(TERMS) * HD
NEG = -3.0e10
EPS = 1e-5
OFFSET_A, OFFSET_B, OFFSET_C = 0.0, 0.0, 0.0
LOG1P = [1.99999999981, 0.666666790265, 0.399987112464, 0.286202074065, 0.213985606305, 0.243939073439]
E0, I0 = 16, 64
E8, FF, NF = 8, 512, 4
SB, SH, SD = 8, 4, 32
DI, DS, DC = 256, 16, 4
NCH = DI // P
GD = P // DS
NGR = DI // GD

PACK_A = [("wq0", 128), ("wk0", 128), ("wv0", 128), ("wo0", 128), ("bv0", 128), ("bo0", 128),
          ("cols0", 4), ("wg0", 16), ("bc0", 16), ("w1_0", 1024), ("ws1_0", 128), ("w2_0", 1024),
          ("ws2_0", 128), ("wq1", 128), ("wk1", 128), ("wv1", 128), ("wp1", 128), ("wqs1", 128),
          ("wks1", 128), ("bv1", 128), ("bp1", 128), ("cols1", 4), ("cos1", 512), ("sin1", 512)]
PACK_B = [("wq", 128), ("wk", 128), ("wv", 128), ("wo", 128), ("cols", 2), ("bv", 128), ("bo", 128),
          ("g1", 128), ("be1", 128), ("g2", 128), ("be2", 128), ("wg", 8), ("b1", 32),
          ("w1", 4096), ("w2", 4096)]
PACK_C = [("win", 512), ("convw", 8), ("convb", 2), ("wxd", 256), ("wxb", 256), ("wxc", 256),
          ("wdt", 2), ("bdt", 2), ("alog", 32), ("dcol", 2), ("wout", 256), ("gw", 8), ("eb", 8),
          ("wup", 4096), ("wdn", 4096), ("wq3", 128), ("wk3", 128), ("wv3", 128), ("wo3", 128),
          ("cols3", 2), ("bv3", 128), ("wr3", 8), ("a3", 512), ("b3", 512)]
PACK_K = [("ident", 128), ("tri16", 256), ("sel16", 1024)]
PACK_KB = [("identb", 128), ("causal", 128), ("causalT", 128), ("cornA", 128), ("cornB", 128),
           ("block", 512), ("selG", 512), ("ones", 512)]


def width(pack):
    return sum(n for _, n in pack)


class Pieces:

    def __init__(self, tensor, pack):
        self.tensor, self.at, o = tensor, {}, 0
        for name, n in pack:
            self.at[name] = (o, n)
            o += n

    def __call__(self, name, p=P):
        o, n = self.at[name]
        return self.tensor[0:p, o:o + n]


class Chain:

    def __init__(self, sem):
        self.sem, self.n = sem, 0

    def __call__(self, eng, instruction):
        self.n += 1
        instruction.then_inc(self.sem, 1)
        eng.wait_ge(self.sem, self.n)


class Stream:

    def __init__(self, index, pool, taken, buffers):
        self.index, self.pool, self.taken, self.buf = index, pool, taken, buffers
        self.named, self.order = {}, {}
        self.chain = {e: Chain(self.sem(e + "_chain")) for e in ("vector", "gpsimd")}
        self.moments, self.rstd = self.sem("moments"), self.sem("rstd")
        self.norms = {"vector": 0, "gpsimd": 0}

    def sem(self, name):
        if name not in self.named:
            self.named[name] = self.pool[self.taken[0]]
            self.taken[0] += 1
        return self.named[name]

    def signals(self, stage, absent=()):
        return Signals(self, stage, absent)


class Signals:
    ONCE = ("normed", "turned", "hT_ready", "done")

    def __init__(self, st, stage, absent):
        self.st, self.stage, self.value = st, stage, {}
        for name in self.ONCE:
            if name not in absent:
                st.order[name] = self.value[name] = st.order.get(name, 0) + 1

    def __call__(self, name):
        return self.st.sem(name if name in self.ONCE else self.stage + name)

    def once(self, name):
        return self.st.sem(name), self.value[name]


def take_turns(programs):
    due = [[next(p), n, p] for n, p in enumerate(programs)]
    while due:
        first = min(due, key=lambda d: (d[0], d[1]))
        mark = next(first[2], None)
        if mark is None:
            due.remove(first)
        else:
            first[0] = mark


ENGINES = ("vector", "gpsimd", "scalar", "sync", "tensor")


def build(nc, x, pa, pb, pc, pk, pkb, b2, sel_y, out):
    top = ExitStack()
    with top:
        def sb(ctx, name, shape, dt=F32):
            return ctx.enter_context(nc.sbuf_tensor(name, shape, dt))

        load_sem = top.enter_context(nc.semaphore("weights_loaded"))
        pool = [top.enter_context(nc.semaphore(f"signal_{i}")) for i in range(150)]
        banks = top.enter_context(nc.psum_tensor("banks", [P, 2, 4, 512], F32))
        kc = Pieces(sb(top, "kc", [P, width(PACK_K)]), PACK_K)
        kb = Pieces(sb(top, "kb", [P, width(PACK_KB)], BF16), PACK_KB)
        ident, identb = kc("ident"), kb("identb")
        mhalf = sb(top, "mhalf", [P, NT])
        x1 = nc.dram_tensor("x1", (B * T, C), F32, kind="Internal").ap()
        x2 = nc.dram_tensor("x2", (B * T, C), F32, kind="Internal").ap()
        parts_dram = nc.dram_tensor("parts_dram", (2, 3, 2, P, T), BF16, kind="Internal").ap()
        dt_dram = nc.dram_tensor("dt_dram", (2, 3, 2, DI, T), BF16, kind="Internal").ap()
        ROOM = 64 * 256

        def buffers(s):
            names = {"x": [P, NT, C], "y": [P, NT, C], "h": [P, NT, C], "base": [P, NT, C], "hT": [P, T],
                     "stats": [P, NT, 6], "mom": [P, NT, 2], "veps": [P, NT], "rstd": [P, NT],
                     "room": [P, ROOM]}
            return {k: sb(top, f"{k}_{s}", v) for k, v in names.items()}

        memory = [buffers(0), buffers(1)]
        loads = [0]

        def stage_block(body):
            with nc.Block() as block:
                body(block)
            nc.all_engine_barrier()

        class Room:

            def __init__(self, st):
                self.t, self.at = st.buf["room"], 0

            def __call__(self, shape, dt=F32):
                n = int(np.prod(shape[1:]))
                words = n if dt == F32 else n // 2
                assert self.at + words <= ROOM, (self.at, words)
                flat = self.t[0:shape[0], self.at:self.at + words]
                self.at += words
                if dt == BF16:
                    flat = flat.bitcast(BF16)
                if len(shape) == 2:
                    return flat
                names = "abcde"[:len(shape) - 1]
                return flat.rearrange("p (%s) -> p %s" % (" ".join(names), " ".join(names)),
                                      **{k: s for k, s in zip(names, shape[1:])})

        def run(index, streams_stages):
            with nc.Block() as block:
                def programs(name, eng):
                    return [program(name, eng) for program in streams_stages]

                @block.vector
                def _(dve):
                    take_turns(programs("vector", dve))

                @block.gpsimd
                def _(gp):
                    take_turns(programs("gpsimd", gp))

                @block.scalar
                def _(act):
                    take_turns(programs("scalar", act))

                @block.sync
                def _(sp):
                    take_turns(programs("sync", sp))

                @block.tensor
                def _(pe):
                    take_turns(programs("tensor", pe))
            nc.gpsimd.sem_clear(range(pool[0].num, pool[-1].num + 1))
            nc.all_engine_barrier()

        def chain_of(stages, start):
            def program(name, eng):
                t = start
                for stage, length, entry in stages:
                    yield t
                    if entry is not None and (name != "sync" or "sync" in stage):
                        eng.wait_ge(*entry)
                    if name in stage:
                        for mark in stage[name](eng):
                            yield t + mark
                    t += length
            return program

        def norm_vector(st, dve, src, dst, t=0.0):
            stats, mom, rstd, link = st.buf["stats"], st.buf["mom"], st.buf["rstd"], st.chain["vector"]
            st.norms["vector"] += 1
            n = st.norms["vector"]
            yield t
            for j in range(NT):
                i = dve.bn_stats(stats[:, j, :], src[:, j, :])
            link(dve, i)
            for j in range(NT):
                i = dve.bn_aggr(mom[:, j, :], stats[:, j, :])
            i.then_inc(st.moments, 1)
            yield t + 2.0
            dve.wait_ge(st.rstd, n)
            for j in range(NT):
                i = dve.tensor_scalar(dst[:, j, :], src[:, j, :], mom[:, j, 0:1], rstd[:, j:j + 1],
                                      ALU.subtract, ALU.mult)
            return i

        def norm_gpsimd(st, gp, t=0.0):
            st.norms["gpsimd"] += 1
            yield t + 1.0
            gp.wait_ge(st.moments, st.norms["gpsimd"])
            st.chain["gpsimd"](gp, gp.tensor_scalar(st.buf["veps"][:, :], st.buf["mom"][:, :, 1], EPS, None, ALU.add))
            gp.tensor_tensor(st.buf["rstd"][:, :], st.buf["veps"][:, :], mhalf[:, :], ALU.pow).then_inc(st.rstd, 1)

        def turn(pe, src, bank):
            for j in range(NT):
                i = pe.transpose(bank[:, j * P:(j + 1) * P], src[:, j, :], ident)
            return i

        def tiles(bank):
            return bank.rearrange("p (t c) -> p t c", t=NT)

        def attention(st, tag, src, wq, wk, wv, wo, bq, bk, bv, bo, scale, causal, corners, swapped,
                      affine, double):
            buf, link = st.buf, st.chain["vector"]
            bank = banks[:, st.index]
            res, base, hT, h = buf["x"], buf["base"], buf["hT"], buf["h"]
            MAXB, VALB = bank[:, 0, :], bank[:, 3, :]
            room = Room(st)
            Qs, Ks = room([KT + 1, H, T], BF16), room([KT + 1, H, T], BF16)
            vaug = room([P, NT, H, 32])
            oT, onorm = room([P, T]), room([P, NT, C])
            mx, rden = room([P, NG, 16]), room([P, NG, NT, GH])
            negm = room([16, NG, P], BF16)
            mark = room.at
            prob = room([P, 2, GH, T])
            room.at = mark
            q32, r32, ro = room([P, 2, T]), room([P, 2, T]), room([P, 2, T])
            parts = room([P, 3, 2, T], BF16)
            first_query = [P * kt if causal else 0 for kt in range(NT)]
            keys = [P * (j + 1) if causal else T for j in range(NT)]

            S = st.signals(tag)

            U, M0 = 0.62, 26.0
            if double:
                M0 += 4.0
            LAG = 22

            def max_at(n):
                return M0 + n * U

            def score_at(n):
                return M0 + (n + LAG) * U

            def vector(dve):
                if double:
                    i = yield from norm_vector(st, dve, res, src)
                    link(dve, i)
                    i = yield from norm_vector(st, dve, src, h, 4.0)
                else:
                    i = yield from norm_vector(st, dve, res, src)
                i.then_inc(S("normed"), 1)
                t = 4.0 if double else 0.0
                yield t + 5.0
                dve.wait_ge(*S.once("turned"))
                if affine:
                    i = dve.tensor_scalar(hT[:, :], VALB, affine[0], affine[1], ALU.mult, ALU.add)
                else:
                    i = dve.tensor_copy(hT[:, :], VALB)
                i.then_inc(S("hT_ready"), 1)
                yield t + 8.0
                if swapped:
                    dve.wait_ge(S("qk_projected"), 1)
                    for i, (b, s) in enumerate(((bq, swapped[2]), (bk, swapped[3]))):
                        dve.scalar_tensor_tensor(q32[:, i, :], bank[:, i, :], b, swapped[4], ALU.add, ALU.mult)
                        k = dve.scalar_tensor_tensor(ro[:, i, :], bank[:, 2 + i, :], s, swapped[5],
                                                     ALU.add, ALU.mult)
                    link(dve, k)
                    link(dve, dve.tensor_tensor(q32, q32, ro, ALU.add))
                    dve.tensor_copy(parts[:, 0], q32).then_inc(S("qk_taken"), 1)
                    dve.wait_ge(S("qk_taken"), 1)
                else:
                    dve.wait_ge(S("qk_taken"), 2)
                    link(dve, dve.tensor_copy(parts[:, 0], q32))
                link(dve, dve.tensor_tensor(r32, q32, parts[:, 0], ALU.subtract))
                link(dve, dve.tensor_copy(parts[:, 1], r32))
                dve.tensor_tensor(parts[:, 2], r32, parts[:, 1], ALU.subtract).then_inc(S("parts_ready"), 1)
                yield t + 12.0
                dve.wait_ge(S("v_projected"), 1)
                dve.wait_ge(S("vaug_set"), 2)
                for j in range(NT):
                    i = dve.tensor_tensor(vaug[:, j, :, 0:HD],
                                          bank[:, 2, j * P:(j + 1) * P].rearrange("p (h d) -> p h d", h=H),
                                          bv.rearrange("p (h d) -> p h d", h=H), ALU.add)
                i.then_inc(S("v_ready"), 1)
                for n in range(70 + LAG):
                    if n < 64:
                        yield max_at(n) + 0.2
                        dve.wait_ge(S("max_scored"), n + 1)
                        dve.tensor_reduce(mx[:, n // 16, n % 16:n % 16 + 1], MAXB[:, 0:keys[n % NT]], AX.X,
                                          ALU.max).then_inc(S("max_reduced"), 1)
                        if n % 16 == 15:
                            k = n // 16
                            yield max_at(n) + 0.4
                            dve.wait_ge(S("max_turned"), k + 1)
                            dve.tensor_scalar(negm[:, k, :], MAXB[0:16, 0:P], -1.0, None,
                                              ALU.mult).then_inc(S("negmax_ready"), 1)
                    m = n - LAG
                    if m >= 37 - 16 and (m - 21) % 16 == 0:
                        g = (m - 21) // 16
                        yield score_at(m) + 0.3
                        dve.wait_ge(S("o_turned"), g + 1)
                        o4 = VALB.rearrange("p (t h w) -> p t h w", t=NT, h=GH)
                        link(dve, dve.reciprocal(rden[:, g, :, :], o4[:, :, :, HD]))
                        dve.tensor_tensor(
                            onorm[:, :, g * 32:(g + 1) * 32].rearrange("p t (h d) -> p t h d", h=GH),
                            o4[:, :, :, 0:HD],
                            rden[:, g, :, :].unsqueeze(3).broadcast_to([P, NT, GH, HD]),
                            ALU.mult).then_inc(S("o_normed"), 1)
                end = score_at(69)
                yield end + 1.5
                dve.wait_ge(S("o_back"), 1)
                dve.tensor_copy(hT[:, :], MAXB).then_inc(S("oT_ready"), 1)
                yield end + 3.0
                dve.wait_ge(S("out_projected"), 1)
                dve.wait_ge(S("base_ready"), 1)
                dve.tensor_tensor(res[:, :, :], base[:, :, :], tiles(bank[:, 1, :]), ALU.add).then_inc(S("done"), 1)

            def gpsimd(gp):
                chain = st.chain["gpsimd"]
                yield 0.0
                chain(gp, gp.memset(vaug, 0.0))
                i = gp.memset(vaug[:, :, :, HD:HD + 1], 1.0)
                i.then_inc(S("vaug_set"), 2)
                yield from norm_gpsimd(st, gp)
                if double:
                    yield from norm_gpsimd(st, gp, 4.0)
                yield 9.0
                gp.wait_ge(*S.once("normed"))
                frm = res
                if double:
                    chain(gp, gp.tensor_tensor(base[:, :, :], res[:, :, :], src[:, :, :], ALU.add))
                    frm = base
                if bo is not None:
                    for j in range(NT):
                        i = gp.tensor_tensor(base[:, j, :], frm[:, j, :], bo, ALU.add)
                else:
                    i = gp.tensor_copy(base[:, :, :], frm[:, :, :])
                i.then_inc(S("base_ready"), 1)

            def scalar(act):
                yield 7.0 + (4.0 if double else 0.0)
                if not swapped:
                    act.wait_ge(S("qk_projected"), 1)
                    act.activation(q32[:, 0, :], bank[:, 0, :], ACT.Identity, bias=bq).then_inc(S("qk_taken"), 1)
                    act.activation(q32[:, 1, :], bank[:, 1, :], ACT.Identity, bias=bk).then_inc(S("qk_taken"), 1)
                for n in range(64 + 5):
                    if n < 64:
                        yield score_at(n) + 0.2
                        kt, q0 = n // 4 % NT, first_query[n // 4 % NT]
                        if n >= 8 and n % 4 == 0:
                            act.wait_ge(S("av_done"), n // 4 - 1)
                        act.wait_ge(S("scored"), n + 1)
                        act.activation(prob[:, n // 4 % 2, n % 4, q0:T], bank[:, 1 + n % 2, q0:T],
                                       ACT.Exp, scale=scale).then_inc(S("exped"), 1)
                    if n >= 20 and (n - 20) % 16 == 0:
                        g = (n - 20) // 16
                        yield score_at(n) + 0.3
                        act.wait_ge(S("av_done"), 4 * (g + 1))
                        if g >= 1:
                            act.wait_ge(S("o_turned"), g)
                        act.activation(oT, VALB, ACT.Copy).then_inc(S("av_taken"), 1)

            def sync(sp):
                t = 4.0 if double else 0.0
                yield t + 9.0
                sp.dma_start(Ks[KT:KT + 1, :, :], kb("ones", H)).then_inc(S("grouped"), 16)
                yield t + 12.5
                sp.wait_ge(S("parts_ready"), 1)
                scratch = parts_dram[st.index]
                for i in range(3):
                    sp.dma_start(scratch[i].rearrange("q p t -> p q t"), parts[:, i]).then_inc(S("parts_stored"), 16)
                yield t + 15.0
                sp.wait_ge(S("parts_stored"), 48)
                for k, (tq, tk) in enumerate(TERMS):
                    sp.dma_start(Qs[k * HD:(k + 1) * HD, :, :],
                                 scratch[tq, 0].rearrange("(h d) t -> d h t", d=HD)).then_inc(S("grouped"), 16)
                    sp.dma_start(Ks[k * HD:(k + 1) * HD, :, :],
                                 scratch[tk, 1].rearrange("(h d) t -> d h t", d=HD)).then_inc(S("grouped"), 16)
                for g in range(NG):
                    yield max_at(16 * g + 15) + 0.5
                    sp.wait_ge(S("negmax_ready"), g + 1)
                    sp.dma_start(Qs[KT:KT + 1, g * GH:(g + 1) * GH, :], negm[:, g, :]).then_inc(S("negmax_placed"), 16)

            def tensor(pe):
                t = 4.0 if double else 0.0
                yield t + 4.0
                pe.wait_ge(*S.once("normed"))
                turn(pe, h if double else src, VALB).then_inc(S("turned"), 1)
                yield t + 6.0
                pe.wait_ge(*S.once("hT_ready"))
                pe.matmul(bank[:, 0, :], wq, hT[:, :], start=True, stop=True)
                i = pe.matmul(bank[:, 1, :], wk, hT[:, :], start=True, stop=True)
                if swapped:
                    pe.matmul(bank[:, 2, :], swapped[0], hT[:, :], start=True, stop=True)
                    i = pe.matmul(bank[:, 3, :], swapped[1], hT[:, :], start=True, stop=True)
                i.then_inc(S("qk_projected"), 1)
                yield t + 9.0
                if swapped:
                    pe.wait_ge(S("qk_taken"), 1)
                for j in range(NT):
                    i = pe.matmul(bank[:, 2, j * P:(j + 1) * P], hT[:, j * P:(j + 1) * P], wv,
                                  start=True, stop=True)
                i.then_inc(S("v_projected"), 1)

                def max_unit(n):
                    h, j = n // NT, n % NT
                    if n == 0:
                        pe.wait_ge(S("grouped"), 16 * (1 + 2 * len(TERMS)))
                        pe.wait_ge(S("qk_taken"), 1 if swapped else 2)
                    if n % 16 == 0 and n:
                        pe.wait_ge(S("negmax_ready"), n // 16)
                    elif n:
                        pe.wait_ge(S("max_reduced"), n)
                    masks = []
                    if causal:
                        masks = [(j * P, kb("causal"))]
                    if corners and j == 0:
                        masks = [(T - P, kb("cornB"))]
                    if corners and j == NT - 1:
                        masks = [(0, kb("cornA"))]
                    m = pe.matmul(MAXB[:, 0:keys[j]], Qs[0:KT, h, j * P:(j + 1) * P], Ks[0:KT, h, 0:keys[j]],
                                  start=True, stop=not masks)
                    for c, mask in masks:
                        m = pe.matmul(MAXB[:, c:c + P], identb, mask, start=False, stop=True)
                    m.then_inc(S("max_scored"), 1)

                def score_unit(n):
                    g, kt, hl = n // 16, n // 4 % NT, n % 4
                    head, q0 = g * GH + hl, first_query[kt]
                    if n % 16 == 0:
                        pe.wait_ge(S("negmax_placed"), 16 * (g + 1))
                    if n == 0:
                        pe.wait_ge(S("v_ready"), 1)
                    if n >= 2:
                        pe.wait_ge(S("exped"), n - 1)
                    b = bank[:, 1 + n % 2, :]
                    masks = []
                    if causal:
                        masks = [(q0, kb("causalT"))]
                    if corners and kt == NT - 1:
                        masks = [(0, kb("cornA"))]
                    if corners and kt == 0:
                        masks = [(T - P, kb("cornB"))]
                    i = pe.matmul(b[:, q0:T], Ks[0:KT + 1, head, kt * P:(kt + 1) * P], Qs[0:KT + 1, head, q0:T],
                                  start=True, stop=not masks)
                    for c, mask in masks:
                        i = pe.matmul(b[:, c:c + P], identb, mask, start=False, stop=True)
                    i.then_inc(S("scored"), 1)

                def value_pack(a):
                    g, kt = divmod(a, NT)
                    pe.wait_ge(S("exped"), 4 * (a + 1))
                    if kt == 0 and g >= 1:
                        pe.wait_ge(S("o_normed"), g)
                    q0 = first_query[kt]
                    for hl in range(GH):
                        m = pe.matmul(VALB[32 * hl:32 * hl + 32, q0:T], vaug[:, kt, g * GH + hl, :],
                                      prob[:, a % 2, hl, q0:T], start=kt == 0, stop=kt == NT - 1,
                                      skip_group_check=True)
                    m.then_inc(S("av_done"), 1)

                for n in range(70 + LAG):
                    if n < 64:
                        yield max_at(n)
                        max_unit(n)
                        if n % 16 == 15:
                            yield max_at(n) + 0.3
                            pe.wait_ge(S("max_reduced"), n + 1)
                            pe.transpose(MAXB[0:16, 0:P], mx[:, n // 16, :], ident).then_inc(S("max_turned"), 1)
                    m = n - LAG
                    if 0 <= m < 64:
                        yield score_at(m)
                        score_unit(m)
                    if m % 4 == 3 and 7 <= m < 64 + 4:
                        yield score_at(m) + 0.01
                        value_pack(m // 4 - 1)
                    if m >= 21 and (m - 21) % 16 == 0:
                        g = (m - 21) // 16
                        yield score_at(m) + 0.1
                        pe.wait_ge(S("av_taken"), g + 1)
                        for j in range(NT):
                            i = pe.transpose(VALB[:, j * P:(j + 1) * P], oT[:, j * P:(j + 1) * P], ident)
                        i.then_inc(S("o_turned"), 1)
                end = score_at(69)
                yield end + 1.0
                pe.wait_ge(S("o_normed"), NG)
                turn(pe, onorm, MAXB).then_inc(S("o_back"), 1)
                yield end + 2.0
                pe.wait_ge(S("oT_ready"), 1)
                for j in range(NT):
                    i = pe.matmul(bank[:, 1, j * P:(j + 1) * P], hT[:, j * P:(j + 1) * P], wo,
                                  start=True, stop=True)
                i.then_inc(S("out_projected"), 1)

            program = {"vector": vector, "gpsimd": gpsimd, "scalar": scalar, "sync": sync, "tensor": tensor}
            return program, score_at(69) + 4.5, S.once("done")

        def tri(n):
            full = kc("tri16").rearrange("p (a b) -> p a b", a=16)
            return full[:, 0:n, 0:n]

        def rank(st, dve, big, vals, n, ranks, t=NT):
            link = st.chain["vector"]
            shape = [P, t, n, n]
            other, own = vals.unsqueeze(2).broadcast_to(shape), vals.unsqueeze(3).broadcast_to(shape)
            gt, eq = (big[:, i, 0:t * n * n].rearrange("p (t a b) -> p t a b", t=t, a=n) for i in range(2))
            dve.tensor_tensor(gt, other, own, ALU.is_gt)
            link(dve, dve.tensor_tensor(eq, other, own, ALU.is_equal))
            link(dve, dve.tensor_tensor(eq, eq, tri(n).unsqueeze(1).broadcast_to(shape), ALU.mult))
            link(dve, dve.tensor_tensor(gt, gt, eq, ALU.add))
            link(dve, dve.tensor_reduce(ranks, gt, AX.X, ALU.add))

        def load_constants(block):
            wide = memory[0]["room"][:, 0:width(PACK_KB)]

            @block.sync
            def _(sp):
                sp.dma_start(kc.tensor[:, :], pk).then_inc(load_sem, 16)
                sp.dma_start(wide, pkb).then_inc(load_sem, 16)
                sp.wait_ge(load_sem, 32)

            @block.vector
            def _(dve):
                dve.wait_ge(load_sem, 32)
                dve.tensor_copy(kb.tensor[:, :], wide)

            @block.gpsimd
            def _(gp):
                gp.memset(mhalf[:, :], -0.5)
        loads[0] = 32
        stage_block(load_constants)

        def load_weights(pairs):
            def body(block):
                @block.sync
                def _(sp):
                    for tensor, src in pairs:
                        n = tensor.shape[1]
                        for a in range(0, n, 2048):
                            sp.dma_start(tensor[:, a:min(n, a + 2048)], src[:, a:min(n, a + 2048)]).then_inc(load_sem, 16)
                            loads[0] += 16
                    sp.wait_ge(load_sem, loads[0])
            stage_block(body)

        def load_x(st, views):
            def sync(sp):
                yield 0.0
                for own, v in views:
                    sp.dma_start(own, v).then_inc(st.sem("x_loaded"), 16)
            return {"sync": sync}, 3.0, (st.sem("x_loaded"), 16 * len(views))

        def store_x(st, views):
            def sync(sp):
                yield 0.0
                for own, v in views:
                    sp.dma_start(v, own).then_inc(st.sem("x_stored"), 16)
                sp.wait_ge(st.sem("x_stored"), 16 * len(views))
            return {"sync": sync}, 3.0, None

        def streams_of(plan, offset):
            taken, programs = [0], []
            for s in range(2):
                st = Stream(s, pool, taken, memory[s])
                stages, entry = [], None
                for program, length, result in plan(st):
                    stages.append((program, length, entry))
                    entry = result
                programs.append(chain_of(stages, s * offset))
            run(None, programs)

        def moe0(st, wa):
            buf, link = st.buf, st.chain["vector"]
            bank = banks[:, st.index]
            x_sb, y_sb, hT = buf["x"], buf["y"], buf["hT"]
            room = Room(st)
            hid, relu, big = room([P, 9, T]), room([P, 2, T]), room([P, 2, 1024])
            sc, gsc, cwT = room([P, 12, NT, E0]), room([P, 8, NT, 4, 2]), room([E0, T])
            elog, choice, masked, ranks, sel, wsel = (sc[:, i] for i in range(6))

            S = st.signals("moe0_")

            def vector(dve):
                i = yield from norm_vector(st, dve, x_sb, y_sb)
                i.then_inc(S("normed"), 1)
                yield 5.0
                dve.wait_ge(*S.once("turned"))
                dve.tensor_copy(hT[:, :], bank[:, 0, :]).then_inc(S("hT_ready"), 1)
                yield 8.0
                dve.wait_ge(S("exp_logits"), 1)
                link(dve, dve.tensor_scalar(sc[:, 6], elog, 1.0, None, ALU.add))
                link(dve, dve.reciprocal(sc[:, 7], sc[:, 6]))
                sig = sc[:, 7]
                link(dve, dve.tensor_tensor(choice, sig, wa("bc0").unsqueeze(1).broadcast_to([P, NT, E0]), ALU.add))
                yield 9.0
                c4 = choice.rearrange("p t (g q r) -> p (t g) q r", q=2, r=2)
                hi, lo = (gsc[:, i].rearrange("p t g q -> p (t g) q") for i in range(2))
                dve.tensor_tensor(hi, c4[:, :, :, 0], c4[:, :, :, 1], ALU.max)
                link(dve, dve.tensor_tensor(lo, c4[:, :, :, 0], c4[:, :, :, 1], ALU.min))
                t1, t2, t3 = (gsc[:, i, :, :, 0].rearrange("p t g -> p (t g)") for i in (2, 3, 4))
                dve.tensor_tensor(t1, hi[:, :, 0], hi[:, :, 1], ALU.max)
                dve.tensor_tensor(t2, hi[:, :, 0], hi[:, :, 1], ALU.min)
                link(dve, dve.tensor_tensor(t3, lo[:, :, 0], lo[:, :, 1], ALU.max))
                link(dve, dve.tensor_tensor(t2, t2, t3, ALU.max))
                gs, gr = sc[:, 8, :, 0:4], sc[:, 9, :, 0:4]
                link(dve, dve.tensor_tensor(gs, gsc[:, 2, :, :, 0], gsc[:, 3, :, :, 0], ALU.add))
                yield 11.0
                rank(st, dve, big, gs, 4, gr)
                yield 13.0
                link(dve, dve.tensor_scalar(gr, gr, 1.5, None, ALU.is_lt))
                link(dve, dve.tensor_tensor(masked.rearrange("p t (g r) -> p t g r", g=4),
                                            choice.rearrange("p t (g r) -> p t g r", g=4),
                                            gr.unsqueeze(3).broadcast_to([P, NT, 4, 4]), ALU.mult))
                rank(st, dve, big, masked, E0, ranks)
                yield 19.0
                link(dve, dve.tensor_scalar(sel, ranks, 3.5, None, ALU.is_lt))
                link(dve, dve.tensor_tensor(wsel, sel, sig, ALU.mult))
                tot = sc[:, 10, :, 0:1]
                link(dve, dve.tensor_reduce(tot, wsel, AX.X, ALU.add))
                link(dve, dve.tensor_scalar(tot, tot, 1e-20, None, ALU.add))
                link(dve, dve.reciprocal(sc[:, 11, :, 0:1], tot))
                link(dve, dve.tensor_scalar(wsel, wsel, 2.5, None, ALU.mult))
                dve.tensor_tensor(sc[:, 6], wsel, sc[:, 11, :, 0:1].broadcast_to([P, NT, E0]),
                                  ALU.mult).then_inc(S("weights_ready"), 1)
                yield 22.5
                dve.wait_ge(S("weights_turned"), 1)
                dve.tensor_copy(cwT, bank[0:E0, 0, :]).then_inc(S("cwT_ready"), 1)
                for c in range(8):
                    yield 24.5 + c * 0.9
                    dve.wait_ge(S("squared"), c + 1)
                    dve.wait_ge(S("spread"), c + 1)
                    dve.tensor_tensor(hid[:, c, :], hid[:, c, :], bank[:, 1 + c % 2, :],
                                      ALU.mult).then_inc(S("weighted"), 1)
                yield 42.0
                dve.wait_ge(S("moe_out"), 1)
                dve.tensor_tensor(x_sb[:, :, :], x_sb[:, :, :], tiles(bank[:, 3, :]), ALU.add).then_inc(S("done"), 1)

            def gpsimd(gp):
                yield from norm_gpsimd(st, gp)
                for c in range(9):
                    yield 8.2 + c * 1.1
                    gp.wait_ge(S("relued"), c + 1)
                    gp.tensor_tensor(hid[:, c, :], relu[:, c % 2, :], relu[:, c % 2, :], ALU.mult).then_inc(S("squared"), 1)

            def scalar(act):
                yield 7.0
                act.wait_ge(S("logits"), 1)
                act.activation(elog, bank[:, 3, 0:NT * E0].rearrange("p (t e) -> p t e", t=NT), ACT.Exp,
                               scale=-1.0).then_inc(S("exp_logits"), 1)
                for c in range(9):
                    yield 8.0 + c * 1.1
                    act.wait_ge(S("hidden"), c + 1)
                    if c >= 2:
                        act.wait_ge(S("squared"), c - 1)
                    act.activation(relu[:, c % 2, :], bank[:, 1 + c % 2, :], ACT.Relu).then_inc(S("relued"), 1)

            def tensor(pe):
                yield 4.0
                pe.wait_ge(*S.once("normed"))
                turn(pe, y_sb, bank[:, 0, :]).then_inc(S("turned"), 1)
                yield 6.0
                pe.wait_ge(*S.once("hT_ready"))
                for j in range(NT):
                    i = pe.matmul(bank[:, 3, j * E0:(j + 1) * E0], hT[:, j * P:(j + 1) * P], wa("wg0"),
                                  start=True, stop=True)
                i.then_inc(S("logits"), 1)
                for c in range(9):
                    yield 7.0 + c * 1.1
                    if c >= 2:
                        pe.wait_ge(S("relued"), c - 1)
                    w = wa("w1_0")[:, c * P:(c + 1) * P] if c < 8 else wa("ws1_0")
                    pe.matmul(bank[:, 1 + c % 2, :], w, hT[:, :], start=True, stop=True).then_inc(S("hidden"), 1)
                yield 22.0
                pe.wait_ge(S("weights_ready"), 1)
                for j in range(NT):
                    i = pe.transpose(bank[0:E0, 0, j * P:(j + 1) * P], sc[:, 6, j, :], ident)
                i.then_inc(S("weights_turned"), 1)
                yield 23.0
                pe.wait_ge(S("cwT_ready"), 1)
                pe.wait_ge(S("relued"), 9)
                for c in range(8):
                    yield 24.0 + c * 0.9
                    if c >= 2:
                        pe.wait_ge(S("weighted"), c - 1)
                    pe.matmul(bank[:, 1 + c % 2, :], kc("sel16", E0)[:, c * P:(c + 1) * P], cwT,
                              start=True, stop=True).then_inc(S("spread"), 1)
                for j in range(NT):
                    for c in range(9):
                        yield 32.5 + (j * 9 + c) * 0.23
                        if j == 0 and c == 0:
                            pe.wait_ge(S("weighted"), 8)
                            pe.wait_ge(S("squared"), 9)
                        w = wa("w2_0")[:, c * P:(c + 1) * P] if c < 8 else wa("ws2_0")
                        i = pe.matmul(bank[:, 3, j * P:(j + 1) * P], hid[:, c, j * P:(j + 1) * P], w,
                                      start=c == 0, stop=c == 8)
                i.then_inc(S("moe_out"), 1)

            return {"vector": vector, "gpsimd": gpsimd, "scalar": scalar, "tensor": tensor}, 43.0, S.once("done")

        with ExitStack() as ctx:
            w_a = sb(ctx, "w_a", [P, width(PACK_A)])
            wa = Pieces(w_a, PACK_A)
            load_weights([(w_a, pa)])
            x_b = x.rearrange("(b t p) c -> p b t c", b=B, p=P)
            x1_b = x1.rearrange("(b t p) c -> p b t c", b=B, p=P)
            with nc.Fori(0, B // 2) as pair:
                def plan_a(st):
                    own, b = st.buf["x"][:, :, :], bass.ds(pair * 2 + st.index, 1)
                    c0, c1 = wa("cols0"), wa("cols1")
                    yield load_x(st, [(own, x_b[:, b, :, :])])
                    yield attention(st, "a0_", st.buf["y"], wa("wq0"), wa("wk0"), wa("wv0"), wa("wo0"),
                                    c0[:, 2:3], c0[:, 3:4], wa("bv0"), wa("bo0"), float(HD) ** -0.5, False, False,
                                    None, (c0[:, 0:1], c0[:, 1:2]), True)
                    yield moe0(st, wa)
                    yield attention(st, "a1_", st.buf["y"], wa("wq1"), wa("wk1"), wa("wv1"), wa("wp1"),
                                    c1[:, 0:1], c1[:, 1:2], wa("bv1"), wa("bp1"), float(HD) ** -0.5, True, False,
                                    (wa("wqs1"), wa("wks1"), c1[:, 2:3], c1[:, 3:4], wa("cos1"), wa("sin1")),
                                    None, False)
                    yield store_x(st, [(own, x1_b[:, b, :, :])])

                streams_of(plan_a, OFFSET_A)

        def experts(st, S, t0, func, w_up, w_down, bias, weight, acc, hbuf, logits_read):
            bank, hT = banks[:, st.index], st.buf["hT"]
            E = 7.4

            def up_at(n):
                return t0 + n // NF * E + n % NF * 0.9

            def down_at(e):
                return t0 + (e + 1) * E + 3.7

            def tensor(pe):
                def up(n):
                    if n >= 2:
                        pe.wait_ge(S("acted"), n - 1)
                    pe.matmul(bank[:, n % 2, :], w_up[:, n * P:(n + 1) * P], hT[:, :],
                              start=True, stop=True).then_inc(S("up"), 1)

                def down(e, j):
                    if j == 0:
                        pe.wait_ge(S("acted"), NF * (e + 1))
                        if e == 0:
                            pe.wait_ge(S(logits_read), 1)
                        if e >= 2:
                            pe.wait_ge(S("mixed"), e - 1)
                    for f in range(NF):
                        n = e * NF + f
                        i = pe.matmul(bank[:, 2 + e % 2, j * P:(j + 1) * P], hbuf[:, n % 8, j * P:(j + 1) * P],
                                      w_down[:, n * P:(n + 1) * P], start=f == 0, stop=f == NF - 1)
                    if j == NT - 1:
                        i.then_inc(S("down"), 1)

                for e in range(E8 + 1):
                    if e < E8:
                        for f in range(NF):
                            yield up_at(e * NF + f)
                            up(e * NF + f)
                    if e >= 1:
                        for j in range(NT):
                            yield down_at(e - 1) + 0.9 * j
                            down(e - 1, j)

            def scalar(act):
                for n in range(E8 * NF):
                    yield up_at(n) + 0.5
                    act.wait_ge(S("up"), n + 1)
                    if n % NF == 0 and n >= 2 * NF:
                        act.wait_ge(S("down"), n // NF - 1)
                    act.activation(hbuf[:, n % 8, :], bank[:, n % 2, :], func,
                                   bias=bias[:, n:n + 1] if bias is not None else 0.0).then_inc(S("acted"), 1)

            def vector(dve):
                for e in range(E8):
                    yield down_at(e) + 3.6
                    dve.wait_ge(S("down"), e + 1)
                    if e:
                        dve.wait_ge(S("mixed"), e)
                    for j in range(NT):
                        src = bank[:, 2 + e % 2, j * P:(j + 1) * P]
                        if e == 0:
                            i = dve.tensor_scalar(acc[:, j, :], src, weight[:, j, e:e + 1], None, ALU.mult)
                        else:
                            i = dve.scalar_tensor_tensor(acc[:, j, :], src, weight[:, j, e:e + 1], acc[:, j, :],
                                                         ALU.mult, ALU.add)
                    i.then_inc(S("mixed"), 1)
                dve.wait_ge(S("mixed"), E8)

            return tensor, scalar, vector, down_at(E8 - 1) + 4.6

        def rep(piece):
            return piece.unsqueeze(1).broadcast_to([P, NT, C])

        def mha(st, wb):
            buf, link = st.buf, st.chain["vector"]
            bank = banks[:, st.index]
            x_sb, y_sb, h_sb, hT, base = buf["x"], buf["y"], buf["h"], buf["hT"], buf["base"]
            room = Room(st)
            hold, acc = room([P, NT, C]), room([P, NT, C])
            qkT, v_sb = room([P, 2, T]), room([P, NT, C])
            s32, pT = room([P, SH, T]), room([P, SH, T])
            smx, ssum, srec = room([P, SH * NT]), room([P, SH * NT]), room([P, SH * NT])

            S = st.signals("mha_")

            def by_head(t):
                return t.rearrange("p h (j k) -> p (h j) k", j=NT)

            def vector(dve):
                i = yield from norm_vector(st, dve, x_sb, y_sb)
                i.then_inc(S("normed"), 1)
                yield 5.0
                dve.wait_ge(*S.once("turned"))
                dve.tensor_copy(hT[:, :], bank[:, 3, :]).then_inc(S("hT_ready"), 1)
                yield 8.0
                dve.wait_ge(S("v_projected"), 1)
                dve.tensor_tensor(v_sb, tiles(bank[:, 2, :]), rep(wb("bv")), ALU.add).then_inc(S("v_ready"), 1)
                yield 14.0
                dve.wait_ge(S("scored"), 1)
                link(dve, dve.tensor_reduce(smx, by_head(bank), AX.X, ALU.max))
                dve.tensor_tensor(by_head(s32), by_head(bank), smx.unsqueeze(2).broadcast_to([P, SH * NT, P]),
                                  ALU.subtract).then_inc(S("centred"), 1)
                yield 21.0
                dve.wait_ge(S("exped"), 1)
                link(dve, dve.tensor_reduce(ssum, by_head(s32), AX.X, ALU.add))
                link(dve, dve.reciprocal(srec, ssum))
                yield 28.0
                dve.wait_ge(S("av"), 1)
                dve.tensor_tensor(h_sb[:, :, :].rearrange("p t (h d) -> p t h d", h=SH),
                                  bank[:, 0, :].rearrange("p (t h d) -> p t h d", t=NT, h=SH),
                                  srec.rearrange("p (h j) -> p j h", h=SH).unsqueeze(3).broadcast_to([P, NT, SH, SD]),
                                  ALU.mult).then_inc(S("o_normed"), 1)
                yield 31.0
                dve.wait_ge(S("o_back"), 1)
                dve.tensor_copy(hT[:, :], bank[:, 1, :]).then_inc(S("oT_ready"), 1)
                yield 33.5
                dve.wait_ge(S("base_ready"), 1)
                dve.wait_ge(S("out_projected"), 1)
                link(dve, dve.tensor_tensor(acc, base[:, :, :], tiles(bank[:, 2, :]), ALU.add))
                i = yield from norm_vector(st, dve, acc, h_sb, 34.0)
                link(dve, i)
                link(dve, dve.tensor_tensor(h_sb[:, :, :], h_sb[:, :, :], rep(wb("g1")), ALU.mult))
                dve.tensor_tensor(hold, h_sb[:, :, :], rep(wb("be1")), ALU.add).then_inc(S("done"), 1)

            def gpsimd(gp):
                yield from norm_gpsimd(st, gp)
                yield 5.0
                gp.wait_ge(*S.once("normed"))
                for j in range(NT):
                    i = gp.tensor_tensor(base[:, j, :], y_sb[:, j, :], wb("bo"), ALU.add)
                i.then_inc(S("base_ready"), 1)
                yield from norm_gpsimd(st, gp, 34.0)

            def scalar(act):
                yield 8.0
                act.wait_ge(S("qk_projected"), 1)
                act.activation(qkT[:, 0, :], bank[:, 0, :], ACT.Identity, bias=wb("cols")[:, 0:1])
                act.activation(qkT[:, 1, :], bank[:, 1, :], ACT.Identity, bias=wb("cols")[:, 1:2]).then_inc(S("qk_taken"), 1)
                yield 19.0
                act.wait_ge(S("centred"), 1)
                act.activation(s32, s32, ACT.Exp, scale=float(SD) ** -0.5).then_inc(S("exped"), 1)
                yield 25.0
                act.wait_ge(S("p_turned"), 1)
                act.activation(pT, bank, ACT.Copy).then_inc(S("pT_ready"), 1)

            def tensor(pe):
                yield 4.0
                pe.wait_ge(*S.once("normed"))
                turn(pe, y_sb, bank[:, 3, :]).then_inc(S("turned"), 1)
                yield 6.0
                pe.wait_ge(*S.once("hT_ready"))
                pe.matmul(bank[:, 0, :], wb("wq"), hT[:, :], start=True, stop=True)
                pe.matmul(bank[:, 1, :], wb("wk"), hT[:, :], start=True, stop=True).then_inc(S("qk_projected"), 1)
                for j in range(NT):
                    i = pe.matmul(bank[:, 2, j * P:(j + 1) * P], hT[:, j * P:(j + 1) * P], wb("wv"),
                                  start=True, stop=True)
                i.then_inc(S("v_projected"), 1)
                yield 10.0
                pe.wait_ge(S("qk_taken"), 1)
                pe.wait_ge(S("v_ready"), 1)
                for h in range(SH):
                    pe.matmul(bank[:, h, :], identb, kb("block"), start=True, stop=False, skip_group_check=True)
                for j in range(NT):
                    for h in range(SH):
                        i = pe.matmul(bank[:, h, j * P:(j + 1) * P], qkT[SD * h:SD * (h + 1), 0, j * P:(j + 1) * P],
                                      qkT[SD * h:SD * (h + 1), 1, j * P:(j + 1) * P], start=False,
                                      stop=j == NT - 1, skip_group_check=True)
                i.then_inc(S("scored"), 1)
                yield 22.0
                pe.wait_ge(S("exped"), 1)
                for h in range(SH):
                    for j in range(NT):
                        i = pe.transpose(bank[:, h, j * P:(j + 1) * P], s32[:, h, j * P:(j + 1) * P], ident)
                i.then_inc(S("p_turned"), 1)
                yield 27.0
                pe.wait_ge(S("pT_ready"), 1)
                for j in range(NT):
                    for h in range(SH):
                        i = pe.matmul(bank[:, 0, j * P + h * SD:j * P + (h + 1) * SD], pT[:, h, j * P:(j + 1) * P],
                                      v_sb[:, j, h * SD:(h + 1) * SD], start=True, stop=True)
                i.then_inc(S("av"), 1)
                yield 30.0
                pe.wait_ge(S("o_normed"), 1)
                turn(pe, h_sb, bank[:, 1, :]).then_inc(S("o_back"), 1)
                yield 32.0
                pe.wait_ge(S("oT_ready"), 1)
                for j in range(NT):
                    i = pe.matmul(bank[:, 2, j * P:(j + 1) * P], hT[:, j * P:(j + 1) * P], wb("wo"),
                                  start=True, stop=True)
                i.then_inc(S("out_projected"), 1)

            return {"vector": vector, "gpsimd": gpsimd, "scalar": scalar, "tensor": tensor}, 40.0, S.once("done")

        def moe1(st, wb, b2_sb):
            buf, link = st.buf, st.chain["vector"]
            bank = banks[:, st.index]
            x_sb, h_sb, hT, base = buf["x"], buf["h"], buf["hT"], buf["base"]
            room = Room(st)
            hold, acc = room([P, NT, C]), room([P, NT, C])
            hbuf, lg, big8, mT = room([P, 8, T]), room([P, 4, NT, E8]), room([P, 2, 256]), room([E8, T])
            mask = lg[:, 2]

            S = st.signals("moe1_", absent=("normed",))

            parts = experts(st, S, 8.0, ACT.Relu, wb("w1"), wb("w2"), wb("b1"), mask, acc, hbuf, "mask_ready")
            end = parts[3]

            def vector(dve):
                yield 1.0
                dve.wait_ge(*S.once("turned"))
                dve.tensor_copy(hT[:, :], bank[:, 3, :]).then_inc(S("hT_ready"), 1)
                yield 4.0
                dve.wait_ge(S("logits"), 1)
                link(dve, dve.tensor_copy(lg[:, 0], bank[:, 2, 0:NT * E8].rearrange("p (t e) -> p t e", t=NT)))
                rank(st, dve, big8, lg[:, 0], E8, lg[:, 1])
                dve.tensor_scalar(mask, lg[:, 1], 0.5, None, ALU.is_lt).then_inc(S("mask_ready"), 1)
                dve.wait_ge(S("mask_ready"), 1)
                yield from parts[2](dve)
                yield end + 1.0
                dve.wait_ge(S("mask_turned"), 1)
                dve.tensor_copy(mT, bank[0:E8, 0, :]).then_inc(S("mT_ready"), 1)
                link(dve, dve.tensor_tensor(acc, acc, hold, ALU.add))
                yield end + 3.0
                dve.wait_ge(S("bias2"), 1)
                link(dve, dve.tensor_tensor(acc, acc, tiles(bank[:, 1, :]), ALU.add))
                i = yield from norm_vector(st, dve, acc, h_sb, end + 3.5)
                link(dve, i)
                link(dve, dve.tensor_tensor(h_sb[:, :, :], h_sb[:, :, :], rep(wb("g2")), ALU.mult))
                dve.wait_ge(S("base_ready"), 1)
                dve.tensor_tensor(x_sb[:, :, :], h_sb[:, :, :], base[:, :, :], ALU.add).then_inc(S("done"), 1)

            def gpsimd(gp):
                yield 1.0
                for j in range(NT):
                    i = gp.tensor_tensor(base[:, j, :], x_sb[:, j, :], wb("be2"), ALU.add)
                i.then_inc(S("base_ready"), 1)
                yield from norm_gpsimd(st, gp, end + 3.5)

            def tensor(pe):
                yield 0.0
                turn(pe, hold, bank[:, 3, :]).then_inc(S("turned"), 1)
                yield 3.0
                pe.wait_ge(*S.once("hT_ready"))
                for j in range(NT):
                    i = pe.matmul(bank[:, 2, j * E8:(j + 1) * E8], hT[:, j * P:(j + 1) * P], wb("wg"),
                                  start=True, stop=True)
                i.then_inc(S("logits"), 1)
                yield from parts[0](pe)
                yield end
                pe.wait_ge(S("mask_ready"), 1)
                for j in range(NT):
                    i = pe.transpose(bank[0:E8, 0, j * P:(j + 1) * P], lg[:, 2, j, :], ident)
                i.then_inc(S("mask_turned"), 1)
                yield end + 2.0
                pe.wait_ge(S("mT_ready"), 1)
                for j in range(NT):
                    i = pe.matmul(bank[:, 1, j * P:(j + 1) * P], mT[:, j * P:(j + 1) * P], b2_sb[:, :],
                                  start=True, stop=True)
                i.then_inc(S("bias2"), 1)

            return {"vector": vector, "gpsimd": gpsimd, "scalar": parts[1], "tensor": tensor}, end + 9.0, S.once("done")

        with ExitStack() as ctx:
            w_b = sb(ctx, "w_b", [P, width(PACK_B)])
            wb = Pieces(w_b, PACK_B)
            b2_sb = sb(ctx, "b2_sb", [E8, C])
            load_weights([(w_b, pb), (b2_sb, b2)])

            def slices(st, t, i):
                v = t.rearrange("(s i j l) c -> s l i j c", s=SB, i=T // 64, j=NT)
                return [(st.buf["x"][s * 16:(s + 1) * 16, :, :], v[s, :, bass.ds(i, 1), :, :]) for s in range(SB)]

            with nc.Fori(0, T // 128) as pair:
                def plan_b(st):
                    yield load_x(st, slices(st, x1, pair * 2 + st.index))
                    yield mha(st, wb)
                    yield moe1(st, wb, b2_sb)
                    yield store_x(st, slices(st, x2, pair * 2 + st.index))

                streams_of(plan_b, OFFSET_B)

        def mamba(st, wc, acoef, sel_sum):
            buf, link = st.buf, st.chain["vector"]
            bank = banks[:, st.index]
            x_sb, y_sb, hT = buf["x"], buf["y"], buf["hT"]
            room = Room(st)
            xs, zs, Bb, Cb = room([P, 2, T]), room([P, 2, T]), room([P, T]), room([P, T])
            xpad = room([P, NCH, DC - 1 + T])
            mark = room.at
            conv, e2, u2 = room([P, 2, T]), room([P, 2, T]), room([P, 2, T])
            dtx, r2, parts2 = room([P, 2, 2, T]), room([P, 2, 2, T]), room([P, 3, 2, 2, T], BF16)
            room.at = mark
            G = room([96, 2, 8, T], BF16)
            ab, ub, hb, hc = room([P, 2, T]), room([P, 2, T]), room([P, 3, T]), room([P, 3, T])
            room.at = mark
            yf = room([P, 2, T])

            S = st.signals("mamba_")

            G0, GU = 62.0, 1.3

            def vector(dve):
                i = yield from norm_vector(st, dve, x_sb, y_sb)
                i.then_inc(S("normed"), 1)
                yield 5.0
                dve.memset(xpad[:, :, 0:DC - 1], 0.0)
                dve.wait_ge(*S.once("turned"))
                dve.tensor_copy(hT[:, :], bank[:, 3, :]).then_inc(S("hT_ready"), 1)
                yield 12.0
                dve.wait_ge(S("x_taken"), 1)
                for c in range(NCH):
                    i = dve.tensor_scalar(conv[:, c, :], xpad[:, c, 0:T], wc("convw")[:, c * DC:c * DC + 1],
                                          wc("convb")[:, c:c + 1], ALU.mult, ALU.add)
                link(dve, i)
                for k in range(1, DC):
                    yield 12.0 + 1.2 * k
                    for c in range(NCH):
                        i = dve.scalar_tensor_tensor(conv[:, c, :], xpad[:, c, k:k + T],
                                                     wc("convw")[:, c * DC + k:c * DC + k + 1], conv[:, c, :],
                                                     ALU.mult, ALU.add)
                    if k < DC - 1:
                        link(dve, i)
                i.then_inc(S("convolved"), 1)
                yield 17.0
                dve.wait_ge(S("z_exp"), 1)
                link(dve, dve.tensor_scalar(zs, zs, 1.0, None, ALU.add))
                link(dve, dve.reciprocal(zs, zs))
                dve.tensor_tensor(zs, bank[:, 2:4, :], zs, ALU.mult).then_inc(S("z_done"), 1)
                yield 21.0
                dve.wait_ge(S("x_exp"), 1)
                link(dve, dve.tensor_scalar(e2, e2, 1.0, None, ALU.add))
                link(dve, dve.reciprocal(e2, e2))
                dve.tensor_tensor(xs, conv, e2, ALU.mult).then_inc(S("xs_ready"), 1)
                yield 30.0
                dve.wait_ge(S("x_dbl"), 1)
                for c in range(NCH):
                    i = dve.tensor_scalar(u2[:, c, :], bank[:, 0, :], wc("wdt")[:, c:c + 1], wc("bdt")[:, c:c + 1],
                                          ALU.mult, ALU.add)
                i.then_inc(S("dt_in"), 1)
                e, s, z, q = r2[:, 1], r2[:, 0], e2, conv
                yield 34.0
                dve.wait_ge(S("e_ready"), 1)
                link(dve, dve.tensor_scalar(z, e, 2.0, None, ALU.add))
                link(dve, dve.reciprocal(q, z))
                link(dve, dve.tensor_tensor(s, e, q, ALU.mult))
                link(dve, dve.tensor_tensor(z, s, s, ALU.mult))
                link(dve, dve.tensor_scalar(q, z, LOG1P[-1], None, ALU.mult))
                for k, coefficient in enumerate(LOG1P[-2:0:-1]):
                    yield 38.0 + 1.2 * k
                    link(dve, dve.scalar_tensor_tensor(q, q, coefficient, z, ALU.add, ALU.mult))
                link(dve, dve.scalar_tensor_tensor(q, q, LOG1P[0], s, ALU.add, ALU.mult))
                yield 44.0
                link(dve, dve.scalar_tensor_tensor(dtx[:, 0, :, :], u2, 0.0, q, ALU.max, ALU.add))
                link(dve, dve.tensor_tensor(dtx[:, 1, :, :], dtx[:, 0, :, :], xs, ALU.mult))
                yield 46.0
                link(dve, dve.tensor_copy(parts2[:, 0], dtx))
                link(dve, dve.tensor_tensor(r2, dtx, parts2[:, 0], ALU.subtract))
                yield 49.0
                link(dve, dve.tensor_copy(parts2[:, 1], r2))
                dve.tensor_tensor(parts2[:, 2], r2, parts2[:, 1], ALU.subtract).then_inc(S("parts_ready"), 1)
                dve.wait_ge(S("bc_taken"), 1)
                for g in range(NGR):
                    yield G0 + g * GU + 0.3
                    if g >= 2:
                        dve.wait_ge(S("scanned"), g - 1)
                    dve.wait_ge(S("dtx_spread"), g + 1)
                    dve.tensor_tensor(ub[:, g % 2, :], bank[:, 1, :], Bb, ALU.mult).then_inc(S("u_ready"), 1)
                    yield G0 + g * GU + 0.9
                    dve.wait_ge(S("decay"), g + 1)
                    dve.wait_ge(S("u_ready"), g + 1)
                    if g >= 3:
                        dve.wait_ge(S("hc_ready"), g - 2)
                    dve.tensor_tensor_scan(hb[:, g % 3, :], ab[:, g % 2, :], ub[:, g % 2, :], 0.0,
                                           ALU.mult, ALU.add).then_inc(S("scanned"), 1)
                end = G0 + NGR * GU + 4.0
                yield end
                dve.wait_ge(S("summed"), NGR)
                for c in range(NCH):
                    i = dve.scalar_tensor_tensor(yf[:, c, :], xs[:, c, :], wc("dcol")[:, c:c + 1], bank[:, 2 + c, :],
                                                 ALU.mult, ALU.add)
                link(dve, i)
                dve.tensor_tensor(yf, yf, zs, ALU.mult).then_inc(S("gated"), 1)
                yield end + 5.0
                dve.wait_ge(S("out_projected"), 1)
                dve.tensor_tensor(x_sb[:, :, :], x_sb[:, :, :], tiles(bank[:, 0, :]), ALU.add).then_inc(S("done"), 1)

            def gpsimd(gp):
                yield from norm_gpsimd(st, gp)
                yield 52.0
                gp.wait_ge(S("bc_taken"), 1)
                for g in range(NGR):
                    yield G0 + g * GU + 1.6
                    gp.wait_ge(S("scanned"), g + 1)
                    if g >= 3:
                        gp.wait_ge(S("summed"), g - 2)
                    gp.tensor_tensor(hc[:, g % 3, :], hb[:, g % 3, :], Cb, ALU.mult).then_inc(S("hc_ready"), 1)

            def scalar(act):
                yield 11.0
                act.wait_ge(S("in_projected"), 1)
                act.activation(xpad[:, :, DC - 1:DC - 1 + T], bank[:, 0:2, :], ACT.Copy).then_inc(S("x_taken"), 1)
                act.activation(zs, bank[:, 2:4, :], ACT.Exp, scale=-1.0).then_inc(S("z_exp"), 1)
                yield 18.0
                act.wait_ge(S("convolved"), 1)
                act.activation(e2, conv, ACT.Exp, scale=-1.0).then_inc(S("x_exp"), 1)
                yield 30.5
                act.wait_ge(S("x_dbl"), 1)
                act.activation(Bb, bank[:, 1, :], ACT.Copy)
                act.activation(Cb, bank[:, 2, :], ACT.Copy).then_inc(S("bc_taken"), 1)
                yield 32.0
                act.wait_ge(S("dt_in"), 1)
                act.activation(r2[:, 0], u2, ACT.Abs).then_inc(S("abs_ready"), 1)
                act.wait_ge(S("abs_ready"), 1)
                act.activation(r2[:, 1], r2[:, 0], ACT.Exp, scale=-1.0).then_inc(S("e_ready"), 1)
                for g in range(NGR):
                    yield G0 + g * GU + 0.2
                    act.wait_ge(S("dt_spread"), g + 1)
                    if g >= 2:
                        act.wait_ge(S("scanned"), g - 1)
                    act.activation(ab[:, g % 2, :], bank[:, 0, :], ACT.Exp, scale=acoef[:, g:g + 1]).then_inc(S("decay"), 1)

            def sync(sp):
                scratch = dt_dram[st.index]
                yield 51.0
                sp.wait_ge(S("parts_ready"), 1)
                for i in range(3):
                    for q in range(2):
                        sp.dma_start(scratch[i, q].rearrange("(c p) t -> p c t", p=P),
                                     parts2[:, i, q]).then_inc(S("parts_stored"), 16)
                yield 55.0
                sp.wait_ge(S("parts_stored"), 96)
                for i in range(3):
                    for q in range(2):
                        sp.dma_start(G[32 * i:32 * i + 32, q, :, :],
                                     scratch[i, q].rearrange("(b l) t -> l b t", l=32)).then_inc(S("grouped"), 16)

            def tensor(pe):
                yield 4.0
                pe.wait_ge(*S.once("normed"))
                turn(pe, y_sb, bank[:, 3, :]).then_inc(S("turned"), 1)
                yield 6.0
                pe.wait_ge(*S.once("hT_ready"))
                for c in range(4):
                    i = pe.matmul(bank[:, c, :], wc("win")[:, c * P:(c + 1) * P], hT[:, :], start=True, stop=True)
                i.then_inc(S("in_projected"), 1)
                yield 25.0
                pe.wait_ge(S("xs_ready"), 1)
                pe.wait_ge(S("z_done"), 1)
                for n, w in enumerate(("wxd", "wxb", "wxc")):
                    for c in range(NCH):
                        i = pe.matmul(bank[:, n, :], wc(w)[:, c * P:(c + 1) * P], xs[:, c, :],
                                      start=c == 0, stop=c == NCH - 1)
                i.then_inc(S("x_dbl"), 1)
                yield 61.0
                pe.wait_ge(S("grouped"), 96)
                pe.wait_ge(S("bc_taken"), 1)

                def spread(g):
                    if g:
                        pe.wait_ge(S("decay"), g)
                    sel = kb("selG", 96)[:, (g % 4) * P:(g % 4 + 1) * P]
                    pe.matmul(bank[:, 0, :], sel, G[:, 0, g // 4, :], start=True, stop=True).then_inc(S("dt_spread"), 1)
                    if g:
                        pe.wait_ge(S("u_ready"), g)
                    pe.matmul(bank[:, 1, :], sel, G[:, 1, g // 4, :], start=True, stop=True).then_inc(S("dtx_spread"), 1)

                def collect(g):
                    pe.wait_ge(S("hc_ready"), g + 1)
                    c, q = g // 16, g // 4 % 4
                    pe.matmul(bank[32 * q:32 * q + 32, 2 + c, :], sel_sum[:, (g % 4) * 32:(g % 4 + 1) * 32],
                              hc[:, g % 3, :], start=g % 4 == 0, stop=g % 4 == 3,
                              skip_group_check=True).then_inc(S("summed"), 1)

                for g in range(NGR + 2):
                    if g < NGR:
                        yield G0 + g * GU
                        spread(g)
                    if g >= 2:
                        yield G0 + g * GU + 0.5
                        collect(g - 2)
                end = G0 + NGR * GU + 4.0
                yield end + 3.0
                pe.wait_ge(S("gated"), 1)
                for j in range(NT):
                    for c in range(NCH):
                        i = pe.matmul(bank[:, 0, j * P:(j + 1) * P], yf[:, c, j * P:(j + 1) * P],
                                      wc("wout")[:, c * P:(c + 1) * P], start=c == 0, stop=c == NCH - 1)
                i.then_inc(S("out_projected"), 1)

            program = {"vector": vector, "gpsimd": gpsimd, "scalar": scalar, "sync": sync, "tensor": tensor}
            return program, G0 + NGR * GU + 10.0, S.once("done")

        def moe2(st, wc):
            buf, link = st.buf, st.chain["vector"]
            bank = banks[:, st.index]
            x_sb, y_sb, h_sb, hT, base = buf["x"], buf["y"], buf["h"], buf["hT"], buf["base"]
            room = Room(st)
            acc, hbuf, lg, big8 = room([P, NT, C]), room([P, 8, T]), room([P, 7, NT, E8]), room([P, 2, 256])

            S = st.signals("moe2_")

            parts = experts(st, S, 12.0, ACT.Gelu, wc("wup"), wc("wdn"), None, lg[:, 5], acc, hbuf, "centred")
            end = parts[3]

            def tensor(pe):
                yield 4.0
                pe.wait_ge(*S.once("normed"))
                turn(pe, y_sb, bank[:, 3, :]).then_inc(S("turned"), 1)
                yield 6.0
                pe.wait_ge(*S.once("hT_ready"))
                for j in range(NT):
                    i = pe.matmul(bank[:, 2, j * E8:(j + 1) * E8], hT[:, j * P:(j + 1) * P], wc("gw"),
                                  start=True, stop=True)
                i.then_inc(S("logits"), 1)
                yield from parts[0](pe)

            def vector(dve):
                i = yield from norm_vector(st, dve, x_sb, y_sb)
                i.then_inc(S("normed"), 1)
                yield 5.0
                dve.wait_ge(*S.once("turned"))
                dve.tensor_copy(hT[:, :], bank[:, 3, :]).then_inc(S("hT_ready"), 1)
                yield 7.0
                dve.wait_ge(S("logits"), 1)
                row = [P, NT, E8]
                link(dve, dve.tensor_tensor(lg[:, 0], bank[:, 2, 0:NT * E8].rearrange("p (t e) -> p t e", t=NT),
                                            wc("eb").unsqueeze(1).broadcast_to(row), ALU.add))
                link(dve, dve.tensor_reduce(lg[:, 6, :, 0:1], lg[:, 0], AX.X, ALU.max))
                dve.tensor_tensor(lg[:, 1], lg[:, 0], lg[:, 6, :, 0:1].broadcast_to(row),
                                  ALU.subtract).then_inc(S("centred"), 1)
                yield 9.0
                dve.wait_ge(S("exped"), 1)
                link(dve, dve.tensor_reduce(lg[:, 6, :, 1:2], lg[:, 2], AX.X, ALU.add))
                link(dve, dve.reciprocal(lg[:, 6, :, 2:3], lg[:, 6, :, 1:2]))
                link(dve, dve.tensor_tensor(lg[:, 3], lg[:, 2], lg[:, 6, :, 2:3].broadcast_to(row), ALU.mult))
                rank(st, dve, big8, lg[:, 3], E8, lg[:, 4])
                yield 12.0
                link(dve, dve.tensor_scalar(lg[:, 4], lg[:, 4], 1.5, None, ALU.is_lt))
                link(dve, dve.tensor_tensor(lg[:, 3], lg[:, 3], lg[:, 4], ALU.mult))
                link(dve, dve.tensor_reduce(lg[:, 6, :, 3:4], lg[:, 3], AX.X, ALU.add))
                link(dve, dve.tensor_scalar(lg[:, 6, :, 4:5], lg[:, 6, :, 3:4], 1e-6, None, ALU.add))
                link(dve, dve.reciprocal(lg[:, 6, :, 5:6], lg[:, 6, :, 4:5]))
                link(dve, dve.tensor_tensor(lg[:, 5], lg[:, 3], lg[:, 6, :, 5:6].broadcast_to(row), ALU.mult))
                yield from parts[2](dve)
                i = yield from norm_vector(st, dve, acc, h_sb, end)
                link(dve, i)
                dve.wait_ge(S("base_ready"), 1)
                dve.tensor_tensor(x_sb[:, :, :], h_sb[:, :, :], base[:, :, :], ALU.add).then_inc(S("done"), 1)

            def scalar(act):
                yield 8.0
                act.wait_ge(S("centred"), 1)
                act.activation(lg[:, 2], lg[:, 1], ACT.Exp).then_inc(S("exped"), 1)
                yield from parts[1](act)

            def gpsimd(gp):
                yield from norm_gpsimd(st, gp)
                yield 4.0
                gp.wait_ge(*S.once("normed"))
                gp.tensor_tensor(base[:, :, :], x_sb[:, :, :], y_sb[:, :, :], ALU.add).then_inc(S("base_ready"), 1)
                yield from norm_gpsimd(st, gp, end)

            program = {"vector": vector, "gpsimd": gpsimd, "scalar": scalar, "tensor": tensor}
            return program, end + 5.0, S.once("done")

        def lora3(st, wc):
            buf, link = st.buf, st.chain["vector"]
            bank = banks[:, st.index]
            x_sb, y_sb, hT, base = buf["x"], buf["y"], buf["hT"], buf["base"]
            room = Room(st)
            mid, gt, cls, big8 = room([P, 4, T]), room([P, 8, E8]), room([P, P]), room([P, 2, 256])

            S = st.signals("lora_")

            def vector(dve):
                i = yield from norm_vector(st, dve, x_sb, y_sb)
                i.then_inc(S("normed"), 1)
                yield 5.0
                dve.wait_ge(*S.once("turned"))
                link(dve, dve.tensor_copy(hT[:, :], bank[:, 3, :]))
                dve.tensor_copy(cls, hT[:, 0:1].broadcast_to([P, P])).then_inc(S("hT_ready"), 1)
                yield 7.0
                dve.wait_ge(S("logits"), 1)
                link(dve, dve.tensor_copy(gt[:, 0], bank[:, 3, 0:E8]))
                rank(st, dve, big8, gt[:, 0:1], E8, gt[:, 1:2], 1)
                link(dve, dve.tensor_scalar(gt[:, 1], gt[:, 1], 1.5, None, ALU.is_lt))
                link(dve, dve.tensor_reduce(gt[:, 6, 0:1], gt[:, 0], AX.X, ALU.max))
                dve.tensor_scalar(gt[:, 2], gt[:, 0], gt[:, 6, 0:1], None, ALU.subtract).then_inc(S("centred"), 1)
                yield 10.0
                dve.wait_ge(S("exped"), 1)
                link(dve, dve.tensor_tensor(gt[:, 4], gt[:, 3], gt[:, 1], ALU.mult))
                link(dve, dve.tensor_reduce(gt[:, 6, 1:2], gt[:, 4], AX.X, ALU.add))
                link(dve, dve.reciprocal(gt[:, 6, 2:3], gt[:, 6, 1:2]))
                link(dve, dve.tensor_scalar(gt[:, 5], gt[:, 4], gt[:, 6, 2:3], None, ALU.mult))
                pair = gt[:, 5].rearrange("p (c two) -> p c two", two=2)
                dve.tensor_copy(gt[0:64, 7, 0:4], pair[0:64, :, 0])
                dve.tensor_copy(gt[64:128, 7, 0:4], pair[64:128, :, 1]).then_inc(S("gates_ready"), 1)
                yield 22.0
                dve.wait_ge(S("out"), 1)
                dve.wait_ge(S("base_ready"), 1)
                dve.tensor_tensor(x_sb[:, :, :], base[:, :, :], tiles(bank[:, 2, :]), ALU.add).then_inc(S("done"), 1)

            def gpsimd(gp):
                yield from norm_gpsimd(st, gp)
                yield 4.0
                gp.wait_ge(*S.once("normed"))
                gp.tensor_tensor(base[:, :, :], x_sb[:, :, :], y_sb[:, :, :], ALU.add).then_inc(S("base_ready"), 1)

            def scalar(act):
                yield 9.0
                act.wait_ge(S("centred"), 1)
                act.activation(gt[:, 3], gt[:, 2], ACT.Exp).then_inc(S("exped"), 1)
                for c in range(4):
                    yield 12.0 + c
                    if c == 0:
                        act.wait_ge(S("gates_ready"), 1)
                    act.wait_ge(S("mid"), c + 1)
                    act.activation(mid[:, c, :], bank[:, c % 2, :], ACT.Copy, scale=gt[:, 7, c:c + 1]).then_inc(S("mid_ready"), 1)

            def tensor(pe):
                yield 4.0
                pe.wait_ge(*S.once("normed"))
                turn(pe, y_sb, bank[:, 3, :]).then_inc(S("turned"), 1)
                yield 6.0
                pe.wait_ge(*S.once("hT_ready"))
                pe.matmul(bank[:, 3, 0:E8], cls, wc("wr3"), start=True, stop=True).then_inc(S("logits"), 1)
                for c in range(4):
                    yield (6.0 if c < 2 else 11.0) + c
                    if c >= 2:
                        pe.wait_ge(S("mid_ready"), c - 1)
                    pe.matmul(bank[:, c % 2, :], wc("a3")[:, c * P:(c + 1) * P], hT[:, :], start=True,
                              stop=True).then_inc(S("mid"), 1)
                yield 17.0
                pe.wait_ge(S("mid_ready"), 4)
                for j in range(NT):
                    for c in range(4):
                        i = pe.matmul(bank[:, 2, j * P:(j + 1) * P], mid[:, c, j * P:(j + 1) * P],
                                      wc("b3")[:, c * P:(c + 1) * P], start=c == 0, stop=c == 3)
                i.then_inc(S("out"), 1)

            return {"vector": vector, "gpsimd": gpsimd, "scalar": scalar, "tensor": tensor}, 23.0, S.once("done")

        with ExitStack() as ctx:
            w_c = sb(ctx, "w_c", [P, width(PACK_C)])
            wc = Pieces(w_c, PACK_C)
            acoef = sb(ctx, "acoef", [P, NGR])
            sel_sum = sb(ctx, "sel_sum", [P, P])
            load_weights([(w_c, pc), (sel_sum, sel_y)])

            def decay_rates(block):
                @block.scalar
                def _(act):
                    act.activation(acoef[:, :], wc("alog"), ACT.Exp).then_inc(load_sem, 1)

                @block.vector
                def _(dve):
                    dve.wait_ge(load_sem, loads[0] + 1)
                    dve.tensor_scalar(acoef[:, :], acoef[:, :], -1.0, None, ALU.mult)
            stage_block(decay_rates)

            x2_b = x2.rearrange("(b t p) c -> p b t c", b=B, p=P)
            out_b = out.rearrange("(b t p) c -> p b t c", b=B, p=P)
            with nc.Fori(0, B // 2) as pair:
                def plan_c(st):
                    own, b = st.buf["x"][:, :, :], bass.ds(pair * 2 + st.index, 1)
                    c3 = wc("cols3")
                    yield load_x(st, [(own, x2_b[:, b, :, :])])
                    yield mamba(st, wc, acoef, sel_sum)
                    yield moe2(st, wc)
                    yield attention(st, "a3_", st.buf["y"], wc("wq3"), wc("wk3"), wc("wv3"), wc("wo3"),
                                    c3[:, 0:1], c3[:, 1:2], wc("bv3"), None, float(HD) ** -0.5, False, True,
                                    None, None, False)
                    yield lora3(st, wc)
                    yield store_x(st, [(own, out_b[:, b, :, :])])

                streams_of(plan_c, OFFSET_C)


def fixed_tables():
    ident = np.eye(P, dtype=np.float32)
    tri16 = np.tile((np.arange(16)[None, :] < np.arange(16)[:, None]).astype(np.float32).reshape(1, 256), (P, 1))
    sel16 = np.zeros((P, 8, P), np.float32)
    for e in range(E0):
        sel16[e, e // 2, (e % 2) * 64:(e % 2 + 1) * 64] = 1
    sel_y = np.zeros((P, 4, 32), np.float32)
    for n in range(DS):
        for l in range(GD):
            for j in range(4):
                sel_y[n * GD + l, j, j * GD + l] = 1
    p = np.arange(P)
    causal = np.where(p[None, :] > p[:, None], NEG, 0.0)
    corner_a, corner_b = np.zeros((P, P)), np.zeros((P, P))
    corner_a[P - 1, 0] = NEG
    corner_b[0, P - 1] = NEG
    same = np.where(p[None, :] % 16 == p[:, None] % 16, 0.0, NEG)
    sel_g = np.zeros((P, 4, P))
    for part in range(3):
        for j in range(4):
            for l in range(GD):
                sel_g[part * 32 + j * GD + l, j, l::GD] = 1
    kb = np.concatenate([ident, causal, causal.T, corner_a, corner_b, np.tile(same, (1, 4)),
                         sel_g.reshape(P, -1), np.ones((P, 512))], 1).astype(np.float32)
    theta = np.power(np.float32(10000.0), (2.0 * np.arange(HD // 2) / HD).astype(np.float32)).astype(np.float32)
    angle = (np.arange(T, dtype=np.float32)[None, :] * theta[:, None]).astype(np.float32).astype(np.float64)
    rows = np.arange(P) % HD
    cos = np.cos(angle)[rows // 2].astype(np.float32)
    sin = (np.sin(angle)[rows // 2] * np.where(rows % 2 == 0, -1.0, 1.0)[:, None]).astype(np.float32)
    return np.concatenate([ident, tri16, sel16.reshape(P, -1)], 1), kb, sel_y.reshape(P, P), cos, sin


def kernel(**inputs):
    import concourse.bacc as bacc
    from concourse.bass_utils import run_bass_kernel_spmd

    a = {k: np.asarray(v) for k, v in inputs.items()}

    def row(v):
        return np.broadcast_to(v.reshape(1, -1), (P, v.size))

    def packed(pieces, pack):
        for (name, n) in pack:
            assert pieces[name].shape == (P, n), (name, pieces[name].shape)
        return np.ascontiguousarray(np.concatenate([pieces[name] for name, _ in pack], 1))

    tables, tables_b, sel_y, cos, sin = fixed_tables()
    wqkv0, bqkv0 = a["L0_attn_w_qkv"], a["L0_attn_b_qkv"]
    swap = np.arange(P) ^ 1
    pa = {
        "wq0": wqkv0[:, 0:128], "wk0": wqkv0[:, 128:256], "wv0": wqkv0[:, 256:384], "wo0": a["L0_attn_w_out"],
        "bv0": row(bqkv0[256:384]), "bo0": row(a["L0_attn_b_out"]),
        "cols0": np.stack([a["L0_attn_ln_gamma"], a["L0_attn_ln_beta"], bqkv0[0:128], bqkv0[128:256]], 1),
        "wg0": a["L0_ffn_Wg"].T, "bc0": row(a["L0_ffn_bias_corr"]),
        "w1_0": a["L0_ffn_W1"].reshape(1024, 128).T, "ws1_0": a["L0_ffn_Ws1"].T,
        "w2_0": a["L0_ffn_W2"].transpose(0, 2, 1).reshape(8, 128, 128).transpose(1, 0, 2).reshape(128, 1024),
        "ws2_0": a["L0_ffn_Ws2"].T,
        "wq1": a["L1_attn_Wq"].T, "wk1": a["L1_attn_Wk"].T, "wv1": a["L1_attn_Wv"].T, "wp1": a["L1_attn_Wp"].T,
        "wqs1": a["L1_attn_Wq"][swap].T, "wks1": a["L1_attn_Wk"][swap].T,
        "bv1": row(a["L1_attn_bv"]), "bp1": row(a["L1_attn_bp"]),
        "cols1": np.stack([a["L1_attn_bq"], a["L1_attn_bk"], a["L1_attn_bq"][swap], a["L1_attn_bk"][swap]], 1),
        "cos1": cos, "sin1": sin,
    }
    wqkv, bqkv = a["L1_ffn_Wqkv"], a["L1_ffn_bqkv"]
    pb = {
        "wq": wqkv[0:128].T, "wk": wqkv[128:256].T, "wv": wqkv[256:384].T, "wo": a["L1_ffn_Wo"].T,
        "cols": np.stack([bqkv[0:128], bqkv[128:256]], 1), "bv": row(bqkv[256:384]), "bo": row(a["L1_ffn_bo"]),
        "g1": row(a["L1_ffn_g1"]), "be1": row(a["L1_ffn_be1"]), "g2": row(a["L1_ffn_g2"]),
        "be2": row(a["L1_ffn_be2"]), "wg": a["L1_ffn_Wg"].T,
        "b1": a["L1_ffn_b1"].reshape(32, 128).T,
        "w1": a["L1_ffn_W1"].transpose(1, 0, 2).reshape(128, 4096),
        "w2": a["L1_ffn_W2"].reshape(32, 128, 128).transpose(1, 0, 2).reshape(128, 4096),
    }
    wx = a["L2_attn_W_x"]

    def chunked(w):
        return w.reshape(2, 128, -1).transpose(1, 0, 2).reshape(128, -1)

    state = np.arange(P) // GD
    pc = {
        "win": a["L2_attn_W_in"], "convw": chunked(a["L2_attn_conv_w"]), "convb": chunked(a["L2_attn_conv_b"]),
        "wxd": chunked(wx[:, np.zeros(P, int)]), "wxb": chunked(wx[:, 1 + state]), "wxc": chunked(wx[:, 17 + state]),
        "wdt": chunked(a["L2_attn_w_dt"]), "bdt": chunked(a["L2_attn_b_dt"]),
        "alog": a["L2_attn_A_log"].reshape(NGR, GD, DS).transpose(2, 1, 0).reshape(P, NGR),
        "dcol": chunked(a["L2_attn_D"]), "wout": chunked(a["L2_attn_W_out"]),
        "gw": a["L2_ffn_gate_w"].T, "eb": row(a["L2_ffn_expert_bias"]),
        "wup": a["L2_ffn_w_up"].transpose(2, 0, 1).reshape(128, 4096),
        "wdn": a["L2_ffn_w_down"].transpose(0, 2, 1).reshape(32, 128, 128).transpose(1, 0, 2).reshape(128, 4096),
        "wq3": a["L3_attn_Wq"].T, "wk3": a["L3_attn_Wk"].T, "wv3": a["L3_attn_Wv"].T, "wo3": a["L3_attn_Wo"].T,
        "cols3": np.stack([a["L3_attn_bq"], a["L3_attn_bk"]], 1), "bv3": row(a["L3_attn_bv"]),
        "wr3": a["L3_ffn_Wr"].T, "a3": a["L3_ffn_A"].reshape(512, 128).T,
        "b3": a["L3_ffn_Bw"].transpose(0, 2, 1).reshape(4, 128, 128).transpose(1, 0, 2).reshape(128, 512),
    }
    arrays = {"x": np.ascontiguousarray(a["L0_attn_x"].reshape(B * T, C)), "pa": packed(pa, PACK_A),
              "pb": packed(pb, PACK_B), "pc": packed(pc, PACK_C), "pk": tables, "pkb": tables_b,
              "b2": np.ascontiguousarray(a["L1_ffn_b2"]), "sel_y": sel_y}
    nc = bacc.Bacc("TRN2", target_bir_lowering=False, num_devices=1)
    handles = {k: nc.dram_tensor(f"in_{k}", v.shape, mybir.dt.from_np(v.dtype), kind="ExternalInput").ap()
               for k, v in arrays.items()}
    out = nc.dram_tensor("out", (B * T, C), F32, kind="ExternalOutput").ap()
    build(nc, *(handles[k] for k in ("x", "pa", "pb", "pc", "pk", "pkb", "b2", "sel_y")), out)
    r = run_bass_kernel_spmd(nc, [{f"in_{k}": v for k, v in arrays.items()}], core_ids=[0])
    return r.results[0]["out"].reshape(B, T, C)
```

```python
from contextlib import ExitStack

import concourse.bass as bass
import numpy as np
from concourse import mybir

F32 = mybir.dt.float32
BF16, I32 = mybir.dt.bfloat16, mybir.dt.int32
ALU = mybir.AluOpType
ACT = mybir.ActivationFunctionType
AX = mybir.AxisListType

P = 128
B, T, C = 8, 512, 128
NT = T // P
H, HD = 16, 8
GH = 4
NG = H // GH
TERMS = [(0, 0), (1, 0), (2, 0), (0, 1), (1, 1), (0, 2)]
KT = len(TERMS) * HD
TOP_HALF = -65536
NEG = -3.0e10
EPS = 1e-5
OFFSET_A, OFFSET_C = 11.0, 11.0
LOG1P = [0.999999969882, -0.499994931336, 0.33319096488, -0.248429790329, 0.191059928245,
         -0.13663213965, 0.0782255570325, -0.0295049865433, 0.00523262925133]
E0, I0 = 16, 64
E8, FF, NF = 8, 512, 4
SB, SH, SD = 8, 4, 32
DI, DS, DC = 256, 16, 4
NCH = DI // P
GD = P // DS
NGR = DI // GD

PACK_A = [("wq0", 128), ("wk0", 128), ("wv0", 128), ("wo0", 128), ("bv0", 128), ("bo0", 128),
          ("cols0", 4), ("wg0", 16), ("bc0", 16), ("w1_0", 1024), ("ws1_0", 128), ("w2_0", 1024),
          ("ws2_0", 128), ("wq1", 128), ("wk1", 128), ("wv1", 128), ("wp1", 128), ("wqs1", 128),
          ("wks1", 128), ("bv1", 128), ("bp1", 128), ("cols1", 4), ("cos1", 512), ("sin1", 512)]
PACK_B = [("wq", 128), ("wk", 128), ("wv", 128), ("wo", 128), ("cols", 2), ("bv", 128), ("bo", 128),
          ("g1", 128), ("be1", 128), ("g2", 128), ("be2", 128), ("wg", 8), ("b1", 32),
          ("w1", 4096), ("w2", 4096)]
PACK_C = [("win", 512), ("convw", 8), ("convb", 2), ("wxd", 256), ("wxb", 256), ("wxc", 256),
          ("wdt", 2), ("bdt", 2), ("alog", 32), ("dcol", 2), ("wout", 256), ("gw", 8), ("eb", 8),
          ("wup", 4096), ("wdn", 4096), ("wq3", 128), ("wk3", 128), ("wv3", 128), ("wo3", 128),
          ("cols3", 2), ("bv3", 128), ("wr3", 8), ("a3", 512), ("b3", 512)]
PACK_K = [("ident", 128), ("tri16", 256)]
PACK_KB = [("identb", 128), ("causal", 128), ("causalT", 128), ("cornA", 128), ("cornB", 128),
           ("block", 512), ("selG", 512), ("ones", 512), ("sel16", 1024)]


def width(pack):
    return sum(n for _, n in pack)


class Pieces:

    def __init__(self, tensor, pack):
        self.tensor, self.at, o = tensor, {}, 0
        for name, n in pack:
            self.at[name] = (o, n)
            o += n

    def __call__(self, name, p=P):
        o, n = self.at[name]
        return self.tensor[0:p, o:o + n]


class Chain:

    def __init__(self, sem):
        self.sem, self.n = sem, 0

    def __call__(self, eng, instruction):
        self.n += 1
        instruction.then_inc(self.sem, 1)
        eng.wait_ge(self.sem, self.n)


class Stream:

    def __init__(self, index, pool, taken, buffers):
        self.index, self.pool, self.taken, self.buf = index, pool, taken, buffers
        self.named, self.order = {}, {}
        self.chain = {e: Chain(self.sem(e + "_chain")) for e in ("vector", "gpsimd")}
        self.moments, self.rstd = self.sem("moments"), self.sem("rstd")
        self.norms = {"vector": 0, "gpsimd": 0}

    def sem(self, name):
        if name not in self.named:
            self.named[name] = self.pool[self.taken[0]]
            self.taken[0] += 1
        return self.named[name]

    def signals(self, stage, absent=()):
        return Signals(self, stage, absent)


class Signals:
    ONCE = ("normed", "turned", "hT_ready", "done")

    def __init__(self, st, stage, absent):
        self.st, self.stage, self.value = st, stage, {}
        for name in self.ONCE:
            if name not in absent:
                st.order[name] = self.value[name] = st.order.get(name, 0) + 1

    def __call__(self, name):
        return self.st.sem(name if name in self.ONCE else self.stage + name)

    def once(self, name):
        return self.st.sem(name), self.value[name]


def take_turns(programs):
    due = [[next(p), n, p] for n, p in enumerate(programs)]
    while due:
        first = min(due, key=lambda d: (d[0], d[1]))
        mark = next(first[2], None)
        if mark is None:
            due.remove(first)
        else:
            first[0] = mark


ENGINES = ("vector", "gpsimd", "scalar", "sync", "tensor")


def build(nc, x, pa, pb, pc, pk, pkb, b2, sel_y, out):
    top = ExitStack()
    with top:
        def sb(ctx, name, shape, dt=F32):
            return ctx.enter_context(nc.sbuf_tensor(name, shape, dt))

        load_sem = top.enter_context(nc.semaphore("weights_loaded"))
        pool = [top.enter_context(nc.semaphore(f"signal_{i}")) for i in range(150)]
        banks = top.enter_context(nc.psum_tensor("banks", [P, 2, 4, 512], F32))
        kc = Pieces(sb(top, "kc", [P, width(PACK_K)]), PACK_K)
        kb = Pieces(sb(top, "kb", [P, width(PACK_KB)], BF16), PACK_KB)
        ident, identb = kc("ident"), kb("identb")
        mhalf = sb(top, "mhalf", [P, NT])
        x1 = nc.dram_tensor("x1", (B * T, C), F32, kind="Internal").ap()
        x2 = nc.dram_tensor("x2", (B * T, C), F32, kind="Internal").ap()
        parts_dram = nc.dram_tensor("parts_dram", (2, 3, 2, P, T), BF16, kind="Internal").ap()
        dt_dram = nc.dram_tensor("dt_dram", (2, 3, 2, DI, T), BF16, kind="Internal").ap()
        ROOM = 64 * 256

        def buffers(s):
            names = {"x": [P, NT, C], "y": [P, NT, C], "h": [P, NT, C], "base": [P, NT, C], "hT": [P, T],
                     "stats": [P, NT, 6], "mom": [P, NT, 2], "veps": [P, NT], "rstd": [P, NT],
                     "room": [P, ROOM]}
            return {k: sb(top, f"{k}_{s}", v) for k, v in names.items()}

        memory = [buffers(0), buffers(1)]
        loads = [0]

        def stage_block(body):
            with nc.Block() as block:
                body(block)
            nc.all_engine_barrier()

        class Room:

            def __init__(self, st):
                self.t, self.at = st.buf["room"], 0

            def __call__(self, shape, dt=F32):
                n = int(np.prod(shape[1:]))
                words = n if dt == F32 else n // 2
                assert self.at + words <= ROOM, (self.at, words)
                flat = self.t[0:shape[0], self.at:self.at + words]
                self.at += words
                if dt == BF16:
                    flat = flat.bitcast(BF16)
                if len(shape) == 2:
                    return flat
                names = "abcde"[:len(shape) - 1]
                return flat.rearrange("p (%s) -> p %s" % (" ".join(names), " ".join(names)),
                                      **{k: s for k, s in zip(names, shape[1:])})

        def run(streams_stages):
            with nc.Block() as block:
                def programs(name, eng):
                    return [program(name, eng) for program in streams_stages]

                @block.vector
                def _(dve):
                    take_turns(programs("vector", dve))

                @block.gpsimd
                def _(gp):
                    take_turns(programs("gpsimd", gp))

                @block.scalar
                def _(act):
                    take_turns(programs("scalar", act))

                @block.sync
                def _(sp):
                    take_turns(programs("sync", sp))

                @block.tensor
                def _(pe):
                    take_turns(programs("tensor", pe))
            nc.gpsimd.sem_clear(range(pool[0].num, pool[-1].num + 1))
            nc.all_engine_barrier()

        def chain_of(stages, first):
            def program(name, eng):
                start = first
                for stage, length, entry in stages:
                    yield start
                    if entry is not None and (name != "sync" or "sync" in stage):
                        eng.wait_ge(*entry)
                    if name in stage:
                        for mark in stage[name](eng):
                            yield start + mark
                    start += length
            return program

        def norm_vector(st, dve, src, dst, t=0.0):
            stats, mom, rstd, link = st.buf["stats"], st.buf["mom"], st.buf["rstd"], st.chain["vector"]
            st.norms["vector"] += 1
            n = st.norms["vector"]
            yield t
            for j in range(NT):
                i = dve.bn_stats(stats[:, j, :], src[:, j, :])
            link(dve, i)
            for j in range(NT):
                i = dve.bn_aggr(mom[:, j, :], stats[:, j, :])
            i.then_inc(st.moments, 1)
            yield t + 2.0
            dve.wait_ge(st.rstd, n)
            for j in range(NT):
                i = dve.tensor_scalar(dst[:, j, :], src[:, j, :], mom[:, j, 0:1], rstd[:, j:j + 1],
                                      ALU.subtract, ALU.mult)
            return i

        def norm_gpsimd(st, gp, t=0.0):
            st.norms["gpsimd"] += 1
            yield t + 1.0
            gp.wait_ge(st.moments, st.norms["gpsimd"])
            st.chain["gpsimd"](gp, gp.tensor_scalar(st.buf["veps"][:, :], st.buf["mom"][:, :, 1], EPS, None, ALU.add))
            gp.tensor_tensor(st.buf["rstd"][:, :], st.buf["veps"][:, :], mhalf[:, :], ALU.pow).then_inc(st.rstd, 1)

        def turn(pe, src, bank):
            for j in range(NT):
                i = pe.transpose(bank[:, j * P:(j + 1) * P], src[:, j, :], ident)
            return i

        def tiles(bank):
            return bank.rearrange("p (t c) -> p t c", t=NT)

        def attention(st, tag, src, wq, wk, wv, wo, bq, bk, bv, bo, scale, causal, corners, swapped,
                      affine, double):
            buf, link = st.buf, st.chain["vector"]
            bank = banks[:, st.index]
            res, base, hT, h = buf["x"], buf["base"], buf["hT"], buf["h"]
            MAXB, VALB = bank[:, 0, :], bank[:, 3, :]
            room = Room(st)
            stacked = room([P, 2, H * T // 2])
            Qs, Ks = (stacked[:, i].bitcast(BF16).rearrange("p (h t) -> p h t", h=H) for i in range(2))
            vaug = room([P, NT, H, 32])
            oT, onorm = room([P, T]), room([P, NT, C])
            mx, rden = room([P, NG, 16]), room([P, NG, NT, GH])
            negm = room([16, NG, P], BF16)
            mark = room.at
            prob = room([P, 2, GH, T])
            room.at = mark
            q32, r32, ro = room([P, 2, T]), room([P, 2, T]), room([P, 2, T])
            parts = room([P, 3, 2, T], BF16)

            def of_part(v):
                return v.rearrange("i (d h) t -> i d (h t)", d=HD)

            first_query = [P * kt if causal else 0 for kt in range(NT)]
            keys = [P * (j + 1) if causal else T for j in range(NT)]

            S = st.signals(tag)

            U, M0, PERIOD, TURN = 0.65, 26.0, 22.0, 3.4
            if double:
                M0 += 4.0
            length = M0 + NG * PERIOD + 8.0

            def max_at(g, u):
                return M0 + g * PERIOD + u * U

            def score_at(g, u):
                return max_at(g, 16 + u) + TURN

            def max_bank(u):
                return bank[:, u % 2, :]

            def vector(dve):
                if double:
                    i = yield from norm_vector(st, dve, res, src)
                    link(dve, i)
                    i = yield from norm_vector(st, dve, src, h, 4.0)
                else:
                    i = yield from norm_vector(st, dve, res, src)
                i.then_inc(S("normed"), 1)
                t = 4.0 if double else 0.0
                yield t + 5.0
                dve.wait_ge(*S.once("turned"))
                if affine:
                    i = dve.tensor_scalar(hT[:, :], VALB, affine[0], affine[1], ALU.mult, ALU.add)
                else:
                    i = dve.tensor_copy(hT[:, :], VALB)
                i.then_inc(S("hT_ready"), 1)
                yield t + 8.0
                if swapped:
                    dve.wait_ge(S("qk_projected"), 1)
                    for i, (b, s) in enumerate(((bq, swapped[2]), (bk, swapped[3]))):
                        dve.scalar_tensor_tensor(q32[:, i, :], bank[:, i, :], b, swapped[4], ALU.add, ALU.mult)
                        k = dve.scalar_tensor_tensor(ro[:, i, :], bank[:, 2 + i, :], s, swapped[5],
                                                     ALU.add, ALU.mult)
                    k.then_inc(S("qk_taken"), 1)
                    dve.wait_ge(S("qk_taken"), 1)
                    link(dve, dve.tensor_tensor(q32, q32, ro, ALU.add))
                else:
                    dve.wait_ge(S("qk_taken"), 2)
                dve.tensor_copy(parts[:, 0], q32).then_inc(S("parts_ready"), 1)
                dve.wait_ge(S("parts_ready"), 1)
                link(dve, dve.tensor_tensor(r32, q32, parts[:, 0], ALU.subtract))
                yield t + 10.0
                dve.tensor_copy(parts[:, 1], r32).then_inc(S("parts_ready"), 1)
                dve.wait_ge(S("parts_ready"), 2)
                dve.tensor_tensor(parts[:, 2], r32, parts[:, 1], ALU.subtract).then_inc(S("parts_ready"), 1)
                yield t + 12.0
                dve.wait_ge(S("v_projected"), 1)
                dve.wait_ge(S("vaug_set"), 2)
                for j in range(NT):
                    i = dve.tensor_tensor(vaug[:, j, :, 0:HD],
                                          bank[:, 2, j * P:(j + 1) * P].rearrange("p (h d) -> p h d", h=H),
                                          bv.rearrange("p (h d) -> p h d", h=H), ALU.add)
                i.then_inc(S("v_ready"), 1)
                for g in range(NG + 1):
                    for u in range(16):
                        if g < NG:
                            yield max_at(g, u) + 0.2
                            dve.wait_ge(S("max_scored"), 16 * g + u + 1)
                            dve.tensor_reduce(mx[:, g, u:u + 1], max_bank(u)[:, 0:keys[u % NT]], AX.X,
                                              ALU.max).then_inc(S("max_reduced"), 1)
                        if g and u == 6:
                            yield max_at(g, u) + 0.4
                            dve.wait_ge(S("o_turned"), g)
                            o4 = VALB.rearrange("p (t h w) -> p t h w", t=NT, h=GH)
                            link(dve, dve.reciprocal(rden[:, g - 1, :, :], o4[:, :, :, HD]))
                            dve.tensor_tensor(
                                onorm[:, :, (g - 1) * 32:g * 32].rearrange("p t (h d) -> p t h d", h=GH),
                                o4[:, :, :, 0:HD],
                                rden[:, g - 1, :, :].unsqueeze(3).broadcast_to([P, NT, GH, HD]),
                                ALU.mult).then_inc(S("o_normed"), 1)
                    if g < NG:
                        yield max_at(g, 16) + 0.4
                        dve.wait_ge(S("max_turned"), g + 1)
                        dve.tensor_scalar(negm[:, g, :], MAXB[0:16, 0:P], -1.0, None,
                                          ALU.mult).then_inc(S("negmax_ready"), 1)
                end = max_at(NG, 7)
                yield end + 1.5
                dve.wait_ge(S("o_back"), 1)
                dve.tensor_copy(hT[:, :], MAXB).then_inc(S("oT_ready"), 1)
                yield end + 3.0
                dve.wait_ge(S("out_projected"), 1)
                dve.wait_ge(S("base_ready"), 1)
                dve.tensor_tensor(res[:, :, :], base[:, :, :], tiles(bank[:, 1, :]), ALU.add).then_inc(S("done"), 1)

            def gpsimd(gp):
                chain = st.chain["gpsimd"]
                yield from norm_gpsimd(st, gp)
                if double:
                    yield 2.0
                    gp.memset(stacked[:, 0, 0:H * T // 4], 0.0)
                    yield from norm_gpsimd(st, gp, 4.0)
                    yield 6.0
                    gp.memset(stacked[:, 0, H * T // 4:], 0.0)
                else:
                    yield 4.0
                    gp.memset(stacked[:, 0], 0.0)
                yield 7.0
                gp.memset(stacked[:, 1], 0.0).then_inc(S("cleared"), 1)
                yield 9.0
                chain(gp, gp.memset(vaug, 0.0))
                gp.memset(vaug[:, :, :, HD:HD + 1], 1.0).then_inc(S("vaug_set"), 2)
                yield 14.0
                gp.wait_ge(*S.once("normed"))
                frm = res
                if double:
                    chain(gp, gp.tensor_tensor(base[:, :, :], res[:, :, :], src[:, :, :], ALU.add))
                    frm = base
                if bo is not None:
                    for j in range(NT):
                        i = gp.tensor_tensor(base[:, j, :], frm[:, j, :], bo, ALU.add)
                else:
                    i = gp.tensor_copy(base[:, :, :], frm[:, :, :])
                i.then_inc(S("base_ready"), 1)

            def scalar(act):
                yield 7.0 + (4.0 if double else 0.0)
                if not swapped:
                    act.wait_ge(S("qk_projected"), 1)
                    act.activation(q32[:, 0, :], bank[:, 0, :], ACT.Identity, bias=bq).then_inc(S("qk_taken"), 1)
                    act.activation(q32[:, 1, :], bank[:, 1, :], ACT.Identity, bias=bk).then_inc(S("qk_taken"), 1)
                for g in range(NG):
                    for u in range(16):
                        yield score_at(g, u) + 0.2
                        n, kt = 16 * g + u, u // GH
                        if n >= 8 and n % 4 == 0:
                            act.wait_ge(S("av_done"), n // 4 - 1)
                        act.wait_ge(S("scored"), n + 1)
                        act.activation(prob[:, kt % 2, u % GH, first_query[kt]:T], bank[:, 1 + n % 2, first_query[kt]:T],
                                       ACT.Exp, scale=scale).then_inc(S("exped"), 1)
                    yield max_at(g + 1, 4)
                    act.wait_ge(S("av_done"), 4 * (g + 1))
                    if g >= 1:
                        act.wait_ge(S("o_turned"), g)
                    act.activation(oT, VALB, ACT.Copy).then_inc(S("av_taken"), 1)

            def sync(sp):
                t = 4.0 if double else 0.0
                yield t + 9.0
                scratch = parts_dram[st.index]
                for i in range(3):
                    yield t + 10.0 + 2 * i
                    sp.wait_ge(S("parts_ready"), i + 1)
                    sp.dma_start(scratch[i].rearrange("q p t -> p q t"), parts[:, i]).then_inc(S("parts_stored"), 16)
                    yield t + 12.0 + 2 * i
                    sp.wait_ge(S("parts_stored"), 16 * (i + 1))
                    n, first = 3 - i, (0, 3, 5)[i]
                    if i == 0:
                        sp.wait_ge(S("cleared"), 1)
                    sp.dma_start(Ks[first * HD:(first + n) * HD, :, :].rearrange("p h t -> p (h t)"),
                                 of_part(scratch[i:i + 1, 1]).broadcast_to([n, HD, H * T])).then_inc(S("grouped"), 16)
                    n, first = i + 1, (5, 3, 0)[i]
                    sp.dma_start(Qs[first * HD:(first + n) * HD, :, :].rearrange("p h t -> p (h t)"),
                                 of_part(scratch[0:n, 0])).then_inc(S("grouped"), 16)
                sp.dma_start(Ks[KT:KT + 1, :, :], kb("ones", H)).then_inc(S("grouped"), 16)
                for g in range(NG):
                    yield max_at(g, 16) + 0.8
                    sp.wait_ge(S("negmax_ready"), g + 1)
                    sp.dma_start(Qs[KT:KT + 1, g * GH:(g + 1) * GH, :], negm[:, g, :]).then_inc(S("negmax_placed"), 16)

            def tensor(pe):
                t = 4.0 if double else 0.0
                yield t + 4.0
                pe.wait_ge(*S.once("normed"))
                turn(pe, h if double else src, VALB).then_inc(S("turned"), 1)
                yield t + 6.0
                pe.wait_ge(*S.once("hT_ready"))
                pe.matmul(bank[:, 0, :], wq, hT[:, :], start=True, stop=True)
                i = pe.matmul(bank[:, 1, :], wk, hT[:, :], start=True, stop=True)
                if swapped:
                    pe.matmul(bank[:, 2, :], swapped[0], hT[:, :], start=True, stop=True)
                    i = pe.matmul(bank[:, 3, :], swapped[1], hT[:, :], start=True, stop=True)
                i.then_inc(S("qk_projected"), 1)
                yield t + 9.0
                if swapped:
                    pe.wait_ge(S("qk_taken"), 1)
                for j in range(NT):
                    i = pe.matmul(bank[:, 2, j * P:(j + 1) * P], hT[:, j * P:(j + 1) * P], wv,
                                  start=True, stop=True)
                i.then_inc(S("v_projected"), 1)

                def max_unit(g, u):
                    n, h, j = 16 * g + u, g * GH + u // NT, u % NT
                    yield max_at(g, u)
                    if n == 0:
                        pe.wait_ge(S("grouped"), 16 * 7)
                        pe.wait_ge(S("qk_taken"), 1 if swapped else 2)
                    if g and u == 0:
                        pe.wait_ge(S("negmax_ready"), g)
                    elif g and u == 1:
                        pe.wait_ge(S("exped"), 16 * g - 1)
                    elif u >= 2:
                        pe.wait_ge(S("max_reduced"), n - 1)
                    to = max_bank(u)
                    masks = []
                    if causal:
                        masks = [(j * P, kb("causal"))]
                    if corners and j == 0:
                        masks = [(T - P, kb("cornB"))]
                    if corners and j == NT - 1:
                        masks = [(0, kb("cornA"))]
                    m = pe.matmul(to[:, 0:keys[j]], Qs[:, h, j * P:(j + 1) * P], Ks[:, h, 0:keys[j]],
                                  start=True, stop=not masks)
                    for c, mask in masks:
                        m = pe.matmul(to[:, c:c + P], identb, mask, start=False, stop=True)
                    m.then_inc(S("max_scored"), 1)

                def score_unit(g, u):
                    n, kt, head = 16 * g + u, u // GH, g * GH + u % GH
                    q0 = first_query[kt]
                    yield score_at(g, u)
                    if n % 16 == 0:
                        pe.wait_ge(S("negmax_placed"), 16 * (g + 1))
                    if n == 0:
                        pe.wait_ge(S("v_ready"), 1)
                    if n >= 2:
                        pe.wait_ge(S("exped"), n - 1)
                    b = bank[:, 1 + n % 2, :]
                    masks = []
                    if causal:
                        masks = [(q0, kb("causalT"))]
                    if corners and kt == NT - 1:
                        masks = [(0, kb("cornA"))]
                    if corners and kt == 0:
                        masks = [(T - P, kb("cornB"))]
                    i = pe.matmul(b[:, q0:T], Ks[:, head, kt * P:(kt + 1) * P], Qs[:, head, q0:T],
                                  start=True, stop=not masks)
                    for c, mask in masks:
                        i = pe.matmul(b[:, c:c + P], identb, mask, start=False, stop=True)
                    i.then_inc(S("scored"), 1)

                def value_pack(a):
                    g, kt = divmod(a, NT)
                    pe.wait_ge(S("exped"), 4 * (a + 1))
                    if kt == 0 and g >= 1:
                        pe.wait_ge(S("o_normed"), g)
                    q0 = first_query[kt]
                    for hl in range(GH):
                        m = pe.matmul(VALB[32 * hl:32 * hl + 32, q0:T], vaug[:, kt, g * GH + hl, :],
                                      prob[:, a % 2, hl, q0:T], start=kt == 0, stop=kt == NT - 1,
                                      skip_group_check=True)
                    m.then_inc(S("av_done"), 1)

                def turn_maxima(g):
                    yield max_at(g, 16)
                    pe.wait_ge(S("max_reduced"), 16 * (g + 1))
                    pe.transpose(MAXB[0:16, 0:P], mx[:, g, :], ident).then_inc(S("max_turned"), 1)

                def turn_values(g):
                    yield max_at(g + 1, 5)
                    pe.wait_ge(S("av_taken"), g + 1)
                    for j in range(NT):
                        i = pe.transpose(VALB[:, j * P:(j + 1) * P], oT[:, j * P:(j + 1) * P], ident)
                    i.then_inc(S("o_turned"), 1)

                for u in range(16):
                    yield from max_unit(0, u)
                yield from turn_maxima(0)
                for g in range(NG):
                    more = g + 1 < NG
                    for u in range(16):
                        yield from score_unit(g, u)
                        if u in (7, 11, 15):
                            value_pack(NT * g + u // 4 - 1)
                    for u in range(16):
                        if u == 2:
                            yield max_at(g + 1, u)
                            value_pack(NT * g + 3)
                        if u == 5:
                            yield from turn_values(g)
                        if more:
                            yield from max_unit(g + 1, u)
                    if more:
                        yield from turn_maxima(g + 1)
                end = max_at(NG, 7)
                yield end + 1.0
                pe.wait_ge(S("o_normed"), NG)
                turn(pe, onorm, MAXB).then_inc(S("o_back"), 1)
                yield end + 2.0
                pe.wait_ge(S("oT_ready"), 1)
                for j in range(NT):
                    i = pe.matmul(bank[:, 1, j * P:(j + 1) * P], hT[:, j * P:(j + 1) * P], wo,
                                  start=True, stop=True)
                i.then_inc(S("out_projected"), 1)

            program = {"vector": vector, "gpsimd": gpsimd, "scalar": scalar, "sync": sync, "tensor": tensor}
            return program, length, S.once("done")

        def tri(n):
            full = kc("tri16").rearrange("p (a b) -> p a b", a=16)
            return full[:, 0:n, 0:n]

        def rank(st, dve, big, vals, n, ranks, t=NT):
            link = st.chain["vector"]
            shape = [P, t, n, n]
            other, own = vals.unsqueeze(2).broadcast_to(shape), vals.unsqueeze(3).broadcast_to(shape)
            gt, eq = (big[:, i, 0:t * n * n].rearrange("p (t a b) -> p t a b", t=t, a=n) for i in range(2))
            dve.tensor_tensor(gt, other, own, ALU.is_gt)
            link(dve, dve.tensor_tensor(eq, other, own, ALU.is_equal))
            link(dve, dve.tensor_tensor(eq, eq, tri(n).unsqueeze(1).broadcast_to(shape), ALU.mult))
            link(dve, dve.tensor_tensor(gt, gt, eq, ALU.add))
            link(dve, dve.tensor_reduce(ranks, gt, AX.X, ALU.add))

        def load_constants(block):
            wide = memory[0]["room"][:, 0:width(PACK_KB)]

            @block.sync
            def _(sp):
                sp.dma_start(kc.tensor[:, :], pk).then_inc(load_sem, 16)
                sp.dma_start(wide, pkb).then_inc(load_sem, 16)
                sp.wait_ge(load_sem, 32)

            @block.vector
            def _(dve):
                dve.wait_ge(load_sem, 32)
                dve.tensor_copy(kb.tensor[:, :], wide)

            @block.gpsimd
            def _(gp):
                gp.memset(mhalf[:, :], -0.5)
        loads[0] = 32
        stage_block(load_constants)

        def load_weights(pairs):
            def body(block):
                @block.sync
                def _(sp):
                    for tensor, src in pairs:
                        n = tensor.shape[1]
                        for a in range(0, n, 2048):
                            sp.dma_start(tensor[:, a:min(n, a + 2048)], src[:, a:min(n, a + 2048)]).then_inc(load_sem, 16)
                            loads[0] += 16
                    sp.wait_ge(load_sem, loads[0])
            stage_block(body)

        def load_x(st, views):
            def sync(sp):
                yield 0.0
                for own, v in views:
                    sp.dma_start(own, v).then_inc(st.sem("x_loaded"), 16)
            return {"sync": sync}, 3.0, (st.sem("x_loaded"), 16 * len(views))

        def store_x(st, views):
            def sync(sp):
                yield 0.0
                for own, v in views:
                    sp.dma_start(v, own).then_inc(st.sem("x_stored"), 16)
                sp.wait_ge(st.sem("x_stored"), 16 * len(views))
            return {"sync": sync}, 3.0, None

        def round_of(plans, offset=0.0):
            taken, programs = [0], []
            for s, plan in plans:
                st = Stream(s, pool, taken, memory[s])
                stages, entry = [], None
                for program, length, result in plan(st):
                    stages.append((program, length, entry))
                    entry = result
                programs.append(chain_of(stages, s * offset))
            run(programs)

        def together(plan, rounds, offset):
            with nc.Fori(0, rounds) as r:
                round_of([(s, lambda st, s=s: plan(st, r * 2 + s)) for s in range(2)], offset)

        def staggered(early, late, rounds):
            def whole(st, n):
                yield from early(st, n)
                yield from late(st, n)

            def shifted(st, n):
                yield from late(st, n)
                yield from early(st, n + 2)

            round_of([(1, lambda st: early(st, 1))])
            with nc.Fori(0, rounds - 1) as r:
                round_of([(0, lambda st: whole(st, r * 2)), (1, lambda st: shifted(st, r * 2 + 1))])
            last = 2 * (rounds - 1)
            round_of([(0, lambda st: whole(st, last)), (1, lambda st: late(st, last + 1))])

        def moe0(st, wa):
            buf, link = st.buf, st.chain["vector"]
            bank = banks[:, st.index]
            x_sb, y_sb, hT = buf["x"], buf["y"], buf["hT"]
            room = Room(st)
            hid, relu, big = room([P, 9, T]), room([P, 2, T]), room([P, 2, 1024])
            sc, gsc, cwT = room([P, 12, NT, E0]), room([P, 8, NT, 4, 2]), room([3 * E0, T], BF16)
            w_parts = room([P, NT, 3 * E0])
            elog, choice, masked, ranks, sel, wsel = (sc[:, i] for i in range(6))

            S = st.signals("moe0_")

            def vector(dve):
                i = yield from norm_vector(st, dve, x_sb, y_sb)
                i.then_inc(S("normed"), 1)
                yield 5.0
                dve.wait_ge(*S.once("turned"))
                dve.tensor_copy(hT[:, :], bank[:, 0, :]).then_inc(S("hT_ready"), 1)
                yield 8.0
                dve.wait_ge(S("exp_logits"), 1)
                link(dve, dve.tensor_scalar(sc[:, 6], elog, 1.0, None, ALU.add))
                link(dve, dve.reciprocal(sc[:, 7], sc[:, 6]))
                sig = sc[:, 7]
                link(dve, dve.tensor_tensor(choice, sig, wa("bc0").unsqueeze(1).broadcast_to([P, NT, E0]), ALU.add))
                yield 9.0
                c4 = choice.rearrange("p t (g q r) -> p (t g) q r", q=2, r=2)
                hi, lo = (gsc[:, i].rearrange("p t g q -> p (t g) q") for i in range(2))
                dve.tensor_tensor(hi, c4[:, :, :, 0], c4[:, :, :, 1], ALU.max)
                link(dve, dve.tensor_tensor(lo, c4[:, :, :, 0], c4[:, :, :, 1], ALU.min))
                t1, t2, t3 = (gsc[:, i, :, :, 0].rearrange("p t g -> p (t g)") for i in (2, 3, 4))
                dve.tensor_tensor(t1, hi[:, :, 0], hi[:, :, 1], ALU.max)
                dve.tensor_tensor(t2, hi[:, :, 0], hi[:, :, 1], ALU.min)
                link(dve, dve.tensor_tensor(t3, lo[:, :, 0], lo[:, :, 1], ALU.max))
                link(dve, dve.tensor_tensor(t2, t2, t3, ALU.max))
                gs, gr = sc[:, 8, :, 0:4], sc[:, 9, :, 0:4]
                link(dve, dve.tensor_tensor(gs, gsc[:, 2, :, :, 0], gsc[:, 3, :, :, 0], ALU.add))
                yield 11.0
                rank(st, dve, big, gs, 4, gr)
                yield 13.0
                link(dve, dve.tensor_scalar(gr, gr, 1.5, None, ALU.is_lt))
                link(dve, dve.tensor_tensor(masked.rearrange("p t (g r) -> p t g r", g=4),
                                            choice.rearrange("p t (g r) -> p t g r", g=4),
                                            gr.unsqueeze(3).broadcast_to([P, NT, 4, 4]), ALU.mult))
                rank(st, dve, big, masked, E0, ranks)
                yield 19.0
                link(dve, dve.tensor_scalar(sel, ranks, 3.5, None, ALU.is_lt))
                link(dve, dve.tensor_tensor(wsel, sel, sig, ALU.mult))
                tot = sc[:, 10, :, 0:1]
                link(dve, dve.tensor_reduce(tot, wsel, AX.X, ALU.add))
                link(dve, dve.tensor_scalar(tot, tot, 1e-20, None, ALU.add))
                link(dve, dve.reciprocal(sc[:, 11, :, 0:1], tot))
                link(dve, dve.tensor_scalar(wsel, wsel, 2.5, None, ALU.mult))
                link(dve, dve.tensor_tensor(sc[:, 6], wsel, sc[:, 11, :, 0:1].broadcast_to([P, NT, E0]), ALU.mult))
                w, high, mid, low = sc[:, 6], *(w_parts[:, :, i * E0:(i + 1) * E0] for i in range(3))
                link(dve, dve.tensor_scalar(high.bitcast(I32), w.bitcast(I32), TOP_HALF, None, ALU.bitwise_and))
                link(dve, dve.tensor_tensor(w, w, high, ALU.subtract))
                link(dve, dve.tensor_scalar(mid.bitcast(I32), w.bitcast(I32), TOP_HALF, None, ALU.bitwise_and))
                dve.tensor_tensor(low, w, mid, ALU.subtract).then_inc(S("weights_ready"), 1)
                yield 22.5
                dve.wait_ge(S("weights_turned"), 1)
                dve.tensor_copy(cwT, bank[0:3 * E0, 0, :]).then_inc(S("cwT_ready"), 1)
                for c in range(8):
                    yield 24.5 + c * 0.6
                    dve.wait_ge(S("squared"), c + 1)
                    dve.wait_ge(S("spread"), c + 1)
                    dve.tensor_tensor(hid[:, c, :], hid[:, c, :], bank[:, 1 + c % 2, :],
                                      ALU.mult).then_inc(S("weighted"), 1)
                yield 42.0
                dve.wait_ge(S("moe_out"), 1)
                dve.tensor_tensor(x_sb[:, :, :], x_sb[:, :, :], tiles(bank[:, 3, :]), ALU.add).then_inc(S("done"), 1)

            def gpsimd(gp):
                yield from norm_gpsimd(st, gp)
                for c in range(9):
                    yield 8.2 + c * 1.1
                    gp.wait_ge(S("relued"), c + 1)
                    gp.tensor_tensor(hid[:, c, :], relu[:, c % 2, :], relu[:, c % 2, :], ALU.mult).then_inc(S("squared"), 1)

            def scalar(act):
                yield 7.0
                act.wait_ge(S("logits"), 1)
                act.activation(elog, bank[:, 3, 0:NT * E0].rearrange("p (t e) -> p t e", t=NT), ACT.Exp,
                               scale=-1.0).then_inc(S("exp_logits"), 1)
                for c in range(9):
                    yield 8.0 + c * 1.1
                    act.wait_ge(S("hidden"), c + 1)
                    if c >= 2:
                        act.wait_ge(S("squared"), c - 1)
                    act.activation(relu[:, c % 2, :], bank[:, 1 + c % 2, :], ACT.Relu).then_inc(S("relued"), 1)

            def tensor(pe):
                yield 4.0
                pe.wait_ge(*S.once("normed"))
                turn(pe, y_sb, bank[:, 0, :]).then_inc(S("turned"), 1)
                yield 6.0
                pe.wait_ge(*S.once("hT_ready"))
                for j in range(NT):
                    i = pe.matmul(bank[:, 3, j * E0:(j + 1) * E0], hT[:, j * P:(j + 1) * P], wa("wg0"),
                                  start=True, stop=True)
                i.then_inc(S("logits"), 1)
                for c in range(9):
                    yield 7.0 + c * 1.1
                    if c >= 2:
                        pe.wait_ge(S("relued"), c - 1)
                    w = wa("w1_0")[:, c * P:(c + 1) * P] if c < 8 else wa("ws1_0")
                    pe.matmul(bank[:, 1 + c % 2, :], w, hT[:, :], start=True, stop=True).then_inc(S("hidden"), 1)
                yield 22.0
                pe.wait_ge(S("weights_ready"), 1)
                for j in range(NT):
                    i = pe.transpose(bank[0:3 * E0, 0, j * P:(j + 1) * P], w_parts[:, j, :], ident)
                i.then_inc(S("weights_turned"), 1)
                yield 23.0
                pe.wait_ge(S("cwT_ready"), 1)
                pe.wait_ge(S("relued"), 9)
                for c in range(8):
                    yield 24.0 + c * 0.6
                    if c >= 2:
                        pe.wait_ge(S("weighted"), c - 1)
                    pe.matmul(bank[:, 1 + c % 2, :], kb("sel16", 3 * E0)[:, c * P:(c + 1) * P], cwT,
                              start=True, stop=True).then_inc(S("spread"), 1)
                for j in range(NT):
                    for c in range(9):
                        yield 32.5 + (j * 9 + c) * 0.23
                        if j == 0 and c == 0:
                            pe.wait_ge(S("weighted"), 8)
                            pe.wait_ge(S("squared"), 9)
                        w = wa("w2_0")[:, c * P:(c + 1) * P] if c < 8 else wa("ws2_0")
                        i = pe.matmul(bank[:, 3, j * P:(j + 1) * P], hid[:, c, j * P:(j + 1) * P], w,
                                      start=c == 0, stop=c == 8)
                i.then_inc(S("moe_out"), 1)

            return {"vector": vector, "gpsimd": gpsimd, "scalar": scalar, "tensor": tensor}, 43.0, S.once("done")

        with ExitStack() as ctx:
            w_a = sb(ctx, "w_a", [P, width(PACK_A)])
            wa = Pieces(w_a, PACK_A)
            load_weights([(w_a, pa)])
            x_b = x.rearrange("(b t p) c -> p b t c", b=B, p=P)
            x1_b = x1.rearrange("(b t p) c -> p b t c", b=B, p=P)

            def plan_a(st, n):
                own, b = st.buf["x"][:, :, :], bass.ds(n, 1)
                c0, c1 = wa("cols0"), wa("cols1")
                yield load_x(st, [(own, x_b[:, b, :, :])])
                yield attention(st, "a0_", st.buf["y"], wa("wq0"), wa("wk0"), wa("wv0"), wa("wo0"),
                                c0[:, 2:3], c0[:, 3:4], wa("bv0"), wa("bo0"), float(HD) ** -0.5, False, False,
                                None, (c0[:, 0:1], c0[:, 1:2]), True)
                yield moe0(st, wa)
                yield attention(st, "a1_", st.buf["y"], wa("wq1"), wa("wk1"), wa("wv1"), wa("wp1"),
                                c1[:, 0:1], c1[:, 1:2], wa("bv1"), wa("bp1"), float(HD) ** -0.5, True, False,
                                (wa("wqs1"), wa("wks1"), c1[:, 2:3], c1[:, 3:4], wa("cos1"), wa("sin1")),
                                None, False)
                yield store_x(st, [(own, x1_b[:, b, :, :])])

            together(plan_a, B // 2, OFFSET_A)

        def experts(st, S, t0, share, func, w_up, w_down, bias, weight, acc, hbuf, logits_read):
            bank, hT = banks[:, st.index], st.buf["hT"]
            E = share

            def up_at(n):
                return t0 + n // NF * E + n % NF * 0.9

            def down_at(e):
                return t0 + (e + 1) * E + 3.7

            def tensor(pe):
                def up(n):
                    if n >= 2:
                        pe.wait_ge(S("acted"), n - 1)
                    pe.matmul(bank[:, n % 2, :], w_up[:, n * P:(n + 1) * P], hT[:, :],
                              start=True, stop=True).then_inc(S("up"), 1)

                def down(e, j):
                    if j == 0:
                        pe.wait_ge(S("acted"), NF * (e + 1))
                        if e == 0:
                            pe.wait_ge(S(logits_read), 1)
                        if e >= 2:
                            pe.wait_ge(S("mixed"), e - 1)
                    for f in range(NF):
                        n = e * NF + f
                        i = pe.matmul(bank[:, 2 + e % 2, j * P:(j + 1) * P], hbuf[:, n % 8, j * P:(j + 1) * P],
                                      w_down[:, n * P:(n + 1) * P], start=f == 0, stop=f == NF - 1)
                    if j == NT - 1:
                        i.then_inc(S("down"), 1)

                for e in range(E8 + 1):
                    if e < E8:
                        for f in range(NF):
                            yield up_at(e * NF + f)
                            up(e * NF + f)
                    if e >= 1:
                        for j in range(NT):
                            yield down_at(e - 1) + 0.9 * j
                            down(e - 1, j)

            def scalar(act):
                for n in range(E8 * NF):
                    yield up_at(n) + 0.5
                    act.wait_ge(S("up"), n + 1)
                    if n % NF == 0 and n >= 2 * NF:
                        act.wait_ge(S("down"), n // NF - 1)
                    act.activation(hbuf[:, n % 8, :], bank[:, n % 2, :], func,
                                   bias=bias[:, n:n + 1] if bias is not None else 0.0).then_inc(S("acted"), 1)

            def vector(dve):
                for e in range(E8):
                    yield down_at(e) + 3.6
                    dve.wait_ge(S("down"), e + 1)
                    if e:
                        dve.wait_ge(S("mixed"), e)
                    for j in range(NT):
                        src = bank[:, 2 + e % 2, j * P:(j + 1) * P]
                        if e == 0:
                            i = dve.tensor_scalar(acc[:, j, :], src, weight[:, j, e:e + 1], None, ALU.mult)
                        else:
                            i = dve.scalar_tensor_tensor(acc[:, j, :], src, weight[:, j, e:e + 1], acc[:, j, :],
                                                         ALU.mult, ALU.add)
                    i.then_inc(S("mixed"), 1)
                dve.wait_ge(S("mixed"), E8)

            return tensor, scalar, vector, down_at(E8 - 1) + 4.6

        def rep(piece):
            return piece.unsqueeze(1).broadcast_to([P, NT, C])

        def mha(st, wb):
            buf, link = st.buf, st.chain["vector"]
            bank = banks[:, st.index]
            x_sb, y_sb, h_sb, hT, base = buf["x"], buf["y"], buf["h"], buf["hT"], buf["base"]
            room = Room(st)
            hold, acc = room([P, NT, C]), room([P, NT, C])
            qkT, v_sb = room([P, 2, T]), room([P, NT, C])
            s32, pT = room([P, SH, T]), room([P, SH, T])
            smx, ssum, srec = room([P, SH * NT]), room([P, SH * NT]), room([P, SH * NT])

            S = st.signals("mha_")

            def by_head(t):
                return t.rearrange("p h (j k) -> p (h j) k", j=NT)

            def vector(dve):
                i = yield from norm_vector(st, dve, x_sb, y_sb)
                i.then_inc(S("normed"), 1)
                yield 5.0
                dve.wait_ge(*S.once("turned"))
                dve.tensor_copy(hT[:, :], bank[:, 3, :]).then_inc(S("hT_ready"), 1)
                yield 8.0
                dve.wait_ge(S("v_projected"), 1)
                dve.tensor_tensor(v_sb, tiles(bank[:, 2, :]), rep(wb("bv")), ALU.add).then_inc(S("v_ready"), 1)
                yield 14.0
                dve.wait_ge(S("scored"), 1)
                link(dve, dve.tensor_reduce(smx, by_head(bank), AX.X, ALU.max))
                dve.tensor_tensor(by_head(s32), by_head(bank), smx.unsqueeze(2).broadcast_to([P, SH * NT, P]),
                                  ALU.subtract).then_inc(S("centred"), 1)
                yield 21.0
                dve.wait_ge(S("exped"), 1)
                link(dve, dve.tensor_reduce(ssum, by_head(s32), AX.X, ALU.add))
                link(dve, dve.reciprocal(srec, ssum))
                yield 28.0
                dve.wait_ge(S("av"), 1)
                dve.tensor_tensor(h_sb[:, :, :].rearrange("p t (h d) -> p t h d", h=SH),
                                  bank[:, 0, :].rearrange("p (t h d) -> p t h d", t=NT, h=SH),
                                  srec.rearrange("p (h j) -> p j h", h=SH).unsqueeze(3).broadcast_to([P, NT, SH, SD]),
                                  ALU.mult).then_inc(S("o_normed"), 1)
                yield 31.0
                dve.wait_ge(S("o_back"), 1)
                dve.tensor_copy(hT[:, :], bank[:, 1, :]).then_inc(S("oT_ready"), 1)
                yield 33.5
                dve.wait_ge(S("base_ready"), 1)
                dve.wait_ge(S("out_projected"), 1)
                link(dve, dve.tensor_tensor(acc, base[:, :, :], tiles(bank[:, 2, :]), ALU.add))
                i = yield from norm_vector(st, dve, acc, h_sb, 34.0)
                link(dve, i)
                link(dve, dve.tensor_tensor(h_sb[:, :, :], h_sb[:, :, :], rep(wb("g1")), ALU.mult))
                dve.tensor_tensor(hold, h_sb[:, :, :], rep(wb("be1")), ALU.add).then_inc(S("done"), 1)

            def gpsimd(gp):
                yield from norm_gpsimd(st, gp)
                yield 5.0
                gp.wait_ge(*S.once("normed"))
                for j in range(NT):
                    i = gp.tensor_tensor(base[:, j, :], y_sb[:, j, :], wb("bo"), ALU.add)
                i.then_inc(S("base_ready"), 1)
                yield from norm_gpsimd(st, gp, 34.0)

            def scalar(act):
                yield 8.0
                act.wait_ge(S("qk_projected"), 1)
                act.activation(qkT[:, 0, :], bank[:, 0, :], ACT.Identity, bias=wb("cols")[:, 0:1])
                act.activation(qkT[:, 1, :], bank[:, 1, :], ACT.Identity, bias=wb("cols")[:, 1:2]).then_inc(S("qk_taken"), 1)
                yield 19.0
                act.wait_ge(S("centred"), 1)
                act.activation(s32, s32, ACT.Exp, scale=float(SD) ** -0.5).then_inc(S("exped"), 1)
                yield 25.0
                act.wait_ge(S("p_turned"), 1)
                act.activation(pT, bank, ACT.Copy).then_inc(S("pT_ready"), 1)

            def tensor(pe):
                yield 4.0
                pe.wait_ge(*S.once("normed"))
                turn(pe, y_sb, bank[:, 3, :]).then_inc(S("turned"), 1)
                yield 6.0
                pe.wait_ge(*S.once("hT_ready"))
                pe.matmul(bank[:, 0, :], wb("wq"), hT[:, :], start=True, stop=True)
                pe.matmul(bank[:, 1, :], wb("wk"), hT[:, :], start=True, stop=True).then_inc(S("qk_projected"), 1)
                for j in range(NT):
                    i = pe.matmul(bank[:, 2, j * P:(j + 1) * P], hT[:, j * P:(j + 1) * P], wb("wv"),
                                  start=True, stop=True)
                i.then_inc(S("v_projected"), 1)
                yield 10.0
                pe.wait_ge(S("qk_taken"), 1)
                pe.wait_ge(S("v_ready"), 1)
                for h in range(SH):
                    pe.matmul(bank[:, h, :], identb, kb("block"), start=True, stop=False, skip_group_check=True)
                for j in range(NT):
                    for h in range(SH):
                        i = pe.matmul(bank[:, h, j * P:(j + 1) * P], qkT[SD * h:SD * (h + 1), 0, j * P:(j + 1) * P],
                                      qkT[SD * h:SD * (h + 1), 1, j * P:(j + 1) * P], start=False,
                                      stop=j == NT - 1, skip_group_check=True)
                i.then_inc(S("scored"), 1)
                yield 22.0
                pe.wait_ge(S("exped"), 1)
                for h in range(SH):
                    for j in range(NT):
                        i = pe.transpose(bank[:, h, j * P:(j + 1) * P], s32[:, h, j * P:(j + 1) * P], ident)
                i.then_inc(S("p_turned"), 1)
                yield 27.0
                pe.wait_ge(S("pT_ready"), 1)
                for j in range(NT):
                    for h in range(SH):
                        i = pe.matmul(bank[:, 0, j * P + h * SD:j * P + (h + 1) * SD], pT[:, h, j * P:(j + 1) * P],
                                      v_sb[:, j, h * SD:(h + 1) * SD], start=True, stop=True)
                i.then_inc(S("av"), 1)
                yield 30.0
                pe.wait_ge(S("o_normed"), 1)
                turn(pe, h_sb, bank[:, 1, :]).then_inc(S("o_back"), 1)
                yield 32.0
                pe.wait_ge(S("oT_ready"), 1)
                for j in range(NT):
                    i = pe.matmul(bank[:, 2, j * P:(j + 1) * P], hT[:, j * P:(j + 1) * P], wb("wo"),
                                  start=True, stop=True)
                i.then_inc(S("out_projected"), 1)

            return {"vector": vector, "gpsimd": gpsimd, "scalar": scalar, "tensor": tensor}, 40.0, S.once("done")

        def moe1(st, wb, b2_sb):
            buf, link = st.buf, st.chain["vector"]
            bank = banks[:, st.index]
            x_sb, h_sb, hT, base = buf["x"], buf["h"], buf["hT"], buf["base"]
            room = Room(st)
            hold, acc = room([P, NT, C]), room([P, NT, C])
            hbuf, lg, big8, mT = room([P, 8, T]), room([P, 4, NT, E8]), room([P, 2, 256]), room([E8, T])
            mask = lg[:, 2]

            S = st.signals("moe1_", absent=("normed",))

            parts = experts(st, S, 8.0, 7.4, ACT.Relu, wb("w1"), wb("w2"), wb("b1"), mask, acc, hbuf, "mask_ready")
            end = parts[3]

            def vector(dve):
                yield 1.0
                dve.wait_ge(*S.once("turned"))
                dve.tensor_copy(hT[:, :], bank[:, 3, :]).then_inc(S("hT_ready"), 1)
                yield 4.0
                dve.wait_ge(S("logits"), 1)
                link(dve, dve.tensor_copy(lg[:, 0], bank[:, 2, 0:NT * E8].rearrange("p (t e) -> p t e", t=NT)))
                rank(st, dve, big8, lg[:, 0], E8, lg[:, 1])
                dve.tensor_scalar(mask, lg[:, 1], 0.5, None, ALU.is_lt).then_inc(S("mask_ready"), 1)
                dve.wait_ge(S("mask_ready"), 1)
                yield from parts[2](dve)
                yield end + 1.0
                dve.wait_ge(S("mask_turned"), 1)
                dve.tensor_copy(mT, bank[0:E8, 0, :]).then_inc(S("mT_ready"), 1)
                link(dve, dve.tensor_tensor(acc, acc, hold, ALU.add))
                yield end + 3.0
                dve.wait_ge(S("bias2"), 1)
                link(dve, dve.tensor_tensor(acc, acc, tiles(bank[:, 1, :]), ALU.add))
                i = yield from norm_vector(st, dve, acc, h_sb, end + 3.5)
                link(dve, i)
                link(dve, dve.tensor_tensor(h_sb[:, :, :], h_sb[:, :, :], rep(wb("g2")), ALU.mult))
                dve.wait_ge(S("base_ready"), 1)
                dve.tensor_tensor(x_sb[:, :, :], h_sb[:, :, :], base[:, :, :], ALU.add).then_inc(S("done"), 1)

            def gpsimd(gp):
                yield 1.0
                for j in range(NT):
                    i = gp.tensor_tensor(base[:, j, :], x_sb[:, j, :], wb("be2"), ALU.add)
                i.then_inc(S("base_ready"), 1)
                yield from norm_gpsimd(st, gp, end + 3.5)

            def tensor(pe):
                yield 0.0
                turn(pe, hold, bank[:, 3, :]).then_inc(S("turned"), 1)
                yield 3.0
                pe.wait_ge(*S.once("hT_ready"))
                for j in range(NT):
                    i = pe.matmul(bank[:, 2, j * E8:(j + 1) * E8], hT[:, j * P:(j + 1) * P], wb("wg"),
                                  start=True, stop=True)
                i.then_inc(S("logits"), 1)
                yield from parts[0](pe)
                yield end
                pe.wait_ge(S("mask_ready"), 1)
                for j in range(NT):
                    i = pe.transpose(bank[0:E8, 0, j * P:(j + 1) * P], lg[:, 2, j, :], ident)
                i.then_inc(S("mask_turned"), 1)
                yield end + 2.0
                pe.wait_ge(S("mT_ready"), 1)
                for j in range(NT):
                    i = pe.matmul(bank[:, 1, j * P:(j + 1) * P], mT[:, j * P:(j + 1) * P], b2_sb[:, :],
                                  start=True, stop=True)
                i.then_inc(S("bias2"), 1)

            return {"vector": vector, "gpsimd": gpsimd, "scalar": parts[1], "tensor": tensor}, end + 9.0, S.once("done")

        with ExitStack() as ctx:
            w_b = sb(ctx, "w_b", [P, width(PACK_B)])
            wb = Pieces(w_b, PACK_B)
            b2_sb = sb(ctx, "b2_sb", [E8, C])
            load_weights([(w_b, pb), (b2_sb, b2)])

            def slices(st, t, i):
                v = t.rearrange("(s i j l) c -> s l i j c", s=SB, i=T // 64, j=NT)
                return [(st.buf["x"][s * 16:(s + 1) * 16, :, :], v[s, :, bass.ds(i, 1), :, :]) for s in range(SB)]

            def early_b(st, n):
                yield load_x(st, slices(st, x1, n))
                yield mha(st, wb)

            def late_b(st, n):
                yield moe1(st, wb, b2_sb)
                yield store_x(st, slices(st, x2, n))

            staggered(early_b, late_b, T // 128)

        def mamba(st, wc, acoef, sel_sum):
            buf, link = st.buf, st.chain["vector"]
            bank = banks[:, st.index]
            x_sb, y_sb, hT = buf["x"], buf["y"], buf["hT"]
            room = Room(st)
            xs, zs, Bb, Cb = room([P, 2, T]), room([P, 2, T]), room([P, T]), room([P, T])
            xpad = room([P, NCH, DC - 1 + T])
            mark = room.at
            conv, q2, relu2, e2 = room([P, 2, T]), room([P, 2, T]), room([P, 2, T]), room([P, 2, T])
            dtx, r2, parts2 = room([P, 2, 2, T]), room([P, 2, 2, T]), room([P, 3, 2, 2, T], BF16)
            room.at = mark
            G = room([96, 2, 8, T], BF16)
            ab, ub, hb, hc = room([P, 2, T]), room([P, 2, T]), room([P, 3, T]), room([P, 3, T])
            room.at = mark
            yf = room([P, 2, T])

            S = st.signals("mamba_")

            G0, GU = 62.0, 1.56

            def rests(eng, q):
                yield 40.0
                eng.wait_ge(S("rounded"), 1 + q)
                eng.tensor_tensor(r2[:, q], dtx[:, q], parts2[:, 0, q], ALU.subtract).then_inc(S("rest_%d" % q), 1)
                yield 43.0
                eng.wait_ge(S("rest_%d" % q), 1)
                eng.wait_ge(S("rounded"), 3 + q)
                eng.tensor_tensor(parts2[:, 2, q], r2[:, q], parts2[:, 1, q],
                                  ALU.subtract).then_inc(S("rest_%d" % q), 1)

            def vector(dve):
                i = yield from norm_vector(st, dve, x_sb, y_sb)
                i.then_inc(S("normed"), 1)
                yield 5.0
                dve.wait_ge(*S.once("turned"))
                dve.tensor_copy(hT[:, :], bank[:, 3, :]).then_inc(S("hT_ready"), 1)
                yield 5.5
                link(dve, dve.memset(xpad[:, :, 0:DC - 1], 0.0))
                yield 12.0
                dve.wait_ge(S("x_taken"), 1)
                for c in range(NCH):
                    i = dve.tensor_scalar(conv[:, c, :], xpad[:, c, 0:T], wc("convw")[:, c * DC:c * DC + 1],
                                          wc("convb")[:, c:c + 1], ALU.mult, ALU.add)
                link(dve, i)
                for k in range(1, DC):
                    yield 12.0 + 1.2 * k
                    for c in range(NCH):
                        i = dve.scalar_tensor_tensor(conv[:, c, :], xpad[:, c, k:k + T],
                                                     wc("convw")[:, c * DC + k:c * DC + k + 1], conv[:, c, :],
                                                     ALU.mult, ALU.add)
                    if k < DC - 1:
                        link(dve, i)
                i.then_inc(S("convolved"), 1)
                yield 28.0
                dve.wait_ge(S("e_ready"), 1)
                link(dve, dve.tensor_scalar(q2, e2, LOG1P[-1], None, ALU.mult))
                for k, coefficient in enumerate(LOG1P[-2::-1]):
                    yield 28.5 + 1.1 * k
                    link(dve, dve.scalar_tensor_tensor(q2, q2, coefficient, e2, ALU.add, ALU.mult))
                yield 37.5
                dve.wait_ge(S("e_ready"), 3)
                dve.tensor_tensor(dtx[:, 0], relu2, q2, ALU.add).then_inc(S("dtx_ready"), 1)
                dve.wait_ge(S("dtx_ready"), 1)
                dve.tensor_tensor(dtx[:, 1], dtx[:, 0], xs, ALU.mult).then_inc(S("dtx_ready"), 1)
                yield from rests(dve, 0)
                dve.wait_ge(S("bc_taken"), 1)
                for g in range(NGR):
                    yield G0 + g * GU + 0.3
                    if g >= 2:
                        dve.wait_ge(S("scanned"), g - 1)
                    dve.wait_ge(S("dtx_spread"), g + 1)
                    dve.tensor_tensor(ub[:, g % 2, :], bank[:, 1, :], Bb, ALU.mult).then_inc(S("u_ready"), 1)
                    yield G0 + g * GU + 0.9
                    dve.wait_ge(S("decay"), g + 1)
                    dve.wait_ge(S("u_ready"), g + 1)
                    if g >= 3:
                        dve.wait_ge(S("hc_ready"), g - 2)
                    dve.tensor_tensor_scan(hb[:, g % 3, :], ab[:, g % 2, :], ub[:, g % 2, :], 0.0,
                                           ALU.mult, ALU.add).then_inc(S("scanned"), 1)
                end = G0 + NGR * GU + 4.0
                yield end
                dve.wait_ge(S("summed"), NGR)
                for c in range(NCH):
                    i = dve.scalar_tensor_tensor(yf[:, c, :], xs[:, c, :], wc("dcol")[:, c:c + 1], bank[:, 2 + c, :],
                                                 ALU.mult, ALU.add)
                link(dve, i)
                dve.tensor_tensor(yf, yf, zs, ALU.mult).then_inc(S("gated"), 1)
                yield end + 5.0
                dve.wait_ge(S("out_projected"), 1)
                dve.tensor_tensor(x_sb[:, :, :], x_sb[:, :, :], tiles(bank[:, 0, :]), ALU.add).then_inc(S("done"), 1)

            def gpsimd(gp):
                yield from norm_gpsimd(st, gp)
                yield from rests(gp, 1)
                yield 52.0
                gp.wait_ge(S("bc_taken"), 1)
                for g in range(NGR):
                    yield G0 + g * GU + 1.6
                    gp.wait_ge(S("scanned"), g + 1)
                    if g >= 3:
                        gp.wait_ge(S("summed"), g - 2)
                    gp.tensor_tensor(hc[:, g % 3, :], hb[:, g % 3, :], Cb, ALU.mult).then_inc(S("hc_ready"), 1)

            def scalar(act):
                yield 11.0
                act.wait_ge(S("in_projected"), 1)
                act.activation(xpad[:, :, DC - 1:DC - 1 + T], bank[:, 0:2, :], ACT.Copy).then_inc(S("x_taken"), 1)
                act.activation(zs, bank[:, 2:4, :], ACT.Silu).then_inc(S("z_done"), 1)
                yield 17.0
                act.wait_ge(S("convolved"), 1)
                act.activation(xs, conv, ACT.Silu).then_inc(S("xs_ready"), 1)
                yield 25.0
                act.wait_ge(S("x_dbl"), 1)
                for c in range(NCH):
                    act.activation(r2[:, 0, c, :], bank[:, 0, :], ACT.Abs, bias=wc("bdt")[:, c:c + 1],
                                   scale=wc("wdt")[:, c:c + 1]).then_inc(S("abs_ready"), 1)
                act.wait_ge(S("abs_ready"), 2)
                act.activation(e2, r2[:, 0], ACT.Exp, scale=-1.0).then_inc(S("e_ready"), 1)
                yield 27.5
                for c in range(NCH):
                    act.activation(relu2[:, c, :], bank[:, 0, :], ACT.Relu, bias=wc("bdt")[:, c:c + 1],
                                   scale=wc("wdt")[:, c:c + 1]).then_inc(S("e_ready"), 1)
                yield 30.0
                act.wait_ge(S("x_dbl"), 3)
                act.activation(Bb, bank[:, 1, :], ACT.Copy)
                act.activation(Cb, bank[:, 2, :], ACT.Copy).then_inc(S("bc_taken"), 1)
                for q in range(2):
                    yield 38.8 + q
                    act.wait_ge(S("dtx_ready"), 1 + q)
                    act.activation(parts2[:, 0, q], dtx[:, q], ACT.Copy).then_inc(S("rounded"), 1)
                for q in range(2):
                    yield 42.0 + q
                    act.wait_ge(S("rest_%d" % q), 1)
                    act.activation(parts2[:, 1, q], r2[:, q], ACT.Copy).then_inc(S("rounded"), 1)
                for g in range(NGR):
                    yield G0 + g * GU + 0.2
                    act.wait_ge(S("dt_spread"), g + 1)
                    if g >= 2:
                        act.wait_ge(S("scanned"), g - 1)
                    act.activation(ab[:, g % 2, :], bank[:, 0, :], ACT.Exp, scale=acoef[:, g:g + 1]).then_inc(S("decay"), 1)

            def sync(sp):
                scratch = dt_dram[st.index]
                for i in range(3):
                    yield 39.0 + 3.4 * i
                    if i < 2:
                        sp.wait_ge(S("rounded"), 2 * (i + 1))
                    else:
                        sp.wait_ge(S("rest_0"), 2)
                        sp.wait_ge(S("rest_1"), 2)
                    sp.dma_start(scratch[i].rearrange("q (c p) t -> p (q c) t", p=P),
                                 parts2[:, i].rearrange("p q c t -> p (q c) t")).then_inc(S("parts_stored"), 16)
                    yield 42.0 + 3.4 * i
                    sp.wait_ge(S("parts_stored"), 16 * (i + 1))
                    sp.dma_start(G[32 * i:32 * i + 32, :, :, :].rearrange("l q b t -> l (q b) t"),
                                 scratch[i].rearrange("q (b l) t -> l (q b) t", l=32)).then_inc(S("grouped"), 16)

            def tensor(pe):
                yield 4.0
                pe.wait_ge(*S.once("normed"))
                turn(pe, y_sb, bank[:, 3, :]).then_inc(S("turned"), 1)
                yield 6.0
                pe.wait_ge(*S.once("hT_ready"))
                for c in range(4):
                    i = pe.matmul(bank[:, c, :], wc("win")[:, c * P:(c + 1) * P], hT[:, :], start=True, stop=True)
                i.then_inc(S("in_projected"), 1)
                yield 19.0
                pe.wait_ge(S("xs_ready"), 1)
                pe.wait_ge(S("z_done"), 1)
                for n, w in enumerate(("wxd", "wxb", "wxc")):
                    for c in range(NCH):
                        i = pe.matmul(bank[:, n, :], wc(w)[:, c * P:(c + 1) * P], xs[:, c, :],
                                      start=c == 0, stop=c == NCH - 1)
                    i.then_inc(S("x_dbl"), 1)
                yield 61.0
                pe.wait_ge(S("grouped"), 48)
                pe.wait_ge(S("bc_taken"), 1)

                def spread(g):
                    if g:
                        pe.wait_ge(S("decay"), g)
                    sel = kb("selG", 96)[:, (g % 4) * P:(g % 4 + 1) * P]
                    pe.matmul(bank[:, 0, :], sel, G[:, 0, g // 4, :], start=True, stop=True).then_inc(S("dt_spread"), 1)
                    if g:
                        pe.wait_ge(S("u_ready"), g)
                    pe.matmul(bank[:, 1, :], sel, G[:, 1, g // 4, :], start=True, stop=True).then_inc(S("dtx_spread"), 1)

                def collect(g):
                    pe.wait_ge(S("hc_ready"), g + 1)
                    c, q = g // 16, g // 4 % 4
                    pe.matmul(bank[32 * q:32 * q + 32, 2 + c, :], sel_sum[:, (g % 4) * 32:(g % 4 + 1) * 32],
                              hc[:, g % 3, :], start=g % 4 == 0, stop=g % 4 == 3,
                              skip_group_check=True).then_inc(S("summed"), 1)

                for g in range(NGR + 2):
                    if g < NGR:
                        yield G0 + g * GU
                        spread(g)
                    if g >= 2:
                        yield G0 + g * GU + 0.5
                        collect(g - 2)
                end = G0 + NGR * GU + 4.0
                yield end + 3.0
                pe.wait_ge(S("gated"), 1)
                for j in range(NT):
                    for c in range(NCH):
                        i = pe.matmul(bank[:, 0, j * P:(j + 1) * P], yf[:, c, j * P:(j + 1) * P],
                                      wc("wout")[:, c * P:(c + 1) * P], start=c == 0, stop=c == NCH - 1)
                i.then_inc(S("out_projected"), 1)

            program = {"vector": vector, "gpsimd": gpsimd, "scalar": scalar, "sync": sync, "tensor": tensor}
            return program, G0 + NGR * GU + 10.0, S.once("done")

        def moe2(st, wc):
            buf, link = st.buf, st.chain["vector"]
            bank = banks[:, st.index]
            x_sb, y_sb, h_sb, hT, base = buf["x"], buf["y"], buf["h"], buf["hT"], buf["base"]
            room = Room(st)
            acc, hbuf, lg, big8 = room([P, NT, C]), room([P, 8, T]), room([P, 7, NT, E8]), room([P, 2, 256])

            S = st.signals("moe2_")

            parts = experts(st, S, 12.0, 7.4, ACT.Gelu, wc("wup"), wc("wdn"), None, lg[:, 5], acc, hbuf, "centred")
            end = parts[3]

            def tensor(pe):
                yield 4.0
                pe.wait_ge(*S.once("normed"))
                turn(pe, y_sb, bank[:, 3, :]).then_inc(S("turned"), 1)
                yield 6.0
                pe.wait_ge(*S.once("hT_ready"))
                for j in range(NT):
                    i = pe.matmul(bank[:, 2, j * E8:(j + 1) * E8], hT[:, j * P:(j + 1) * P], wc("gw"),
                                  start=True, stop=True)
                i.then_inc(S("logits"), 1)
                yield from parts[0](pe)

            def vector(dve):
                i = yield from norm_vector(st, dve, x_sb, y_sb)
                i.then_inc(S("normed"), 1)
                yield 5.0
                dve.wait_ge(*S.once("turned"))
                dve.tensor_copy(hT[:, :], bank[:, 3, :]).then_inc(S("hT_ready"), 1)
                yield 7.0
                dve.wait_ge(S("logits"), 1)
                row = [P, NT, E8]
                link(dve, dve.tensor_tensor(lg[:, 0], bank[:, 2, 0:NT * E8].rearrange("p (t e) -> p t e", t=NT),
                                            wc("eb").unsqueeze(1).broadcast_to(row), ALU.add))
                link(dve, dve.tensor_reduce(lg[:, 6, :, 0:1], lg[:, 0], AX.X, ALU.max))
                dve.tensor_tensor(lg[:, 1], lg[:, 0], lg[:, 6, :, 0:1].broadcast_to(row),
                                  ALU.subtract).then_inc(S("centred"), 1)
                yield 9.0
                dve.wait_ge(S("exped"), 1)
                link(dve, dve.tensor_reduce(lg[:, 6, :, 1:2], lg[:, 2], AX.X, ALU.add))
                link(dve, dve.reciprocal(lg[:, 6, :, 2:3], lg[:, 6, :, 1:2]))
                link(dve, dve.tensor_tensor(lg[:, 3], lg[:, 2], lg[:, 6, :, 2:3].broadcast_to(row), ALU.mult))
                rank(st, dve, big8, lg[:, 3], E8, lg[:, 4])
                yield 12.0
                link(dve, dve.tensor_scalar(lg[:, 4], lg[:, 4], 1.5, None, ALU.is_lt))
                link(dve, dve.tensor_tensor(lg[:, 3], lg[:, 3], lg[:, 4], ALU.mult))
                link(dve, dve.tensor_reduce(lg[:, 6, :, 3:4], lg[:, 3], AX.X, ALU.add))
                link(dve, dve.tensor_scalar(lg[:, 6, :, 4:5], lg[:, 6, :, 3:4], 1e-6, None, ALU.add))
                link(dve, dve.reciprocal(lg[:, 6, :, 5:6], lg[:, 6, :, 4:5]))
                link(dve, dve.tensor_tensor(lg[:, 5], lg[:, 3], lg[:, 6, :, 5:6].broadcast_to(row), ALU.mult))
                yield from parts[2](dve)
                i = yield from norm_vector(st, dve, acc, h_sb, end)
                link(dve, i)
                dve.wait_ge(S("base_ready"), 1)
                dve.tensor_tensor(x_sb[:, :, :], h_sb[:, :, :], base[:, :, :], ALU.add).then_inc(S("done"), 1)

            def scalar(act):
                yield 8.0
                act.wait_ge(S("centred"), 1)
                act.activation(lg[:, 2], lg[:, 1], ACT.Exp).then_inc(S("exped"), 1)
                yield from parts[1](act)

            def gpsimd(gp):
                yield from norm_gpsimd(st, gp)
                yield 4.0
                gp.wait_ge(*S.once("normed"))
                gp.tensor_tensor(base[:, :, :], x_sb[:, :, :], y_sb[:, :, :], ALU.add).then_inc(S("base_ready"), 1)
                yield from norm_gpsimd(st, gp, end)

            program = {"vector": vector, "gpsimd": gpsimd, "scalar": scalar, "tensor": tensor}
            return program, end + 5.0, S.once("done")

        def lora3(st, wc):
            buf, link = st.buf, st.chain["vector"]
            bank = banks[:, st.index]
            x_sb, y_sb, hT, base = buf["x"], buf["y"], buf["hT"], buf["base"]
            room = Room(st)
            mid, gt, cls, big8 = room([P, 4, T]), room([P, 8, E8]), room([P, P]), room([P, 2, 256])

            S = st.signals("lora_")

            def vector(dve):
                i = yield from norm_vector(st, dve, x_sb, y_sb)
                i.then_inc(S("normed"), 1)
                yield 5.0
                dve.wait_ge(*S.once("turned"))
                link(dve, dve.tensor_copy(hT[:, :], bank[:, 3, :]))
                dve.tensor_copy(cls, hT[:, 0:1].broadcast_to([P, P])).then_inc(S("hT_ready"), 1)
                yield 7.0
                dve.wait_ge(S("logits"), 1)
                link(dve, dve.tensor_copy(gt[:, 0], bank[:, 3, 0:E8]))
                rank(st, dve, big8, gt[:, 0:1], E8, gt[:, 1:2], 1)
                link(dve, dve.tensor_scalar(gt[:, 1], gt[:, 1], 1.5, None, ALU.is_lt))
                link(dve, dve.tensor_reduce(gt[:, 6, 0:1], gt[:, 0], AX.X, ALU.max))
                dve.tensor_scalar(gt[:, 2], gt[:, 0], gt[:, 6, 0:1], None, ALU.subtract).then_inc(S("centred"), 1)
                yield 10.0
                dve.wait_ge(S("exped"), 1)
                link(dve, dve.tensor_tensor(gt[:, 4], gt[:, 3], gt[:, 1], ALU.mult))
                link(dve, dve.tensor_reduce(gt[:, 6, 1:2], gt[:, 4], AX.X, ALU.add))
                link(dve, dve.reciprocal(gt[:, 6, 2:3], gt[:, 6, 1:2]))
                link(dve, dve.tensor_scalar(gt[:, 5], gt[:, 4], gt[:, 6, 2:3], None, ALU.mult))
                pair = gt[:, 5].rearrange("p (c two) -> p c two", two=2)
                dve.tensor_copy(gt[0:64, 7, 0:4], pair[0:64, :, 0])
                dve.tensor_copy(gt[64:128, 7, 0:4], pair[64:128, :, 1]).then_inc(S("gates_ready"), 1)
                yield 22.0
                dve.wait_ge(S("out"), 1)
                dve.wait_ge(S("base_ready"), 1)
                dve.tensor_tensor(x_sb[:, :, :], base[:, :, :], tiles(bank[:, 2, :]), ALU.add).then_inc(S("done"), 1)

            def gpsimd(gp):
                yield from norm_gpsimd(st, gp)
                yield 4.0
                gp.wait_ge(*S.once("normed"))
                gp.tensor_tensor(base[:, :, :], x_sb[:, :, :], y_sb[:, :, :], ALU.add).then_inc(S("base_ready"), 1)

            def scalar(act):
                yield 9.0
                act.wait_ge(S("centred"), 1)
                act.activation(gt[:, 3], gt[:, 2], ACT.Exp).then_inc(S("exped"), 1)
                for c in range(4):
                    yield 12.0 + c
                    if c == 0:
                        act.wait_ge(S("gates_ready"), 1)
                    act.wait_ge(S("mid"), c + 1)
                    act.activation(mid[:, c, :], bank[:, c % 2, :], ACT.Copy, scale=gt[:, 7, c:c + 1]).then_inc(S("mid_ready"), 1)

            def tensor(pe):
                yield 4.0
                pe.wait_ge(*S.once("normed"))
                turn(pe, y_sb, bank[:, 3, :]).then_inc(S("turned"), 1)
                yield 6.0
                pe.wait_ge(*S.once("hT_ready"))
                pe.matmul(bank[:, 3, 0:E8], cls, wc("wr3"), start=True, stop=True).then_inc(S("logits"), 1)
                for c in range(4):
                    yield (6.0 if c < 2 else 11.0) + c
                    if c >= 2:
                        pe.wait_ge(S("mid_ready"), c - 1)
                    pe.matmul(bank[:, c % 2, :], wc("a3")[:, c * P:(c + 1) * P], hT[:, :], start=True,
                              stop=True).then_inc(S("mid"), 1)
                yield 17.0
                pe.wait_ge(S("mid_ready"), 4)
                for j in range(NT):
                    for c in range(4):
                        i = pe.matmul(bank[:, 2, j * P:(j + 1) * P], mid[:, c, j * P:(j + 1) * P],
                                      wc("b3")[:, c * P:(c + 1) * P], start=c == 0, stop=c == 3)
                i.then_inc(S("out"), 1)

            return {"vector": vector, "gpsimd": gpsimd, "scalar": scalar, "tensor": tensor}, 23.0, S.once("done")

        with ExitStack() as ctx:
            w_c = sb(ctx, "w_c", [P, width(PACK_C)])
            wc = Pieces(w_c, PACK_C)
            acoef = sb(ctx, "acoef", [P, NGR])
            sel_sum = sb(ctx, "sel_sum", [P, P])
            load_weights([(w_c, pc), (sel_sum, sel_y)])

            def decay_rates(block):
                @block.scalar
                def _(act):
                    act.activation(acoef[:, :], wc("alog"), ACT.Exp).then_inc(load_sem, 1)

                @block.vector
                def _(dve):
                    dve.wait_ge(load_sem, loads[0] + 1)
                    dve.tensor_scalar(acoef[:, :], acoef[:, :], -1.0, None, ALU.mult)
            stage_block(decay_rates)

            x2_b = x2.rearrange("(b t p) c -> p b t c", b=B, p=P)
            out_b = out.rearrange("(b t p) c -> p b t c", b=B, p=P)
            def plan_c(st, n):
                own, b = st.buf["x"][:, :, :], bass.ds(n, 1)
                c3 = wc("cols3")
                yield load_x(st, [(own, x2_b[:, b, :, :])])
                yield mamba(st, wc, acoef, sel_sum)
                yield moe2(st, wc)
                yield attention(st, "a3_", st.buf["y"], wc("wq3"), wc("wk3"), wc("wv3"), wc("wo3"),
                                c3[:, 0:1], c3[:, 1:2], wc("bv3"), None, float(HD) ** -0.5, False, True,
                                None, None, False)
                yield lora3(st, wc)
                yield store_x(st, [(own, out_b[:, b, :, :])])

            together(plan_c, B // 2, OFFSET_C)


def fixed_tables():
    ident = np.eye(P, dtype=np.float32)
    tri16 = np.tile((np.arange(16)[None, :] < np.arange(16)[:, None]).astype(np.float32).reshape(1, 256), (P, 1))
    sel16 = np.zeros((P, 8, P), np.float32)
    for e in range(E0):
        sel16[[e, e + E0, e + 2 * E0], e // 2, (e % 2) * 64:(e % 2 + 1) * 64] = 1
    sel_y = np.zeros((P, 4, 32), np.float32)
    for n in range(DS):
        for l in range(GD):
            for j in range(4):
                sel_y[n * GD + l, j, j * GD + l] = 1
    p = np.arange(P)
    causal = np.where(p[None, :] > p[:, None], NEG, 0.0)
    corner_a, corner_b = np.zeros((P, P)), np.zeros((P, P))
    corner_a[P - 1, 0] = NEG
    corner_b[0, P - 1] = NEG
    same = np.where(p[None, :] % 16 == p[:, None] % 16, 0.0, NEG)
    sel_g = np.zeros((P, 4, P))
    for part in range(3):
        for j in range(4):
            for l in range(GD):
                sel_g[part * 32 + j * GD + l, j, l::GD] = 1
    kb = np.concatenate([ident, causal, causal.T, corner_a, corner_b, np.tile(same, (1, 4)),
                         sel_g.reshape(P, -1), np.ones((P, 512)), sel16.reshape(P, -1)], 1).astype(np.float32)
    theta = np.power(np.float32(10000.0), (2.0 * np.arange(HD // 2) / HD).astype(np.float32)).astype(np.float32)
    angle = (np.arange(T, dtype=np.float32)[None, :] * theta[:, None]).astype(np.float32).astype(np.float64)
    rows = np.arange(P) % HD
    cos = np.cos(angle)[rows // 2].astype(np.float32)
    sin = (np.sin(angle)[rows // 2] * np.where(rows % 2 == 0, -1.0, 1.0)[:, None]).astype(np.float32)
    return np.concatenate([ident, tri16], 1), kb, sel_y.reshape(P, P), cos, sin


def kernel(**inputs):
    import concourse.bacc as bacc
    from concourse.bass_utils import run_bass_kernel_spmd

    a = {k: np.asarray(v) for k, v in inputs.items()}

    def row(v):
        return np.broadcast_to(v.reshape(1, -1), (P, v.size))

    def packed(pieces, pack):
        for (name, n) in pack:
            assert pieces[name].shape == (P, n), (name, pieces[name].shape)
        return np.ascontiguousarray(np.concatenate([pieces[name] for name, _ in pack], 1))

    tables, tables_b, sel_y, cos, sin = fixed_tables()
    wqkv0, bqkv0 = a["L0_attn_w_qkv"], a["L0_attn_b_qkv"]
    order = np.arange(P).reshape(H, HD).T.reshape(-1)
    swap = order ^ 1
    pa = {
        "wq0": wqkv0[:, 0:128][:, order], "wk0": wqkv0[:, 128:256][:, order], "wv0": wqkv0[:, 256:384], "wo0": a["L0_attn_w_out"],
        "bv0": row(bqkv0[256:384]), "bo0": row(a["L0_attn_b_out"]),
        "cols0": np.stack([a["L0_attn_ln_gamma"], a["L0_attn_ln_beta"], bqkv0[0:128][order],
                           bqkv0[128:256][order]], 1),
        "wg0": a["L0_ffn_Wg"].T, "bc0": row(a["L0_ffn_bias_corr"]),
        "w1_0": a["L0_ffn_W1"].reshape(1024, 128).T, "ws1_0": a["L0_ffn_Ws1"].T,
        "w2_0": a["L0_ffn_W2"].transpose(0, 2, 1).reshape(8, 128, 128).transpose(1, 0, 2).reshape(128, 1024),
        "ws2_0": a["L0_ffn_Ws2"].T,
        "wq1": a["L1_attn_Wq"][order].T, "wk1": a["L1_attn_Wk"][order].T, "wv1": a["L1_attn_Wv"].T, "wp1": a["L1_attn_Wp"].T,
        "wqs1": a["L1_attn_Wq"][swap].T, "wks1": a["L1_attn_Wk"][swap].T,
        "bv1": row(a["L1_attn_bv"]), "bp1": row(a["L1_attn_bp"]),
        "cols1": np.stack([a["L1_attn_bq"][order], a["L1_attn_bk"][order], a["L1_attn_bq"][swap], a["L1_attn_bk"][swap]], 1),
        "cos1": cos[order], "sin1": sin[order],
    }
    wqkv, bqkv = a["L1_ffn_Wqkv"], a["L1_ffn_bqkv"]
    pb = {
        "wq": wqkv[0:128].T, "wk": wqkv[128:256].T, "wv": wqkv[256:384].T, "wo": a["L1_ffn_Wo"].T,
        "cols": np.stack([bqkv[0:128], bqkv[128:256]], 1), "bv": row(bqkv[256:384]), "bo": row(a["L1_ffn_bo"]),
        "g1": row(a["L1_ffn_g1"]), "be1": row(a["L1_ffn_be1"]), "g2": row(a["L1_ffn_g2"]),
        "be2": row(a["L1_ffn_be2"]), "wg": a["L1_ffn_Wg"].T,
        "b1": a["L1_ffn_b1"].reshape(32, 128).T,
        "w1": a["L1_ffn_W1"].transpose(1, 0, 2).reshape(128, 4096),
        "w2": a["L1_ffn_W2"].reshape(32, 128, 128).transpose(1, 0, 2).reshape(128, 4096),
    }
    wx = a["L2_attn_W_x"]

    def chunked(w):
        return w.reshape(2, 128, -1).transpose(1, 0, 2).reshape(128, -1)

    state = np.arange(P) // GD
    pc = {
        "win": a["L2_attn_W_in"], "convw": chunked(a["L2_attn_conv_w"]), "convb": chunked(a["L2_attn_conv_b"]),
        "wxd": chunked(wx[:, np.zeros(P, int)]), "wxb": chunked(wx[:, 1 + state]), "wxc": chunked(wx[:, 17 + state]),
        "wdt": chunked(a["L2_attn_w_dt"]), "bdt": chunked(a["L2_attn_b_dt"]),
        "alog": a["L2_attn_A_log"].reshape(NGR, GD, DS).transpose(2, 1, 0).reshape(P, NGR),
        "dcol": chunked(a["L2_attn_D"]), "wout": chunked(a["L2_attn_W_out"]),
        "gw": a["L2_ffn_gate_w"].T, "eb": row(a["L2_ffn_expert_bias"]),
        "wup": a["L2_ffn_w_up"].transpose(2, 0, 1).reshape(128, 4096),
        "wdn": a["L2_ffn_w_down"].transpose(0, 2, 1).reshape(32, 128, 128).transpose(1, 0, 2).reshape(128, 4096),
        "wq3": a["L3_attn_Wq"][order].T, "wk3": a["L3_attn_Wk"][order].T, "wv3": a["L3_attn_Wv"].T, "wo3": a["L3_attn_Wo"].T,
        "cols3": np.stack([a["L3_attn_bq"][order], a["L3_attn_bk"][order]], 1), "bv3": row(a["L3_attn_bv"]),
        "wr3": a["L3_ffn_Wr"].T, "a3": a["L3_ffn_A"].reshape(512, 128).T,
        "b3": a["L3_ffn_Bw"].transpose(0, 2, 1).reshape(4, 128, 128).transpose(1, 0, 2).reshape(128, 512),
    }
    arrays = {"x": np.ascontiguousarray(a["L0_attn_x"].reshape(B * T, C)), "pa": packed(pa, PACK_A),
              "pb": packed(pb, PACK_B), "pc": packed(pc, PACK_C), "pk": tables, "pkb": tables_b,
              "b2": np.ascontiguousarray(a["L1_ffn_b2"]), "sel_y": sel_y}
    nc = bacc.Bacc("TRN2", target_bir_lowering=False, num_devices=1)
    handles = {k: nc.dram_tensor(f"in_{k}", v.shape, mybir.dt.from_np(v.dtype), kind="ExternalInput").ap()
               for k, v in arrays.items()}
    out = nc.dram_tensor("out", (B * T, C), F32, kind="ExternalOutput").ap()
    build(nc, *(handles[k] for k in ("x", "pa", "pb", "pc", "pk", "pkb", "b2", "sel_y")), out)
    r = run_bass_kernel_spmd(nc, [{f"in_{k}": v for k, v in arrays.items()}], core_ids=[0])
    return r.results[0]["out"].reshape(B, T, C)
```
